# Optimizing a Trainium2 kernel written in Bass

```python
import numpy as np
import jax
import jax.numpy as jnp

def _softmax(x, axis=-1):
    return jax.nn.softmax(x, axis=axis)

def _gelu(x):
    return jax.nn.gelu(x, approximate=True)

def _silu(x):
    return jax.nn.silu(x)

def _sigmoid(x):
    return jax.nn.sigmoid(x)

def _layernorm(x, axis=-1, eps=1e-05):
    m = jnp.mean(x, axis=axis, keepdims=True)
    v = jnp.var(x, axis=axis, keepdims=True)
    return (x - m) / jnp.sqrt(v + eps)

def _scatter_add(tgt, idx, src, axis=0):
    return tgt.at[idx].add(src)

def _segment_sum(src, seg, n):
    return jax.ops.segment_sum(src, seg, n)
kernel_name = 'mk_adj_resnorm_d2_adj_r2_16832d'

def setup_inputs(seed: int=0):
    np.random.seed(seed)
    _w = jnp.asarray

    def _rec_inputs():
        import jax
        import jax.numpy as jnp
        _gk = jax.random.key(seed)
        x = -0.000929 + 1 * jax.random.normal(jax.random.fold_in(_gk, 1), (8, 1024, 64), jnp.float32)
        _w = (1.0 + jnp.arange(1024, dtype=jnp.float32)) ** (-0.5)
        _w = _w / _w.mean()
        _pij = jnp.clip(0.015625 * _w[:, None] * _w[None, :], 0.0, 1.0)
        _a = jax.random.uniform(jax.random.fold_in(_gk, 2), (1024, 1024)) < _pij
        _a = jnp.logical_or(_a, jnp.eye(1024, dtype=bool))
        _af = _a.astype(jnp.float32)
        adj = _af
        return (x, adj)
    x, adj = _rec_inputs()

    def _L0_gnn_setup():
        import jax, jax.numpy as jnp
        import numpy as np
        NEG = -1000000000.0
        key = jax.random.key(seed)
        ks = jax.random.split(key, 14)
        B, N, E, NF, NH = (8, 1024, 64, 64, 64)
        x = jax.random.normal(ks[0], (B, N, NF), dtype=jnp.float32)
        base = jax.nn.one_hot(jax.random.randint(ks[1], (N,), 0, E), E, dtype=jnp.float32)
        extra = (jax.random.uniform(ks[2], (N, E)) < 0.03).astype(jnp.float32)
        H = jnp.clip(base + extra, 0.0, 1.0)
        adj = (jax.random.uniform(ks[3], (N, N)) < 0.01).astype(jnp.float32)
        adj = jnp.clip(adj + jnp.eye(N, dtype=jnp.float32), 0.0, 1.0)
        s_in = 1.0 / np.sqrt(NF)
        s_h = 1.0 / np.sqrt(NH)
        W = jax.random.normal(ks[4], (NF, NH), dtype=jnp.float32) * s_in
        W_ind = jax.random.normal(ks[5], (NF, NH), dtype=jnp.float32) * s_in
        a_node = jax.random.normal(ks[6], (NH,), dtype=jnp.float32) * s_h
        a_gn = jax.random.normal(ks[7], (NH,), dtype=jnp.float32) * s_h
        a_ge = jax.random.normal(ks[8], (NH,), dtype=jnp.float32) * s_h
        fcW = jax.random.normal(ks[9], (NH, 2 * NH), dtype=jnp.float32) * s_h
        fcb = jnp.zeros((2 * NH,), dtype=jnp.float32)
        av = jax.random.normal(ks[10], (2 * NH,), dtype=jnp.float32) / np.sqrt(2 * NH)
        return {'x': x, 'H': H, 'adj': adj, 'nhid': NH, 'W': W, 'W_ind': W_ind, 'a_node': a_node, 'a_gn': a_gn, 'a_ge': a_ge, 'fcW': fcW, 'fcb': fcb, 'av': av}
    _L0_gnn_all = _L0_gnn_setup()
    _L0_gnn_in = {k: v for k, v in _L0_gnn_all.items() if k in ('H', 'W', 'W_ind', 'a_node', 'a_gn', 'a_ge', 'fcW', 'fcb', 'av')}
    del _L0_gnn_all

    def _L1_gnn_setup():
        import jax, jax.numpy as jnp
        import numpy as np
        NEG_INF = -1e+16

        def gat_layer(x, graph, W, b):
            h = x @ W
            s = jnp.einsum('bnd,bmd->bnm', h, h) * graph
            s = jnp.where(s == 0.0, NEG_INF, s)
            a = jax.nn.softmax(s, axis=2)
            return jnp.einsum('bnm,bmd->bnd', a, h) + b
        key = jax.random.key(seed)
        k1, k2, k3, k4, k5, k6 = jax.random.split(key, 6)
        B, N, C_IN, HID, HEADS, C_OUT = (16, 512, 64, 128, 8, 64)
        flow_x = jax.random.normal(k1, (B, N, C_IN), dtype=jnp.float32)
        graph = jax.random.randint(k2, (N, N), 0, 2).astype(jnp.float32)
        Wh = jax.random.normal(k3, (HEADS, C_IN, HID), dtype=jnp.float32)
        bh = jax.random.normal(k4, (HEADS, HID), dtype=jnp.float32)
        W_out = jax.random.normal(k5, (HID * HEADS, C_OUT), dtype=jnp.float32)
        b_out = jax.random.normal(k6, (C_OUT,), dtype=jnp.float32)
        return {'flow_x': flow_x, 'graph': graph, 'Wh': Wh, 'bh': bh, 'W_out': W_out, 'b_out': b_out}
    _L1_gnn_all = _L1_gnn_setup()
    _L1_gnn_in = {k: v for k, v in _L1_gnn_all.items() if k in ('Wh', 'bh', 'W_out', 'b_out')}
    del _L1_gnn_all
    return {'x': x, 'adj': adj, 'L0_gnn_H': _L0_gnn_in['H'], 'L0_gnn_W': _L0_gnn_in['W'], 'L0_gnn_W_ind': _L0_gnn_in['W_ind'], 'L0_gnn_a_node': _L0_gnn_in['a_node'], 'L0_gnn_a_gn': _L0_gnn_in['a_gn'], 'L0_gnn_a_ge': _L0_gnn_in['a_ge'], 'L0_gnn_fcW': _L0_gnn_in['fcW'], 'L0_gnn_fcb': _L0_gnn_in['fcb'], 'L0_gnn_av': _L0_gnn_in['av'], 'L1_gnn_Wh': _L1_gnn_in['Wh'], 'L1_gnn_bh': _L1_gnn_in['bh'], 'L1_gnn_W_out': _L1_gnn_in['W_out'], 'L1_gnn_b_out': _L1_gnn_in['b_out']}

def reference(x, adj, L0_gnn_H, L0_gnn_W, L0_gnn_W_ind, L0_gnn_a_node, L0_gnn_a_gn, L0_gnn_a_ge, L0_gnn_fcW, L0_gnn_fcb, L0_gnn_av, L1_gnn_Wh, L1_gnn_bh, L1_gnn_W_out, L1_gnn_b_out):
    import jax
    import jax.numpy as jnp

    def _L0_gnn_ref(x, H, adj, nhid, W, W_ind, a_node, a_gn, a_ge, fcW, fcb, av):
        import jax, jax.numpy as jnp
        import numpy as np
        NEG = -1000000000.0
        h = x @ W
        maskEN = H.T
        s = jax.nn.leaky_relu(h @ a_node, 0.2)
        logits = jnp.where(maskEN[None, :, :] > 0, s[:, None, :], NEG)
        alpha = jax.nn.softmax(logits, axis=-1)
        agg = jnp.einsum('ben,bnf->bef', alpha, h)
        beta = jax.nn.sigmoid((h @ a_gn)[:, None, :] + (agg @ a_ge)[:, :, None])
        all_he = beta[..., None] * h[:, None, :, :] + (1.0 - beta[..., None]) * agg[:, :, None, :]
        deg = jnp.maximum(adj.sum(-1), 1.0)[:, None]
        industry = jnp.einsum('nm,bmf->bnf', adj / deg, x @ W_ind)
        all_he = jax.nn.elu(all_he)
        he = jax.nn.elu(agg)

        def attn_scores(f):
            return jnp.tanh(f @ fcW + fcb) @ av
        se = attn_scores(he)
        logits2 = jnp.where(H[None, :, :] > 0, se[:, None, :], NEG)
        coefs1 = jax.nn.softmax(logits2, axis=-1)
        g = jnp.einsum('bne,benf->bnf', coefs1, all_he)
        pair = jnp.stack([industry, g], axis=2)
        coefs2 = jax.nn.softmax(attn_scores(pair), axis=-1)
        out = jnp.einsum('bnk,bnkf->bnf', coefs2, pair)
        return out

    def _L1_gnn_ref(flow_x, graph, Wh, bh, W_out, b_out):
        import jax, jax.numpy as jnp
        import numpy as np
        NEG_INF = -1e+16

        def gat_layer(x, graph, W, b):
            h = x @ W
            s = jnp.einsum('bnd,bmd->bnm', h, h) * graph
            s = jnp.where(s == 0.0, NEG_INF, s)
            a = jax.nn.softmax(s, axis=2)
            return jnp.einsum('bnm,bmd->bnd', a, h) + b
        heads = jax.vmap(lambda W, b: gat_layer(flow_x, graph, W, b))(Wh, bh)
        H, B, N, D = heads.shape
        cat = jnp.moveaxis(heads, 0, 2).reshape(B, N, H * D)
        x = jax.nn.leaky_relu(cat, negative_slope=0.01)
        out = gat_layer(x, graph, W_out, b_out)
        return jax.nn.leaky_relu(out, negative_slope=0.01)
    x = _layernorm(x + _L0_gnn_ref(x, L0_gnn_H, adj, 64, L0_gnn_W, L0_gnn_W_ind, L0_gnn_a_node, L0_gnn_a_gn, L0_gnn_a_ge, L0_gnn_fcW, L0_gnn_fcb, L0_gnn_av), axis=-1)
    x = _layernorm(x + _L1_gnn_ref(x, adj, L1_gnn_Wh, L1_gnn_bh, L1_gnn_W_out, L1_gnn_b_out), axis=-1)
    return x

_drawn_inputs = setup_inputs


def setup_inputs(seed=0):
    import zlib

    import numpy as np

    out = dict(_drawn_inputs(seed))
    spreads = {'L0_gnn_fcb': (0.0, 2.0)}
    factors = {'L0_gnn_a_ge': 3.807, 'L1_gnn_b_out': 7.501}
    for name, (base, spread) in spreads.items():
        noise = np.random.default_rng([zlib.crc32(name.encode()), seed]).standard_normal(out[name].shape)
        drawn = base * np.exp(spread * noise) if base else spread * noise
        out[name] = jnp.asarray(drawn.astype(out[name].dtype))
    for name, factor in factors.items():
        out[name] = (out[name] * factor).astype(out[name].dtype)
    return out
```

```python
from contextlib import ExitStack

import concourse.bass as bass
from concourse import mybir

FP32, FP16, BF16, I32 = mybir.dt.float32, mybir.dt.float16, mybir.dt.bfloat16, mybir.dt.int32
ALU, ACT, AX = mybir.AluOpType, mybir.ActivationFunctionType, mybir.AxisListType
RMAX = bass.bass_isa.ReduceOp.max

P = 128
B = 8
N = 1024
F = 64
T = N // P
BP = B // 2
BF = B * F
E = 64
HEADS = 8
HID = 128
HALF = 512
WCOL = 2 * P + 2
MASKED = -1e30
XS = 64.0
PSC = 16384.0
GTOP = 4.0
HTOP = 256.0
EPS = 1e-5
FAST_SLOTS = 10


def residual_graph_layers(nc, a, out, stop=None):
    ctx = ExitStack()
    with ctx:
        sems = {}

        def s(name):
            if name not in sems:
                sems[name] = ctx.enter_context(nc.semaphore(name))
            return sems[name]

        def sb(name, shape, dt=FP32, c=ctx):
            return c.enter_context(nc.sbuf_tensor(name, shape, dt))

        ident = sb("ident", [P, P])
        ident16 = sb("ident16", [P, P], FP16)
        stack_id = sb("stack_id", [P, F])
        x1 = sb("x1", [P, B, T, F])
        adj_mask = sb("adj_mask", [P, T, N], BF16)
        g_hi = sb("g_hi", [P, HEADS, P], FP16)
        g_lo = sb("g_lo", [P, HEADS, P], FP16)
        g_scale = sb("g_scale", [P, HEADS])
        w_out = sb("w_out", [P, HEADS, P])
        bh = sb("bh", [P, HEADS])
        b_out = sb("b_out", [P, F])
        ln_mean = sb("ln_mean", [P, T * B])
        ln_var = sb("ln_var", [P, T * B])

        L0 = ExitStack()
        x_nat = sb("x_nat", [P, T, B, F], c=L0)
        proj = sb("proj", [P, T, BP, WCOL], c=L0)
        adjT = sb("adjT", [P, T, N], c=L0)
        x_t = sb("x_t", [P, BP, N], c=L0)
        industry = x_t[:].rearrange("p a (t q) -> p (a t) q", t=2)
        g_sum = adjT[:, 0:T // 2, :].rearrange("p a (t q) -> p (a t) q", t=2)
        tmp_a = sb("tmp_a", [P, 2, N], c=L0)
        tmp_b = sb("tmp_b", [P, 2, N], c=L0)
        tmp_c = sb("tmp_c", [P, 2, N], c=L0)
        tmp_d = sb("tmp_d", [P, 2, N], c=L0)
        tri = sb("tri", [P, E], c=L0)
        slot_no = sb("slot_no", [P, E], c=L0)
        w_t = sb("w_t", [F, F], c=L0)
        w_cols = sb("w_cols", [F, 2], c=L0)
        w_block = sb("w_block", [P, WCOL], c=L0)
        node_block = sb("node_block", [P, P], c=L0)
        w_all = sb("w_all", [P, HEADS, P], c=L0)
        a_ge = sb("a_ge", [F, 1], c=L0)
        fc_w = sb("fc_w", [P, P], c=L0)
        fc_b = sb("fc_b", [P, 1], c=L0)
        av = sb("av", [P, 1], c=L0)
        av_all = sb("av_all", [P, P], c=L0)
        ones = sb("ones", [P, P], c=L0)
        g_abs = sb("g_abs", [P, HEADS], c=L0)
        g_max = sb("g_max", [P, HEADS], c=L0)
        g_inv = sb("g_inv", [P, HEADS], c=L0)
        mask_t = sb("mask_t", [P, N], c=L0)
        edge_bias = sb("edge_bias", [P, N], BF16, c=L0)
        rank = sb("rank", [E, N], c=L0)
        mask_n = sb("mask_n", [P, T, E], c=L0)
        node_cnt = sb("node_cnt", [P, T], c=L0)
        node_empty = sb("node_empty", [P, T], c=L0)
        edge_max = sb("edge_max", [P, BP], c=L0)
        edge_sum = sb("edge_sum", [P, BP], c=L0)
        edge_inv = sb("edge_inv", [P, BP], c=L0)
        agg = sb("agg", [E, B, F], c=L0)
        agg_t = sb("agg_t", [F, BF], c=L0)
        he_r = sb("he_r", [F, BF], c=L0)
        he_e = sb("he_e", [F, BF], c=L0)
        extra = sb("extra", [E, 17], c=L0)
        se_max = sb("se_max", [P, T, B], c=L0)
        bl = sb("bl", [P, T, B], c=L0)
        th = sb("th", [P, T, B], c=L0)
        wgt = sb("wgt", [P, T, B], c=L0)
        sx = sb("sx", [P, T, B], c=L0)
        vb = sb("vb", [P, T], c=L0)
        coef = sb("coef", [P, T, B], c=L0)
        coef_sum = sb("coef_sum", [P, T, B], c=L0)
        sel = mask_t[0:E, :]
        max_all = sb("max_all", [P, 1], c=L0)
        max_one = sb("max_one", [P, 1], c=L0)
        max_count = sb("max_count", [1, 1], I32, c=L0)
        deg = sb("deg", [P, T], c=L0)
        sc = sb("sc", [P, 2, T, B], c=L0)
        L0.close()

        ax = sb("ax", [P, N], FP16)
        x2 = sb("x2", [P, T, P], FP16)
        y_hi = sb("y_hi", [P, 2, N], FP16)
        y_lo = sb("y_lo", [P, 2, N], FP16)
        masked = sb("masked", [P, 2, N])
        probs = sb("probs", [P, 2, N])
        pt_hi = sb("pt_hi", [P, 2, T, HALF], FP16)
        pt_lo = sb("pt_lo", [P, 2, T, HALF], FP16)
        neg_max = sb("neg_max", [P, 2])
        sums = sb("sums", [P, T])
        sums_o = sb("sums_o", [P, T])
        rinv = sb("rinv", [P, T])
        rinv_o = sb("rinv_o", [P, T])
        cur_scale = sb("cur_scale", [P, 1])
        osum = sb("osum", [P, 2, HALF])
        onorm = sb("onorm", [P, HALF])
        w2 = sb("w2", [P, P])
        zc = sb("zc", [P, 2, HALF])
        zm = sb("zm", [P, 2, HALF])
        cat = sb("cat", [P, HEADS, N])
        h_abs = sb("h_abs", [P, 1])
        h_max = sb("h_max", [P, 1])
        h_unit = sb("h_unit", [P, 1])
        h_inv = sb("h_inv", [P, 1])
        h_scale = sb("h_scale", [P, 1])
        zo = sb("zo", [P, T, F])

        ps = ctx.enter_context(nc.psum_tensor("ps", [P, 8, HALF], FP32))

        def h_of(t, lo=0, hi=BP):
            return proj[:, t, lo:hi, 0:P]

        def layer_norm_act(act, tag, sq_out, centred):
            act.wait_ge(s(tag + "centred"), 1)
            act.activation(sq_out, centred, ACT.Square).then_inc(s(tag + "square"), 1)
            act.wait_ge(s(tag + "var"), 1)
            act.activation(ln_var[:], ln_var[:], ACT.Sqrt).then_inc(s(tag + "sqrt"), 1)

        def pair_scores(pe, j):
            src, b, c = j // 16, j // 2 % 8, j % 2
            pe.wait_ge(s("pair_tanh"), j + 1)
            for i in range(4):
                col = (src * T + c * 4 + i) * B + b
                last = nc.tensor.matmul(ps[:, 6, col:col + 1], tmp_c[:, j % 2, i * P:i * P + P], av[:], start=True, stop=True)
            last.then_inc(s("pair_score"), 1)

        chained = [0]

        def link(ins):
            chained[0] += 1
            ins.then_inc(s("dve_chain"), 1)
            nc.vector.wait_ge(s("dve_chain"), chained[0])

        def layer_norm_dve(dve, tag, xs, sq):
            v = nc.vector
            link(v.tensor_reduce(ln_mean[:], xs, axis=AX.X, op=ALU.add))
            link(v.tensor_scalar(ln_mean[:], ln_mean[:], 1.0 / F, None, ALU.mult))
            v.tensor_tensor(xs, xs, ln_mean[:].unsqueeze(2).to_broadcast([P, T * B, F]), ALU.subtract).then_inc(s(tag + "centred"), 1)
            dve.wait_ge(s(tag + "square"), 1)
            link(v.tensor_reduce(ln_var[:], sq, axis=AX.X, op=ALU.add))
            v.tensor_scalar(ln_var[:], ln_var[:], 1.0 / F, EPS, ALU.mult, ALU.add).then_inc(s(tag + "var"), 1)
            dve.wait_ge(s(tag + "sqrt"), 1)
            link(v.reciprocal(ln_var[:], ln_var[:]))

        block = ctx.enter_context(nc.Block())

        @block.sync
        def _(sp):
            sp.dma_start(ident[:], a["consts"][:, 0:P]).then_inc(s("consts_in"), 16)
            sp.dma_start(tri[:], a["consts"][:, P:P + E]).then_inc(s("consts_in"), 16)
            sp.dma_start(slot_no[:], a["consts"][:, P + E:P + 2 * E]).then_inc(s("consts_in"), 16)
            for b in range(B):
                sp.dma_start(x_nat[:, :, b, :], a["x"][b].rearrange("(t p) f -> p t f", p=P)).then_inc(s("x_in"), 16)
            for half in range(2):
                sp.dma_start(mask_t[half * E:half * E + E, :], a["HT"]).then_inc(s("ht_in"), 16)
            sp.dma_start(mask_n[:], a["H"].rearrange("(t p) e -> p t e", p=P)).then_inc(s("hn_in"), 16)
            for t in range(T):
                sp.dma_start(adjT[:, t, :], a["adjT"][t * P:t * P + P, :]).then_inc(s("adjT_in"), 16)
            for t in range(T):
                if t >= 2:
                    sp.wait_ge(s("mask_made"), t - 1)
                sp.dma_start(tmp_d[:, t % 2, :], a["adj"][t * P:t * P + P, :]).then_inc(s(f"adj_in{t % 2}"), 16)
            if stop != "x1":
                sp.wait_ge(s("x1_ready"), 2)
                for half in range(2):
                    sp.dma_start(w2[half * F:half * F + F, :], a["Wh"][0]).then_inc(s("w2_in"), 16)
                with sp.Fori(1, B * HEADS) as head:
                    sp.wait_ge(s("projected"), 2 * head + 1)
                    for half in range(2):
                        sp.dma_start(w2[half * F:half * F + F, :], a["Wh"][bass.ds(head % HEADS, 1)].rearrange("a f d -> (a f) d")).then_inc(s("w2_in"), 16)
                for q in range(4):
                    sp.wait_ge(s("ln1_out"), q + 1)
                    sp.dma_start(out[2 * q:2 * q + 2].rearrange("b (t p) f -> p b t f", p=P), x1[:, 2 * q:2 * q + 2]).then_inc(s("out_stored"), 16)
                sp.wait_ge(s("out_stored"), 64)
            if stop == "x1":
                sp.wait_ge(s("x1_ready"), 2)
                sp.wait_ge(s("wo_in"), 64)
                sp.dma_start(out.rearrange("b (t p) f -> p b t f", p=P), x1[:]).then_inc(s("out_stored"), 16)
                sp.wait_ge(s("out_stored"), 16)

        @block.scalar
        def _(act):
            act.dma_start(w_t[:], a["WT"]).then_inc(s("w_in"), 16)
            act.dma_start(w_cols[:, 0:1], a["a_node"]).then_inc(s("w_in"), 16)
            act.dma_start(w_cols[:, 1:2], a["a_gn"]).then_inc(s("w_in"), 16)
            act.wait_ge(s("w_block_zero"), 1)
            for half in range(2):
                r = slice(half * F, half * F + F)
                act.dma_start(w_block[r, half * F:half * F + F], a["W"]).then_inc(s("wb_in"), 16)
                act.dma_start(w_block[r, P + half * F:P + half * F + F], a["W_ind"]).then_inc(s("wb_in"), 16)
                act.dma_start(fc_w[r, :], a["fcW"]).then_inc(s("fc_in"), 16)
                act.dma_start(w_all[:, :, r], a["WhT"].rearrange("h d f -> d h f")).then_inc(s("wh_in"), 16)
                act.dma_start(w_out[:, :, r], a["W_out"].rearrange("(h d) f -> d h f", d=HID)).then_inc(s("wo_in"), 16)
            act.dma_start(fc_b[:], a["fcb"]).then_inc(s("fc_in"), 16)
            act.dma_start(av[:], a["av"]).then_inc(s("fc_in"), 16)
            act.dma_start(a_ge[:], a["a_ge"]).then_inc(s("fc_in"), 16)
            act.dma_start(bh[:], a["bhT"]).then_inc(s("wo_in"), 16)
            act.dma_start(b_out[:], a["b_out"].partition_broadcast(P)).then_inc(s("wo_in"), 16)
            for q in range(1, 2 * BP, 2):
                act.wait_ge(s("xt_made"), q + 1)
                act.activation(x_t[:, q // 2, HALF:N], ps[:, q % 4, :], ACT.Copy).then_inc(s("xt_out1"), 1)
            for i in range(1, T * BP, 2):
                act.wait_ge(s("proj_made"), i + 1)
                act.activation(proj[:, i // BP, i % BP, :], ps[:, i % 4, 0:WCOL], ACT.Copy).then_inc(s("proj_out1"), 1)
            for bp in range(BP):
                act.wait_ge(s("edge_masked"), bp + 1)
                if bp:
                    act.wait_ge(s("edge_tr"), bp)
                act.activation(tmp_b[:, 0, :], tmp_a[:, 0, :], ACT.Exp, scale=-1.0, bias=edge_max[:, bp:bp + 1],
                               accum_out=edge_sum[:, bp:bp + 1]).then_inc(s("edge_exp"), 1)
                act.wait_ge(s("edge_tr"), bp + 1)
                if bp:
                    act.wait_ge(s("agg_made"), bp)
                act.activation(tmp_c[:, 0, :], ps[:, 6:8, :], ACT.Copy).then_inc(s("edge_tr_out"), 1)
            act.wait_ge(s("aggt_out"), 1)
            act.activation(he_r[:], agg_t[:], ACT.Relu).then_inc(s("he_re"), 1)
            act.activation(he_e[:], agg_t[:], ACT.Exp).then_inc(s("he_re"), 1)
            act.wait_ge(s("he_hid"), 1)
            act.wait_ge(s("fc_in"), 80)
            act.activation(tmp_b[:, 1, 0:BF], ps[:, 5, :], ACT.Tanh, bias=fc_b[:]).then_inc(s("he_tanh"), 1)

            def slots(tag, start, end):
                act.sem_inc(s(tag + "exp"), 2)
                act.sem_inc(s(tag + "th"), 1)
                act.sem_inc(s(tag + "coef"), 1)
                with act.Fori(start, end) as k:
                    k0 = k - start
                    act.wait_ge(s(tag + "bl"), k0 + 1)
                    act.activation(th[:], bl[:], ACT.Tanh, scale=0.5).then_inc(s(tag + "th"), 1)
                    act.wait_ge(s(tag + "sx"), k0 + 1)
                    act.wait_ge(s(tag + "vc"), 4 * k0 + 1)
                    act.activation(coef[:], sx[:], ACT.Exp).then_inc(s(tag + "coef"), 1)
                    for c in range(4):
                        j = k0 * 4 + c
                        act.wait_ge(s(tag + "z"), j + 1)
                        act.wait_ge(s(tag + "v"), j + 1)
                        act.activation(tmp_b[:, c % 2, :], tmp_a[:, c % 2, :], ACT.Relu).then_inc(s(tag + "relu"), 1)
                        act.activation(tmp_c[:, c % 2, :], tmp_a[:, c % 2, :], ACT.Exp).then_inc(s(tag + "exp"), 1)
            def rest(start, end):
                act.wait_ge(s("max_count"), 1)
                many = act.value_load(max_count[0:1, 0:1], min_val=0, max_val=E)
                with act.If(many > start):
                    act.wait_ge(s("f_g"), 4 * start + 2)
                    act.wait_ge(s("f_csum"), start + 1)
                    slots("s_", start, end)
                    act.wait_ge(s("s_g"), 4 * (end - start) + 2)
                    act.wait_ge(s("s_csum"), end - start + 1)

            slots("f_", 0, FAST_SLOTS)
            rest(FAST_SLOTS, E)

            for j in range(32):
                act.wait_ge(s("pair_hid"), j + 1)
                if j >= 2:
                    act.wait_ge(s("pair_score"), j - 1)
                act.activation(tmp_c[:, j % 2, 0:HALF], ps[:, 4 + j % 2, :], ACT.Tanh, bias=fc_b[:]).then_inc(s("pair_tanh"), 1)
            act.wait_ge(s("pair_diff"), 1)
            act.activation(th[:], bl[:], ACT.Tanh, scale=0.5).then_inc(s("pair_th"), 1)
            layer_norm_act(act, "ln0_", g_sum.rearrange("p t (b f) -> p (t b) f", b=B),
                           industry.rearrange("p t (b f) -> p (t b) f", b=B))

            if stop == "x1":
                return

            def exp(g, t, c, out_unit=False):
                act.wait_ge(s("masked"), g + 2)
                if out_unit:
                    if t == 0:
                        act.wait_ge(s("sums_o_read"), c + 1)
                    acc = sums_o
                else:
                    if t % 4 == 0:
                        act.wait_ge(s("rinv"), c + 1)
                    acc = sums
                act.wait_ge(s("pT"), g + 1)
                act.activation(probs[:, t % 2, :], masked[:, t % 2, :], ACT.Exp, scale=-1.0, bias=neg_max[:, t % 2:t % 2 + 1],
                               accum_out=acc[:, t:t + 1]).then_inc(s("probs"), 1)

            def hi(g, t, c):
                if t % 4 == 0:
                    act.wait_ge(s("pv"), 4 * c + 4)
                act.wait_ge(s("pT"), g + 3)
                act.activation(pt_hi[:, t // 4, :, t % 4 * P:t % 4 * P + P],
                               ps[:, 2 + 2 * (t % 2):4 + 2 * (t % 2), :].rearrange("p a (m n) -> p (a m) n", n=P), ACT.Copy, scale=PSC).then_inc(s("hi"), 1)

            def take_sum(c, cp, cc):
                act.wait_ge(s("pv"), 4 * c + 12)
                act.wait_ge(s("normed"), cp + 1)
                act.activation(osum[:, cc, :], ps[:, 6, :], ACT.Copy).then_inc(s("osum"), 1)

            def take_proj(cp, cc, h):
                act.wait_ge(s("projected"), cp + 2)
                act.wait_ge(s("cat"), cp + 1)
                act.nop(nofuse=True)
                act.activation(zc[:, cc, :], ps[:, 7, :], ACT.Identity, scale=1.0 / (XS * PSC), bias=bh[:, bass.ds(h, 1)]).then_inc(s("z"), 1)

            def take_y(v, cc, u):
                act.wait_ge(s("y"), 2 * v + cc + 1)
                act.wait_ge(s("scores"), 8 * u + 1)
                act.nop(nofuse=True)
                act.activation(y_hi[:, bass.ds(v % 2, 1), cc * HALF:cc * HALF + HALF].rearrange("p a n -> p (a n)"), ps[:, 7, :], ACT.Copy).then_inc(s("y_hi"), 1)

            def head(b, h, first, last):
                v, u = b * HEADS + h, b * (HEADS + 1) + h
                for t in range(T):
                    g = u * T + t
                    if t == 3 and not first:
                        take_sum(2 * u - 1, 2 * v - 1, 1)
                    if t == 7:
                        take_sum(2 * u, 2 * v, 0)
                    if t == 2 and not first:
                        take_proj(2 * v - 2, 0, h - 1)
                    if t == 6 and not first:
                        take_proj(2 * v - 1, 1, h - 1)
                    hi(g, t, 2 * u + t // 4)
                    if t < 7:
                        exp(g + 1, t + 1, 2 * v + (t + 1) // 4)
                    elif not last:
                        exp(g + 1, 0, 2 * v + 2)
                    if t in (3, 7) and not last:
                        take_y(v + 1, t // 4, u)

            act.wait_ge(s("x1_ready"), 2)
            act.wait_ge(s("wo_in"), 64)
            act.sem_inc(s("probs"), 2)
            act.sem_inc(s("osum"), 1)
            with act.Fori(0, B) as b:
                act.wait_ge(s("xt16"), b + 1)
                act.activation(ax[:], ps[:, 7, :].bitcast(FP16), ACT.Copy).then_inc(s("ax"), 1)
                for cc in range(2):
                    take_y(b * HEADS, cc, b * (HEADS + 1))
                exp(b * (HEADS + 1) * T, 0, 2 * b * HEADS)
                head(b, 0, True, False)
                with act.Fori(1, HEADS - 1) as h:
                    head(b, h, False, False)
                head(b, HEADS - 1, False, True)
                v, u = b * HEADS + HEADS, b * (HEADS + 1) + HEADS
                take_proj(2 * v - 2, 0, HEADS - 1)
                take_sum(2 * u - 1, 2 * v - 1, 1)
                take_proj(2 * v - 1, 1, HEADS - 1)
                act.wait_ge(s("h_parts"), 2 * b + 2)
                act.activation(ax[0:F, :], y_hi[0:F, 0, :], ACT.Copy).then_inc(s("h_ax"), 1)
                act.activation(ax[F:P, :], y_lo[F:P, 0, :], ACT.Copy).then_inc(s("h_ax"), 1)
                act.wait_ge(s("h_t"), b + 1)
                act.activation(x2[:], ps[:, 7, :].bitcast(FP16), ACT.Copy).then_inc(s("h_x2"), 1)
                exp(u * T, 0, b, True)
                for t in range(T):
                    if t == 7:
                        act.wait_ge(s("pv"), 4 * (2 * u) + 12)
                        act.wait_ge(s("normed"), 2 * v + 2)
                        act.activation(osum[:, 0, :], ps[:, 6, :], ACT.Copy).then_inc(s("osum"), 1)
                    hi(u * T + t, t, 2 * u + t // 4)
                    if t < 7:
                        exp(u * T + t + 1, t + 1, b, True)
                act.wait_ge(s("pv"), 4 * (2 * u + 1) + 12)
                act.activation(osum[:, 1, :], ps[:, 6, :], ACT.Copy).then_inc(s("osum"), 1)
            layer_norm_act(act, "ln1_", cat[:, 0:4, :].rearrange("p a (c f) -> p (a c) f", f=F), x1[:].rearrange("p b t f -> p (b t) f"))

        @block.tensor
        def _(pe):
            pe.wait_ge(s("w_in"), 48)
            pe.wait_ge(s("consts_in"), 48)
            nc.tensor.matmul(ps[0:F, 4, 0:2], w_t[:], w_cols[:], start=True, stop=True)
            nc.tensor.matmul(ps[F:P, 4, 0:2], w_t[:], w_cols[:], start=True, stop=True).then_inc(s("wa_made"), 1)
            pe.wait_ge(s("wh_in"), 32)
            for h in range(HEADS):
                last = nc.tensor.matmul(ps[:, 5, h * F:h * F + F], w_all[:, h, :], w_all[:, h, 0:F], start=True, stop=True)
            last.then_inc(s("g_made"), 1)
            pe.wait_ge(s("x_in"), 16 * B)
            for q in range(2 * BP):
                if q >= 4:
                    pe.wait_ge(s(f"xt_out{q % 2}"), (q - 4) // 2 + 1)
                for i in range(4):
                    t = (q % 2) * 4 + i
                    last = nc.tensor.transpose(ps[:, q % 4, i * P:i * P + P],
                                               x_nat[:, t, q // 2 * 2:q // 2 * 2 + 2, :].rearrange("p b f -> p (b f)"), ident[:])
                last.then_inc(s("xt_made"), 1)
            pe.wait_ge(s("xt_out0"), BP)
            pe.wait_ge(s("xt_out1"), BP)
            pe.wait_ge(s("w_ready"), 1)
            for i in range(T * BP):
                if i >= 4:
                    pe.wait_ge(s(f"proj_out{i % 2}"), (i - 4) // 2 + 1)
                nc.tensor.matmul(ps[:, i % 4, 0:WCOL], x_t[:, i % BP, i // BP * P:i // BP * P + P], w_block[:],
                                 start=True, stop=True).then_inc(s("proj_made"), 1)
            pe.wait_ge(s("mask_t_made"), 1)
            pe.wait_ge(s("ones_made"), 1)
            for c in range(2):
                last = nc.tensor.matmul(ps[0:E, 6 + c, :], ones[0:E, 0:E], mask_t[0:E, c * HALF:c * HALF + HALF], start=True, stop=True)
            last.then_inc(s("cnt_made"), 1)
            pe.wait_ge(s("eff_made"), 1)
            for c in range(2):
                last = nc.tensor.matmul(ps[0:E, 6 + c, :], tri[0:E, :], tmp_a[0:E, 1, c * HALF:c * HALF + HALF], start=True, stop=True)
            last.then_inc(s("rank_made"), 1)
            pe.wait_ge(s("g_out"), 1)
            pe.wait_ge(s("rank_out"), 1)
            for bp in range(BP):
                if bp:
                    pe.wait_ge(s("edge_lk"), bp)
                for c in range(2):
                    last = nc.tensor.matmul(ps[:, 4 + c, :], node_block[:], x_t[:, bp, c * HALF:c * HALF + HALF], start=True, stop=True)
                last.then_inc(s("edge_s"), 1)
                pe.wait_ge(s("edge_exp"), bp + 1)
                if bp:
                    pe.wait_ge(s("edge_tr_out"), bp)
                for t in range(T):
                    last = nc.tensor.transpose(ps[:, 6 + t // 4, t % 4 * P:t % 4 * P + P], tmp_b[:, 0, t * P:t * P + P], ident[:])
                last.then_inc(s("edge_tr"), 1)
                pe.wait_ge(s("edge_tr_out"), bp + 1)
                if bp == 0:
                    pe.wait_ge(s("proj_out0"), T * BP // 2)
                    pe.wait_ge(s("proj_out1"), T * BP // 2)
                for t in range(T):
                    last = nc.tensor.matmul(ps[:, bp, 0:P], tmp_c[:, 0, t * P:t * P + P], proj[:, t, bp, 0:P], start=(t == 0), stop=(t == T - 1))
                last.then_inc(s("agg_made"), 1)
            pe.wait_ge(s("agg_out"), 2 * BP)
            for b in range(B):
                last = nc.tensor.transpose(ps[0:F, 4, b * E:b * E + E], agg[:, b, :], ident[0:E, 0:E])
            last.then_inc(s("aggt_made"), 1)
            pe.wait_ge(s("he_made"), 1)
            pe.wait_ge(s("fc_in"), 80)
            nc.tensor.matmul(ps[:, 5, :], fc_w[0:F, :], he_r[:], start=True, stop=True).then_inc(s("he_hid"), 1)
            pe.wait_ge(s("he_tanh"), 1)
            for b in range(B):
                nc.tensor.matmul(ps[0:E, 7, b:b + 1], agg_t[:, b * E:b * E + E], a_ge[:], start=True, stop=True)
                nc.tensor.matmul(ps[0:E, 7, 8 + b:9 + b], tmp_b[:, 1, b * E:b * E + E], av[:], start=True, stop=True)
            pe.wait_ge(s("av_all_made"), 1)
            nc.tensor.matmul(ps[:, 6, :], av_all[:], tmp_b[:, 1, 0:BF], start=True, stop=True).then_inc(s("se_made"), 1)
            pe.wait_ge(s("adjT_in"), 16 * T)
            pe.wait_ge(s("extra_out"), 1)
            for t in range(T):
                for m in range(T):
                    last = nc.tensor.matmul(ps[:, 7, 16 + t:17 + t], adjT[:, m, t * P:t * P + P], ones[:, 0:1], start=(m == 0), stop=(m == T - 1))
            last.then_inc(s("deg_made"), 1)
            for t in range(T):
                if t == 0:
                    pe.wait_ge(s("agg_out"), 2 * BP)
                if t >= 4:
                    pe.wait_ge(s("ind_out"), t - 3)
                for m in range(T):
                    last = nc.tensor.matmul(ps[:, t % 4, :], adjT[:, m, t * P:t * P + P], proj[:, m, :, P:2 * P], start=(m == 0), stop=(m == T - 1))
                last.then_inc(s("ind_made"), 1)
            pe.wait_ge(s("ind_out"), T)
            pe.wait_ge(s("neg_ident"), 1)

            def slots(tag, start, end):
                pe.sem_inc(s(tag + "diff"), 1)
                pe.sem_inc(s(tag + "extra"), 1)
                with pe.Fori(start, end) as k:
                    k0 = k - start
                    pe.wait_ge(s(tag + "sel"), k0 + 1)
                    pe.wait_ge(s(tag + "extra_read"), 3 * k0 + 3)
                    for t in range(T):
                        last = nc.tensor.matmul(ps[:, 4, t * 17:t * 17 + 17], sel[:, t * P:t * P + P], extra[:], start=True, stop=True)
                    last.then_inc(s(tag + "extra"), 1)
                    for c in range(4):
                        j = k0 * 4 + c
                        pe.wait_ge(s(tag + "zw"), j + 1)
                        for u in range(2):
                            t = 2 * c + u
                            nc.tensor.matmul(ps[:, 2 * (c % 2) + u, :], sel[:, t * P:t * P + P], agg[:].rearrange("e b f -> e (b f)"), start=True, stop=False)
                            last = nc.tensor.matmul(ps[:, 2 * (c % 2) + u, :], av_all[:], h_of(t), start=False, stop=True)
                        last.then_inc(s(tag + "diff"), 1)
            def rest(start, end):
                pe.wait_ge(s("max_count"), 1)
                many = pe.value_load(max_count[0:1, 0:1], min_val=0, max_val=E)
                with pe.If(many > start):
                    pe.wait_ge(s("f_g"), 4 * start + 2)
                    pe.wait_ge(s("f_csum"), start + 1)
                    slots("s_", start, end)
                    pe.wait_ge(s("s_g"), 4 * (end - start) + 2)
                    pe.wait_ge(s("s_csum"), end - start + 1)

            slots("f_", 0, FAST_SLOTS)
            rest(FAST_SLOTS, E)

            j = 0
            for q in range(8):
                src = (industry, g_sum)[q // 4]
                bp = q % 4
                if q == 0:
                    pe.wait_ge(s("f_zw"), 4 * FAST_SLOTS + 2)
                if q == 4:
                    pe.wait_ge(s("g_final"), 1)
                if q >= 2:
                    pe.wait_ge(s("pair_t_out"), q - 1)
                for t in range(T):
                    last = nc.tensor.transpose(ps[:, 2 * (q % 2) + t // 4, t % 4 * P:t % 4 * P + P], src[:, t, bp * P:bp * P + P], ident[:])
                last.then_inc(s("pair_t"), 1)
                pe.wait_ge(s("pair_t_out"), q + 1)
                for half in range(2):
                    for c in range(2):
                        if j == 0:
                            pe.wait_ge(s("f_extra_read"), 3 * FAST_SLOTS + 3)
                        if j >= 2:
                            pe.wait_ge(s("pair_tanh"), j - 1)
                        r = slice(half * F, half * F + F)
                        nc.tensor.matmul(ps[:, 4 + j % 2, :], fc_w[r, :], tmp_a[r, q % 2, c * HALF:c * HALF + HALF], start=True, stop=True).then_inc(s("pair_hid"), 1)
                        if j >= 1:
                            pair_scores(pe, j - 1)
                        j += 1
            pair_scores(pe, j - 1)

            if stop == "x1":
                return

            def scores(g, t, par, ready):
                pe.wait_ge(s("masked"), g + 1)
                if ready is not None:
                    pe.wait_ge(s("y_out"), ready)
                for part, y in enumerate((y_hi, y_lo)):
                    for c in range(2):
                        last = nc.tensor.matmul(ps[:, c, :], y[:, par, t * P:t * P + P] if isinstance(par, int) else y[:, bass.ds(par, 1), t * P:t * P + P].rearrange("p a n -> p (a n)"),
                                                ax[:, c * HALF:c * HALF + HALF], start=(part == 0), stop=(part == 1), skip_group_check=True)
                last.then_inc(s("scores"), 1)

            def transpose(g, t):
                pe.wait_ge(s("probs"), g + 3)
                pe.wait_ge(s("lo"), g + 1)
                for m in range(T):
                    last = nc.tensor.transpose(ps[:, 2 + 2 * (t % 2) + m // 4, m % 4 * P:m % 4 * P + P], probs[:, t % 2, m * P:m * P + P], ident[:])
                last.then_inc(s("pT"), 1)

            def weigh(c, cc, part):
                if part == 0:
                    pe.wait_ge(s("lo"), 4 * c + 6)
                    pe.wait_ge(s("osum"), c + 1)
                for m in (2 * part, 2 * part + 1):
                    nc.tensor.matmul(ps[:, 6, :], x2[:, m, :], pt_hi[:, cc, m, :], start=(m == 0), stop=False)
                    last = nc.tensor.matmul(ps[:, 6, :], x2[:, m, :], pt_lo[:, cc, m, :], start=False, stop=(m == T - 1))
                last.then_inc(s("pv"), 1)

            def repeat_inverse(cp, cc):
                pe.wait_ge(s("rinv"), cp + 3)
                for i in range(4):
                    last = nc.tensor.transpose(ps[:, 7, i * P:i * P + P], rinv[:, 4 * cc + i:4 * cc + i + 1].to_broadcast([P, P]), ident[:])
                last.then_inc(s("rinv_rows"), 1)

            def project(cp, cc, v):
                pe.wait_ge(s("normed"), cp + 3)
                pe.wait_ge(s("w2_in"), 32 * v + 32)
                nc.tensor.matmul(ps[:, 7, :], w2[:], onorm[:], start=True, stop=True).then_inc(s("projected"), 1)

            def make_y(h, cc):
                ch = slice(cc * HALF, cc * HALF + HALF)
                if isinstance(h, int):
                    hi_w, lo_w = g_hi[:, h, :], g_lo[:, h, :]
                else:
                    hi_w, lo_w = (w[:, bass.ds(h, 1), :].rearrange("p a f -> p (a f)") for w in (g_hi, g_lo))
                nc.tensor.matmul(ps[:, 7, :], hi_w, ax[:, ch], start=True, stop=False)
                nc.tensor.matmul(ps[:, 7, :], lo_w, ax[:, ch], start=False, stop=True).then_inc(s("y"), 1)

            def head(b, h, first, last):
                v, u = b * HEADS + h, b * (HEADS + 1) + h
                for t in range(T):
                    g = u * T + t
                    if t < 7:
                        scores(g + 1, t + 1, v % 2, 2 * v + 2 if t == 3 else None)
                    elif not last:
                        scores(g + 1, 0, (v + 1) % 2, 2 * v + 3)
                    if t >= 4:
                        weigh(2 * u, 0, t - 4)
                    elif not first:
                        weigh(2 * u - 1, 1, t)
                    transpose(g, t)
                    if t == 0 and not first:
                        pe.wait_ge(s("y_out"), 2 * v + 2)
                        repeat_inverse(2 * v - 2, 0)
                    if t == 1 and not first:
                        project(2 * v - 2, 0, v - 1)
                    if t == 2 and not last:
                        if first:
                            pe.wait_ge(s("y_out"), 2 * v + 2)
                        else:
                            pe.wait_ge(s("z"), 2 * v - 1)
                        make_y(h + 1, 0)
                    if t == 4 and not first:
                        if last:
                            pe.wait_ge(s("z"), 2 * v - 1)
                        else:
                            pe.wait_ge(s("y_out"), 2 * v + 3)
                        repeat_inverse(2 * v - 1, 1)
                    if t == 5 and not first:
                        project(2 * v - 1, 1, v - 1)
                    if t == 6 and not last:
                        if first:
                            pe.wait_ge(s("y_out"), 2 * v + 3)
                        else:
                            pe.wait_ge(s("z"), 2 * v)
                        make_y(h + 1, 1)

            pe.wait_ge(s("x1_ready"), 2)
            pe.wait_ge(s("wo_in"), 64)
            pe.sem_inc(s("pT"), 2)
            pe.sem_inc(s("scores"), 1)
            pe.sem_inc(s("projected"), 1)
            pe.sem_inc(s("h_made"), 1)
            pe.sem_inc(s("pv"), 8)
            pe.sem_inc(s("rinv_rows"), 2)
            with pe.Fori(0, B) as b:
                pe.wait_ge(s("x2"), 2 * b + 2)
                pe.wait_ge(s("z_out"), b + 1)
                for t in range(T):
                    last_t = nc.tensor.transpose(ps[:, 7, :].bitcast(FP16)[:, t * P:t * P + P], x2[:, t, :], ident16[:])
                last_t.then_inc(s("xt16"), 1)
                pe.wait_ge(s("ax"), b + 1)
                make_y(0, 0)
                pe.wait_ge(s("y_out"), 2 * HEADS * b + 1)
                make_y(0, 1)
                scores(b * (HEADS + 1) * T, 0, 0, 2 * HEADS * b + 1)
                head(b, 0, True, False)
                with pe.Fori(1, HEADS - 1) as h:
                    head(b, h, False, False)
                head(b, HEADS - 1, False, True)
                v, u = b * HEADS + HEADS, b * (HEADS + 1) + HEADS
                pe.wait_ge(s("z"), 2 * v - 2)
                repeat_inverse(2 * v - 2, 0)
                project(2 * v - 2, 0, v - 1)
                for part in range(4):
                    weigh(2 * u - 1, 1, part)
                pe.wait_ge(s("z"), 2 * v - 1)
                repeat_inverse(2 * v - 1, 1)
                project(2 * v - 1, 1, v - 1)
                pe.wait_ge(s("cat"), 2 * v + 2)
                pe.wait_ge(s("masked"), u * T + 1)
                for c in range(2):
                    for h in range(HEADS):
                        last_t = nc.tensor.matmul(ps[:, c, :], w_out[:, h, :], cat[:, h, c * HALF:c * HALF + HALF], start=(h == 0), stop=(h == HEADS - 1))
                last_t.then_inc(s("h_made"), 1)
                pe.wait_ge(s("h_ax"), 2 * b + 2)
                for t in range(T):
                    last_t = nc.tensor.transpose(ps[:, 7, :].bitcast(FP16)[:, t * P:t * P + P], ax[:, t * P:t * P + P], ident16[:])
                last_t.then_inc(s("h_t"), 1)
                scores(u * T, 0, 0, None)
                pe.wait_ge(s("h_x2"), b + 1)
                for t in range(T):
                    if t < 7:
                        scores(u * T + t + 1, t + 1, 0, None)
                    if t >= 4:
                        weigh(2 * u, 0, t - 4)
                    transpose(u * T + t, t)
                for part in range(4):
                    weigh(2 * u + 1, 1, part)
                pe.wait_ge(s("osum"), 2 * u + 3)
                for t in range(T):
                    last_t = nc.tensor.matmul(ps[:, 7, t * F:t * F + F], osum[:, t // 4, t % 4 * P:t % 4 * P + P], stack_id[:], start=True, stop=True)
                last_t.then_inc(s("zo"), 1)

        @block.vector
        def _(dve):
            v = nc.vector
            v.memset(w_block[:], 0.0).then_inc(s("w_block_zero"), 1)
            link(v.memset(node_block[:], 0.0))
            v.memset(ones[:], 1.0).then_inc(s("ones_made"), 1)
            dve.wait_ge(s("consts_in"), 48)
            v.tensor_copy(ident16[:], ident[:])
            v.tensor_tensor(stack_id[:], ident[:, 0:F], ident[:, F:P], ALU.add)
            dve.wait_ge(s("wa_made"), 1)
            dve.wait_ge(s("w_block_zero"), 1)
            for half in range(2):
                r = slice(half * F, half * F + F)
                v.tensor_copy(w_block[r, 2 * P + half:2 * P + half + 1], ps[r, 4, 1:2])
                v.tensor_copy(node_block[r, half * F:half * F + F], ps[r, 4, 0:1].to_broadcast([F, F])).then_inc(s("wa_out"), 1)
            dve.wait_ge(s("wb_in"), 64)
            dve.wait_ge(s("wa_out"), 2)
            v.nop().then_inc(s("w_ready"), 1)
            for q in range(0, 2 * BP, 2):
                dve.wait_ge(s("xt_made"), q + 1)
                v.tensor_copy(x_t[:, q // 2, 0:HALF], ps[:, q % 4, :]).then_inc(s("xt_out0"), 1)
            dve.wait_ge(s("g_made"), 1)
            gp = ps[:, 5, :].rearrange("p (h f) -> p h f", h=HEADS)
            v.tensor_reduce(g_abs[:], gp, axis=AX.X, op=ALU.max, apply_absolute_value=True).then_inc(s("g_abs"), 1)
            dve.wait_ge(s("g_max"), 1)
            v.tensor_scalar(g_max[:], g_max[:], 1.0 / GTOP, 1e-30, ALU.mult, ALU.max).then_inc(s("g_max"), 1)
            dve.wait_ge(s("g_max"), 2)
            link(v.reciprocal(g_inv[:], g_max[:]))
            v.tensor_scalar(g_scale[:], g_max[:], -1.0 / (XS * XS), None, ALU.mult)
            for dup in range(2):
                link(v.tensor_tensor(g_hi[:, :, dup * F:dup * F + F], gp, g_inv[:].unsqueeze(2).to_broadcast([P, HEADS, F]), ALU.mult))
            gs = tmp_a[:, 0, 0:BF].rearrange("p (h f) -> p h f", h=HEADS)
            link(v.tensor_tensor(gs, gp, g_inv[:].unsqueeze(2).to_broadcast([P, HEADS, F]), ALU.mult))
            for dup in range(2):
                v.tensor_tensor(g_lo[:, :, dup * F:dup * F + F], gs, g_hi[:, :, 0:F], ALU.subtract).then_inc(s("g_out"), 1)
            for i in range(0, T * BP, 2):
                dve.wait_ge(s("proj_made"), i + 1)
                v.tensor_copy(proj[:, i // BP, i % BP, :], ps[:, i % 4, 0:WCOL]).then_inc(s("proj_out0"), 1)
            dve.wait_ge(s("ht_in"), 32)
            v.tensor_scalar(mask_t[:], mask_t[:], 0.0, None, ALU.is_gt).then_inc(s("mask_t_made"), 1)
            dve.wait_ge(s("mask_t_made"), 1)
            link(v.tensor_scalar(edge_bias[:], mask_t[:], -MASKED, MASKED, ALU.mult, ALU.add))
            dve.wait_ge(s("cnt_made"), 1)
            dve.wait_ge(s("g_out"), 2)
            v.scalar_tensor_tensor(tmp_a[0:E, 1, :], ps[0:E, 6:8, :].rearrange("p a b -> p (a b)"), 0.0, mask_t[0:E, :], ALU.is_equal, ALU.add).then_inc(s("eff_made"), 1)
            dve.wait_ge(s("rank_made"), 1)
            dve.wait_ge(s("eff_made"), 1)
            v.tensor_tensor(rank[:], ps[0:E, 6:8, :].rearrange("p a b -> p (a b)"), tmp_a[0:E, 1, :], ALU.mult).then_inc(s("rank_out"), 1)
            link(v.memset(max_all[:], 0.0))
            dve.wait_ge(s("rank_out"), 1)
            v.tensor_reduce(max_all[0:E, :], rank[:], axis=AX.X, op=ALU.max).then_inc(s("max_all"), 1)
            dve.wait_ge(s("hn_in"), 16)
            link(v.tensor_scalar(mask_n[:], mask_n[:], 0.0, None, ALU.is_gt))
            link(v.tensor_reduce(node_cnt[:], mask_n[:], axis=AX.X, op=ALU.add))
            link(v.tensor_scalar(node_empty[:], node_cnt[:], 0.0, None, ALU.is_equal))
            link(v.tensor_tensor(mask_n[:], mask_n[:], node_empty[:].unsqueeze(2).to_broadcast([P, T, E]), ALU.add))
            link(v.tensor_scalar(mask_n[:], mask_n[:], -MASKED, MASKED, ALU.mult, ALU.add))
            for bp in range(BP):
                dve.wait_ge(s("edge_s"), bp + 1)
                if bp:
                    dve.wait_ge(s("edge_exp"), bp)
                e_s = ps[:, 4:6, :].rearrange("p a b -> p (a b)")
                link(v.tensor_copy(tmp_a[:, 1, :], e_s))
                v.scalar_tensor_tensor(tmp_a[:, 1, :], e_s, 0.2, tmp_a[:, 1, :], ALU.mult, ALU.max).then_inc(s("edge_lk"), 1)
                dve.wait_ge(s("edge_lk"), bp + 1)
                v.tensor_tensor_reduce(out=tmp_a[:, 0, :], in0=tmp_a[:, 1, :], in1=edge_bias[:], scale=-1.0, scalar=3e38,
                                       op0=ALU.add, op1=ALU.min, accum_out=edge_max[:, bp:bp + 1]).then_inc(s("edge_masked"), 1)
                dve.wait_ge(s("edge_exp"), bp + 1)
                link(v.reciprocal(edge_inv[:, bp:bp + 1], edge_sum[:, bp:bp + 1]))
                dve.wait_ge(s("agg_made"), bp + 1)
                for half in range(2):
                    r = slice(half * F, half * F + F)
                    v.tensor_scalar(agg[:, 2 * bp + half, :], ps[r, bp, r], edge_inv[r, bp:bp + 1], None, ALU.mult).then_inc(s("agg_out"), 1)
            dve.wait_ge(s("aggt_made"), 1)
            v.tensor_copy(agg_t[:], ps[0:F, 4, :]).then_inc(s("aggt_out"), 1)
            dve.wait_ge(s("he_re"), 2)
            link(v.scalar_tensor_tensor(he_r[:], he_e[:], 1.0, he_r[:], ALU.min, ALU.add))
            v.tensor_scalar(he_r[:], he_r[:], -1.0, None, ALU.add).then_inc(s("he_made"), 1)
            dve.wait_ge(s("fc_in"), 80)
            v.tensor_copy(av_all[:], av[:].to_broadcast([P, P])).then_inc(s("av_all_made"), 1)
            dve.wait_ge(s("se_made"), 1)
            v.memset(extra[:, 16:17], 1.0)
            v.tensor_copy(extra[:, 0:16], ps[0:E, 7, 0:16]).then_inc(s("extra_out"), 1)
            dve.wait_ge(s("max_one"), 1)
            v.tensor_copy(max_count[:], max_one[0:1, :]).then_inc(s("max_count"), 1)
            v.tensor_scalar(av_all[:], ident[:], -1.0, None, ALU.mult).then_inc(s("neg_ident"), 1)
            se = ps[:, 6, :].rearrange("p (b e) -> p b e", b=B)
            tse = [tmp_a[:, i, 0:BF].rearrange("p (b e) -> p b e", b=B) for i in range(2)]
            for t in range(T):
                link(v.tensor_tensor(tse[t % 2], se, mask_n[:, t, :].unsqueeze(1).to_broadcast([P, B, E]), ALU.add))
                link(v.tensor_reduce(se_max[:, t, :], tse[t % 2], axis=AX.X, op=ALU.max))
            for t in range(T):
                dve.wait_ge(s(f"adj_in{t % 2}"), 16 * (t // 2 + 1))
                v.tensor_scalar(adj_mask[:, t, :], tmp_d[:, t % 2, :], 0.0, MASKED, ALU.is_equal, ALU.mult).then_inc(s("mask_made"), 1)
            dve.wait_ge(s("deg_made"), 1)
            link(v.tensor_scalar(deg[:], ps[:, 7, 16:16 + T], 1.0, None, ALU.max))
            link(v.reciprocal(deg[:], deg[:]))
            for t in range(T):
                dve.wait_ge(s("ind_made"), t + 1)
                v.tensor_scalar(industry[:, t, :], ps[:, t % 4, :], deg[:, t:t + 1], None, ALU.mult).then_inc(s("ind_out"), 1)

            def slots(tag, start, end):
                dve.sem_inc(s(tag + "extra_read"), 3)
                dve.sem_inc(s(tag + "zw"), 2)
                dve.sem_inc(s(tag + "v"), 2)
                with dve.Fori(start, end) as k:
                    k0 = k - start
                    dve.wait_ge(s(tag + "diff"), k0 * 4 + 1)
                    dve.wait_ge(s(tag + "extra"), k0 + 1)
                    v.tensor_scalar(sel, rank[:], slot_no[0:E, bass.ds(k, 1)], None, ALU.is_equal).then_inc(s(tag + "sel"), 1)
                    ex = ps[:, 4, 0:T * 17].rearrange("p (t c) -> p t c", t=T)
                    hn = proj[:, :, :, 2 * P:2 * P + 2]
                    dve.wait_ge(s(tag + "extra"), k0 + 2)
                    dve.wait_ge(s(tag + "th"), k0 + 1)
                    v.tensor_tensor(bl[:].rearrange("p t (a b) -> p t a b", a=BP), ex[:, :, 0:8].rearrange("p t (a b) -> p t a b", a=BP), hn, ALU.add).then_inc(s(tag + "bl"), 1)
                    dve.wait_ge(s(tag + "coef"), k0 + 1)
                    v.tensor_tensor(sx[:], ex[:, :, 8:16], se_max[:], ALU.subtract).then_inc(s(tag + "extra_read"), 1)
                    v.tensor_scalar(vb[:], ex[:, :, 16:17].rearrange("p t a -> p (t a)"), -MASKED, MASKED, ALU.mult, ALU.add).then_inc(s(tag + "extra_read"), 1)
                    dve.wait_ge(s(tag + "extra_read"), 3 * k0 + 5)
                    v.tensor_tensor(sx[:], sx[:], vb[:].unsqueeze(2).to_broadcast([P, T, B]), ALU.add).then_inc(s(tag + "sx"), 1)
                    dve.wait_ge(s(tag + "th"), k0 + 2)
                    dve.wait_ge(s(tag + "zw"), 4 * k0 + 2)
                    v.tensor_scalar(wgt[:], th[:], -0.5, 0.5, ALU.mult, ALU.add).then_inc(s(tag + "wgt"), 1)
                    v.nop().then_inc(s(tag + "extra_read"), 1)
                    dve.wait_ge(s(tag + "wgt"), k0 + 1)
                    for c in range(4):
                        j = k0 * 4 + c
                        dve.wait_ge(s(tag + "diff"), j + 2)
                        dve.wait_ge(s(tag + "exp"), j + 1)
                        for u in range(2):
                            t = 2 * c + u
                            w3 = wgt[:, t, :].unsqueeze(2).to_broadcast([P, B, F])
                            last = v.tensor_tensor(tmp_a[:, c % 2, u * HALF:u * HALF + HALF].rearrange("p (b f) -> p b f", b=B), ps[:, 2 * (c % 2) + u, :].rearrange("p (b f) -> p b f", b=B), w3, ALU.mult)
                        last.then_inc(s(tag + "zw"), 1)
                        dve.wait_ge(s(tag + "zw"), j + 3)
                        zz = tmp_a[:, c % 2, :].rearrange("p (u a b) -> p u a b", u=2, a=BP)
                        v.tensor_tensor(zz, zz, proj[:, 2 * c:2 * c + 2, :, 0:P], ALU.add).then_inc(s(tag + "z"), 1)
                        dve.wait_ge(s(tag + "exp"), j + 3)
                        dve.wait_ge(s(tag + "g"), j + 1)
                        v.scalar_tensor_tensor(tmp_d[:, c % 2, :], tmp_c[:, c % 2, :], 1.0, tmp_b[:, c % 2, :], ALU.min, ALU.add).then_inc(s(tag + "v"), 1)
            def rest(start, end):
                dve.wait_ge(s("max_count"), 1)
                many = dve.value_load(max_count[0:1, 0:1], min_val=0, max_val=E)
                with dve.If(many > start):
                    dve.wait_ge(s("f_g"), 4 * start + 2)
                    dve.wait_ge(s("f_csum"), start + 1)
                    slots("s_", start, end)
                    dve.wait_ge(s("s_g"), 4 * (end - start) + 2)
                    dve.wait_ge(s("s_csum"), end - start + 1)

            slots("f_", 0, FAST_SLOTS)
            rest(FAST_SLOTS, E)

            dve.wait_ge(s("f_g"), 4 * FAST_SLOTS + 2)
            dve.wait_ge(s("f_csum"), FAST_SLOTS + 1)
            link(v.reciprocal(coef_sum[:], coef_sum[:]))
            g4 = g_sum.rearrange("p t (b f) -> p (t b) f", b=B)
            link(v.tensor_tensor(g4, g4, coef_sum[:].rearrange("p t b -> p (t b)").unsqueeze(2).to_broadcast([P, T * B, F]), ALU.mult))
            v.tensor_scalar(g_sum, g_sum, -1.0, None, ALU.add).then_inc(s("g_final"), 1)
            for q in range(8):
                dve.wait_ge(s("pair_t"), q + 1)
                if q >= 2:
                    dve.wait_ge(s("pair_hid"), 4 * (q - 1))
                v.tensor_copy(tmp_a[:, q % 2, :], ps[:, 2 * (q % 2):2 * (q % 2) + 2, :].rearrange("p a b -> p (a b)")).then_inc(s("pair_t_out"), 1)
            dve.wait_ge(s("pair_score"), 32)
            link(v.tensor_copy(sc[:].rearrange("p s t b -> p (s t b)"), ps[:, 6, 0:2 * T * B]))
            v.tensor_tensor(bl[:], sc[:, 1, :, :], sc[:, 0, :, :], ALU.subtract).then_inc(s("pair_diff"), 1)
            i4 = industry.rearrange("p t (b f) -> p (t b) f", b=B)
            dve.wait_ge(s("g_final"), 1)
            link(v.tensor_tensor(g4, g4, i4, ALU.subtract))
            dve.wait_ge(s("pair_th"), 1)
            link(v.tensor_scalar(wgt[:], th[:], 0.5, 0.5, ALU.mult, ALU.add))
            link(v.tensor_tensor(g4, g4, wgt[:].rearrange("p t b -> p (t b)").unsqueeze(2).to_broadcast([P, T * B, F]), ALU.mult))
            x4 = x_nat[:].rearrange("p t b f -> p (t b) f")
            link(v.tensor_tensor(i4, i4, x4, ALU.add))
            link(v.tensor_tensor(i4, i4, g4, ALU.add))
            layer_norm_dve(dve, "ln0_", i4, g4)
            for b2 in range(2):
                v.tensor_tensor(x1[:, 4 * b2:4 * b2 + 4, :, :].rearrange("p b t f -> p t b f") if False else x1[:, 4 * b2:4 * b2 + 4, :, :].transpose([0, 2, 1, 3]),
                                industry.rearrange("p t (b f) -> p t b f", b=B)[:, :, 4 * b2:4 * b2 + 4, :],
                                ln_var[:].rearrange("p (t b) -> p t b", b=B)[:, :, 4 * b2:4 * b2 + 4].unsqueeze(3).to_broadcast([P, T, 4, F]), ALU.mult).then_inc(s("x1_ready"), 1)

            if stop == "x1":
                return

            def mask(g, t, scale):
                dve.wait_ge(s("scores"), g + 2)
                dve.wait_ge(s("probs"), g + 1)
                v_.nop(nofuse=True)
                v_.tensor_tensor_reduce(out=masked[:, t % 2, :], in0=ps[:, 0:2, :].rearrange("p a b -> p (a b)"), in1=adj_mask[:, t, :], scale=scale,
                                       scalar=3e38, op0=ALU.add, op1=ALU.min, accum_out=neg_max[:, t % 2:t % 2 + 1]).then_inc(s("masked"), 1)

            def lo(g, t):
                dve.wait_ge(s("hi"), g + 1)
                where = (slice(None), t // 4, slice(None), slice(t % 4 * P, t % 4 * P + P))
                v_.scalar_tensor_tensor(pt_lo[where], ps[:, 2 + 2 * (t % 2):4 + 2 * (t % 2), :].rearrange("p a (m n) -> p (a m) n", n=P), PSC,
                                       pt_hi[where], ALU.mult, ALU.subtract).then_inc(s("lo"), 1)

            def invert(u, cp, cc):
                dve.wait_ge(s("probs"), 8 * u + 4 * cc + 6)
                dve.wait_ge(s("rinv_rows"), cp + 1)
                v_.reciprocal(rinv[:, 4 * cc:4 * cc + 4], sums[:, 4 * cc:4 * cc + 4]).then_inc(s("rinv"), 1)

            def normalise(c, cp, cc):
                dve.wait_ge(s("rinv_rows"), cp + 3)
                dve.wait_ge(s("osum"), c + 2)
                dve.wait_ge(s("projected"), cp + 1)
                v_.tensor_tensor(onorm[:], osum[:, cc, :], ps[:, 7, :], ALU.mult).then_inc(s("normed"), 1)

            def take_y(v, cc):
                where = (slice(None), bass.ds(v % 2, 1), slice(cc * HALF, cc * HALF + HALF))
                dve.wait_ge(s("y_hi"), 2 * v + cc + 1)
                v_.tensor_tensor(y_lo[where].rearrange("p a n -> p (a n)"), ps[:, 7, :], y_hi[where].rearrange("p a n -> p (a n)"), ALU.subtract).then_inc(s("y_out"), 1)

            def head(b, h, first, last):
                v, u = b * HEADS + h, b * (HEADS + 1) + h
                for t in range(T):
                    g = u * T + t
                    if t < 7:
                        mask(g + 1, t + 1, cur_scale[:])
                    elif not last:
                        dve.wait_ge(s("masked"), g + 2)
                        v_.tensor_copy(cur_scale[:], g_scale[:, bass.ds(h + 1, 1)]).then_inc(s("cur_scale"), 1)
                        dve.wait_ge(s("cur_scale"), v + 2)
                        mask(g + 1, 0, cur_scale[:])
                    lo(g, t)
                    if t == 0 and not first:
                        normalise(2 * u - 2, 2 * v - 2, 0)
                    if t == 1 and not first:
                        invert(u - 1, 2 * v - 1, 1)
                    if t == 3 and not last:
                        take_y(v + 1, 0)
                    if t == 4 and not first:
                        normalise(2 * u - 1, 2 * v - 1, 1)
                    if t == 5:
                        invert(u, 2 * v, 0)
                    if t == 7 and not last:
                        take_y(v + 1, 1)

            v_ = nc.vector
            dve.wait_ge(s("x1_ready"), 2)
            dve.sem_inc(s("lo"), 2)
            dve.sem_inc(s("masked"), 1)
            dve.sem_inc(s("sums_o_read"), 1)
            dve.sem_inc(s("z_out"), 1)
            dve.sem_inc(s("x1_done"), 1)
            dve.sem_inc(s("rinv"), 2)
            dve.sem_inc(s("normed"), 2)
            with dve.Fori(0, B) as b:
                xb = x1[:, bass.ds(b, 1), :, :].rearrange("p a t f -> p (a t) f")
                dve.wait_ge(s("pv"), 8 + 8 * (HEADS + 1) * b)
                dve.wait_ge(s("x1_done"), b + 1)
                v_.tensor_scalar(x2[:, :, 0:F], xb, XS, None, ALU.mult).then_inc(s("x2"), 1)
                dve.wait_ge(s("x2"), 2 * b + 1)
                v_.scalar_tensor_tensor(x2[:, :, F:P], xb, XS, x2[:, :, 0:F], ALU.mult, ALU.subtract).then_inc(s("x2"), 1)
                v_.tensor_copy(cur_scale[:], g_scale[:, 0:1]).then_inc(s("cur_scale"), 1)
                for cc in range(2):
                    take_y(b * HEADS, cc)
                dve.wait_ge(s("cur_scale"), b * HEADS + 1)
                mask(b * (HEADS + 1) * T, 0, cur_scale[:])
                head(b, 0, True, False)
                with dve.Fori(1, HEADS - 1) as h:
                    head(b, h, False, False)
                head(b, HEADS - 1, False, True)
                v, u = b * HEADS + HEADS, b * (HEADS + 1) + HEADS
                normalise(2 * u - 2, 2 * v - 2, 0)
                invert(u - 1, 2 * v - 1, 1)
                normalise(2 * u - 1, 2 * v - 1, 1)
                ph = ps[:, 0:2, :].rearrange("p a b -> p (a b)")
                dve.wait_ge(s("h_made"), b + 2)
                v_.tensor_reduce(h_abs[:], ph, axis=AX.X, op=ALU.max, apply_absolute_value=True).then_inc(s("h_abs"), 1)
                dve.wait_ge(s("h_max"), b + 1)
                v_.tensor_scalar(h_unit[:], h_max[:], 1.0 / HTOP, 1e-15, ALU.mult, ALU.max).then_inc(s("h_unit"), 1)
                dve.wait_ge(s("h_unit"), b + 1)
                v_.reciprocal(h_inv[:], h_unit[:]).then_inc(s("h_inv"), 1)
                v_.tensor_scalar(h_scale[:], h_unit[:], h_unit[:], -1.0, ALU.mult, ALU.mult).then_inc(s("h_scale"), 1)
                dve.wait_ge(s("h_inv"), b + 1)
                v_.tensor_scalar(y_hi[:, 0, :], ph, h_inv[:], None, ALU.mult).then_inc(s("h_parts"), 1)
                dve.wait_ge(s("h_parts"), 2 * b + 1)
                v_.scalar_tensor_tensor(y_lo[:, 0, :], ph, h_inv[:], y_hi[:, 0, :], ALU.mult, ALU.subtract).then_inc(s("h_parts"), 1)
                dve.wait_ge(s("h_scale"), b + 1)
                mask(u * T, 0, h_scale[:])
                for t in range(T):
                    if t < 7:
                        mask(u * T + t + 1, t + 1, h_scale[:])
                    lo(u * T + t, t)
                dve.wait_ge(s("probs"), 8 * u + 10)
                v_.reciprocal(rinv_o[:], sums_o[:]).then_inc(s("sums_o_read"), 1)
                dve.wait_ge(s("sums_o_read"), b + 2)
                v_.tensor_scalar(rinv_o[:], rinv_o[:], h_unit[:], 1.0 / PSC, ALU.mult, ALU.mult).then_inc(s("rinv_o"), 1)
                dve.wait_ge(s("rinv_o"), b + 1)
                dve.wait_ge(s("zo"), b + 1)
                v_.tensor_tensor(zo[:], ps[:, 7, :].rearrange("p (t f) -> p t f", f=F), rinv_o[:].unsqueeze(2).to_broadcast([P, T, F]), ALU.mult).then_inc(s("z_out"), 1)
                dve.wait_ge(s("z_out"), b + 2)
                v_.tensor_tensor(zo[:], zo[:], b_out[:].unsqueeze(1).to_broadcast([P, T, F]), ALU.add).then_inc(s("z_bias"), 1)
                dve.wait_ge(s("z_bias"), b + 1)
                v_.scalar_tensor_tensor(zo[:], zo[:], 0.01, zo[:], ALU.mult, ALU.max).then_inc(s("z_leaky"), 1)
                dve.wait_ge(s("z_leaky"), b + 1)
                v_.tensor_tensor(xb, xb, zo[:], ALU.add).then_inc(s("x1_done"), 1)
            dve.wait_ge(s("x1_done"), B + 1)
            xf = x1[:].rearrange("p b t f -> p (b t) f")
            layer_norm_dve(dve, "ln1_", xf, cat[:, 0:4, :].rearrange("p a (c f) -> p (a c) f", f=F))
            for q in range(4):
                v_.tensor_tensor(xf[:, 16 * q:16 * q + 16, :], xf[:, 16 * q:16 * q + 16, :], ln_var[:, 16 * q:16 * q + 16].unsqueeze(2).to_broadcast([P, 16, F]), ALU.mult).then_inc(s("ln1_out"), 1)

        @block.gpsimd
        def _(pool):
            g = nc.gpsimd
            pool.wait_ge(s("g_abs"), 1)
            g.partition_all_reduce(g_max[:], g_abs[:], P, RMAX).then_inc(s("g_max"), 1)
            pool.wait_ge(s("max_all"), 1)
            g.partition_all_reduce(max_one[:], max_all[:], P, RMAX).then_inc(s("max_one"), 1)
            pool.wait_ge(s("ind_made"), T)
            g.memset(g_sum, 0.0).then_inc(s("f_g"), 2)
            g.memset(coef_sum[:], 0.0).then_inc(s("f_csum"), 1)

            def slots(tag, start, end):
                pool.sem_inc(s(tag + "vc"), 1)
                if tag == "s_":
                    pool.sem_inc(s(tag + "g"), 2)
                    pool.sem_inc(s(tag + "csum"), 1)
                with pool.Fori(start, end) as k:
                    k0 = k - start
                    pool.wait_ge(s(tag + "coef"), k0 + 2)
                    pool.wait_ge(s(tag + "csum"), k0 + 1)
                    g.tensor_tensor(coef_sum[:], coef_sum[:], coef[:], ALU.add).then_inc(s(tag + "csum"), 1)
                    for c in range(4):
                        j = k0 * 4 + c
                        vv = tmp_d[:, c % 2, :].rearrange("p (t f) -> p t f", f=F)
                        pool.wait_ge(s(tag + "v"), j + 3)
                        g.tensor_tensor(vv, vv, coef[:, 2 * c:2 * c + 2, :].rearrange("p t b -> p (t b)").unsqueeze(2).to_broadcast([P, 2 * B, F]), ALU.mult).then_inc(s(tag + "vc"), 1)
                        pool.wait_ge(s(tag + "vc"), j + 2)
                        pool.wait_ge(s(tag + "g"), j + 2)
                        gg = g_sum[:, 2 * c:2 * c + 2, :].rearrange("p t q -> p (t q)")
                        g.tensor_tensor(gg, gg, tmp_d[:, c % 2, :], ALU.add).then_inc(s(tag + "g"), 1)
            def rest(start, end):
                pool.wait_ge(s("max_count"), 1)
                many = pool.value_load(max_count[0:1, 0:1], min_val=0, max_val=E)
                with pool.If(many > start):
                    pool.wait_ge(s("f_g"), 4 * start + 2)
                    pool.wait_ge(s("f_csum"), start + 1)
                    slots("s_", start, end)
                    pool.wait_ge(s("s_g"), 4 * (end - start) + 2)
                    pool.wait_ge(s("s_csum"), end - start + 1)

            slots("f_", 0, FAST_SLOTS)
            rest(FAST_SLOTS, E)


            if stop == "x1":
                return

            def leaky(cp, cc, h):
                pool.wait_ge(s("z"), cp + 1)
                pool.nop(nofuse=True)
                g.tensor_scalar(zm[:, cc, :], zc[:, cc, :], 0.0, -0.99, ALU.min, ALU.mult).then_inc(s("zm"), 1)
                pool.wait_ge(s("zm"), cp + 1)
                where = cat[:, bass.ds(h, 1), cc * HALF:cc * HALF + HALF].rearrange("p a n -> p (a n)")
                g.tensor_tensor(where, zc[:, cc, :], zm[:, cc, :], ALU.add).then_inc(s("cat"), 1)

            pool.wait_ge(s("x1_ready"), 2)
            pool.sem_inc(s("cat"), 2)
            with pool.Fori(0, B) as b:
                pool.wait_ge(s("h_made"), b + 1)
                pool.nop(nofuse=True)
                with pool.Fori(0, HEADS) as h:
                    for cc in range(2):
                        pool.wait_ge(s("cat"), 2 * (b * HEADS + h) + cc + 1)
                        leaky(2 * (b * HEADS + h) + cc, cc, h)
                pool.wait_ge(s("h_abs"), b + 1)
                pool.nop(nofuse=True)
                g.partition_all_reduce(h_max[:], h_abs[:], P, RMAX).then_inc(s("h_max"), 1)




def _layout(i):
    import numpy as np
    c = np.ascontiguousarray
    n = {k: np.asarray(v) for k, v in i.items()}
    consts = np.zeros((P, 2 * P), np.float32)
    consts[:, 0:P] = np.eye(P)
    consts[0:E, P:P + E] = np.triu(np.ones((E, E)))
    consts[:, P + E:P + 2 * E] = np.arange(1, E + 1)
    return {
        "consts": consts, "x": c(n["x"]), "adj": c(n["adj"]), "adjT": c(n["adj"].T),
        "H": c(n["L0_gnn_H"]), "HT": c(n["L0_gnn_H"].T), "W": c(n["L0_gnn_W"]), "WT": c(n["L0_gnn_W"].T),
        "W_ind": c(n["L0_gnn_W_ind"]), "a_node": c(n["L0_gnn_a_node"].reshape(F, 1)), "a_gn": c(n["L0_gnn_a_gn"].reshape(F, 1)),
        "a_ge": c(n["L0_gnn_a_ge"].reshape(F, 1)), "fcW": c(n["L0_gnn_fcW"]), "fcb": c(n["L0_gnn_fcb"].reshape(P, 1)),
        "av": c(n["L0_gnn_av"].reshape(P, 1)), "Wh": c(n["L1_gnn_Wh"]), "WhT": c(n["L1_gnn_Wh"].transpose(0, 2, 1)),
        "bhT": c(n["L1_gnn_bh"].T), "W_out": c(n["L1_gnn_W_out"]), "b_out": c(n["L1_gnn_b_out"]),
    }


def kernel(**inputs):
    import concourse.bacc as _bacc
    from concourse.bass_utils import run_bass_kernel_spmd as _run

    nc = _bacc.Bacc("TRN2", target_bir_lowering=False, num_devices=1)
    arrays = _layout(inputs)
    args = {k: nc.dram_tensor(f"in_{k}", v.shape, mybir.dt.from_np(v.dtype), kind="ExternalInput").ap() for k, v in arrays.items()}
    out = nc.dram_tensor("out", (B, N, F), FP32, kind="ExternalOutput").ap()
    residual_graph_layers(nc, args, out)
    r = _run(nc, [{f"in_{k}": v for k, v in arrays.items()}], core_ids=[0])
    return r.results[0]["out"]
```

```python
from contextlib import ExitStack

import concourse.bass as bass
from concourse import mybir

FP32, FP16, BF16, I32 = mybir.dt.float32, mybir.dt.float16, mybir.dt.bfloat16, mybir.dt.int32
ALU, ACT, AX = mybir.AluOpType, mybir.ActivationFunctionType, mybir.AxisListType
RMAX = bass.bass_isa.ReduceOp.max

P = 128
B = 8
N = 1024
F = 64
T = N // P
BP = B // 2
BF = B * F
E = 64
HEADS = 8
HID = 128
HALF = 512
WCOL = 2 * P + 2
MASKED = -1e30
XS = 64.0
PSC = 16384.0
GTOP = 4.0
HTOP = 30000.0
EPS = 1e-5
FAST_SLOTS = 10


def residual_graph_layers(nc, a, out, stop=None):
    ctx = ExitStack()
    with ctx:
        sems = {}

        def s(name):
            if name not in sems:
                sems[name] = ctx.enter_context(nc.semaphore(name))
            return sems[name]

        def sb(name, shape, dt=FP32, c=ctx):
            return c.enter_context(nc.sbuf_tensor(name, shape, dt))

        ident = sb("ident", [P, P])
        ident16 = sb("ident16", [P, P], FP16)
        x1 = sb("x1", [P, B, T, F])
        adj_mask = sb("adj_mask", [P, T, N], BF16)
        g_hi = sb("g_hi", [P, HEADS, P], FP16)
        g_lo = sb("g_lo", [P, HEADS, P], FP16)
        fold16 = sb("fold16", [P, P], FP16)
        fold = sb("fold", [P, P])
        h_unit = sb("h_unit", [P, 1])
        h_inv = sb("h_inv", [P, 1])
        h_scale = sb("h_scale", [P, 1])
        z_scale = sb("z_scale", [P, 1])
        g_scale = sb("g_scale", [P, HEADS])
        w_out = sb("w_out", [P, HEADS, P])
        bh = sb("bh", [P, HEADS])
        b_out = sb("b_out", [P, 1])
        ln_mean = sb("ln_mean", [P, T * B])
        ln_var = sb("ln_var", [P, T * B])

        L0 = ExitStack()
        x_nat = sb("x_nat", [P, T, B, F], c=L0)
        proj = sb("proj", [P, T, BP, WCOL], c=L0)
        adjT = sb("adjT", [P, T, N], c=L0)
        x_t = sb("x_t", [P, BP, N], c=L0)
        industry = x_t[:].rearrange("p a (t q) -> p (a t) q", t=2)
        g_sum = adjT[:, 0:T // 2, :].rearrange("p a (t q) -> p (a t) q", t=2)
        tmp_a = sb("tmp_a", [P, 2, N], c=L0)
        tmp_b = sb("tmp_b", [P, 2, N], c=L0)
        tmp_c = sb("tmp_c", [P, 2, N], c=L0)
        tmp_d = sb("tmp_d", [P, 2, N], c=L0)
        tri = sb("tri", [P, E], c=L0)
        slot_no = sb("slot_no", [P, E], c=L0)
        w_t = sb("w_t", [F, F], c=L0)
        w_cols = sb("w_cols", [F, 2], c=L0)
        w_block = sb("w_block", [P, WCOL], c=L0)
        node_block = sb("node_block", [P, P], c=L0)
        w_all = sb("w_all", [P, HEADS, P], c=L0)
        a_ge = sb("a_ge", [F, 1], c=L0)
        fc_w = sb("fc_w", [P, P], c=L0)
        fc_b = sb("fc_b", [P, 1], c=L0)
        av = sb("av", [P, 1], c=L0)
        av_all = sb("av_all", [P, P], c=L0)
        ones = sb("ones", [P, P], c=L0)
        g_abs = sb("g_abs", [P, HEADS], c=L0)
        w_norm = sb("w_norm", [P, HEADS], c=L0)
        b_abs = sb("b_abs", [P, HEADS], c=L0)
        h_top = sb("h_top", [P, F], c=L0)
        g_max = sb("g_max", [P, HEADS], c=L0)
        g_inv = sb("g_inv", [P, HEADS], c=L0)
        mask_t = sb("mask_t", [P, N], c=L0)
        edge_bias = sb("edge_bias", [P, N], BF16, c=L0)
        rank = sb("rank", [E, N], c=L0)
        mask_n = sb("mask_n", [P, T, E], c=L0)
        node_cnt = sb("node_cnt", [P, T], c=L0)
        node_empty = sb("node_empty", [P, T], c=L0)
        edge_max = sb("edge_max", [P, BP], c=L0)
        edge_sum = sb("edge_sum", [P, BP], c=L0)
        edge_inv = sb("edge_inv", [P, BP], c=L0)
        agg = sb("agg", [E, B, F], c=L0)
        agg_t = sb("agg_t", [F, BF], c=L0)
        he_r = sb("he_r", [F, BF], c=L0)
        he_e = sb("he_e", [F, BF], c=L0)
        extra = sb("extra", [E, 17], c=L0)
        se_max = sb("se_max", [P, T, B], c=L0)
        bl = sb("bl", [P, T, B], c=L0)
        th = sb("th", [P, T, B], c=L0)
        wgt = sb("wgt", [P, T, B], c=L0)
        sx = sb("sx", [P, T, B], c=L0)
        vb = sb("vb", [P, T], c=L0)
        coef = sb("coef", [P, T, B], c=L0)
        coef_sum = sb("coef_sum", [P, T, B], c=L0)
        sel = mask_t[0:E, :]
        max_all = sb("max_all", [P, 1], c=L0)
        max_one = sb("max_one", [P, 1], c=L0)
        max_count = sb("max_count", [1, 1], I32, c=L0)
        deg = sb("deg", [P, T], c=L0)
        sc = sb("sc", [P, 2, T, B], c=L0)
        L0.close()

        ax = sb("ax", [P, B, N], FP16)
        x2 = sb("x2", [P, B, T, P], FP16)
        y_hi = sb("y_hi", [P, 2, N], FP16)
        y_lo = sb("y_lo", [P, 2, N], FP16)
        masked = sb("masked", [P, 2, N])
        probs = sb("probs", [P, 2, N])
        pt_hi = sb("pt_hi", [P, 2, T, HALF], FP16)
        pt_lo = sb("pt_lo", [P, 2, T, HALF], FP16)
        neg_max = sb("neg_max", [P, 2])
        sums = sb("sums", [P, T])
        rinv = sb("rinv", [P, T])
        cur_scale = sb("cur_scale", [P, 1])
        osum = sb("osum", [P, 2, HALF])
        onorm = sb("onorm", [P, HALF])
        w2 = sb("w2", [P, P])
        zc = sb("zc", [P, 2, HALF])
        zm = sb("zm", [P, 2, HALF])
        cat = sb("cat", [P, HEADS, N])

        pt_sq = pt_hi[:].rearrange("p a m n -> p (a m n)").bitcast(FP32).rearrange("p (c f) -> p c f", f=F)
        ps = ctx.enter_context(nc.psum_tensor("ps", [P, 8, HALF], FP32))

        def h_of(t, lo=0, hi=BP):
            return proj[:, t, lo:hi, 0:P]

        def layer_norm_act(act, tag, sq_out, centred):
            act.wait_ge(s(tag + "centred"), 1)
            act.activation(sq_out, centred, ACT.Square).then_inc(s(tag + "square"), 1)
            act.wait_ge(s(tag + "var"), 1)
            act.activation(ln_var[:], ln_var[:], ACT.Sqrt).then_inc(s(tag + "sqrt"), 1)

        def pair_scores(pe, j):
            src, b, c = j // 16, j // 2 % 8, j % 2
            pe.wait_ge(s("pair_tanh"), j + 1)
            for i in range(4):
                col = (src * T + c * 4 + i) * B + b
                last = nc.tensor.matmul(ps[:, 6, col:col + 1], tmp_c[:, j % 2, i * P:i * P + P], av[:], start=True, stop=True)
            last.then_inc(s("pair_score"), 1)

        chained = [0]

        def link(ins):
            chained[0] += 1
            ins.then_inc(s("dve_chain"), 1)
            nc.vector.wait_ge(s("dve_chain"), chained[0])

        def layer_norm_dve(dve, tag, xs, sq):
            v = nc.vector
            link(v.tensor_reduce(ln_mean[:], xs, axis=AX.X, op=ALU.add))
            link(v.tensor_scalar(ln_mean[:], ln_mean[:], 1.0 / F, None, ALU.mult))
            v.tensor_tensor(xs, xs, ln_mean[:].unsqueeze(2).to_broadcast([P, T * B, F]), ALU.subtract).then_inc(s(tag + "centred"), 1)
            dve.wait_ge(s(tag + "square"), 1)
            link(v.tensor_reduce(ln_var[:], sq, axis=AX.X, op=ALU.add))
            v.tensor_scalar(ln_var[:], ln_var[:], 1.0 / F, EPS, ALU.mult, ALU.add).then_inc(s(tag + "var"), 1)
            dve.wait_ge(s(tag + "sqrt"), 1)
            link(v.reciprocal(ln_var[:], ln_var[:]))

        block = ctx.enter_context(nc.Block())

        @block.sync
        def _(sp):
            sp.dma_start(ident[:], a["consts"][:, 0:P]).then_inc(s("consts_in"), 16)
            sp.dma_start(tri[:], a["consts"][:, P:P + E]).then_inc(s("consts_in"), 16)
            sp.dma_start(slot_no[:], a["consts"][:, P + E:P + 2 * E]).then_inc(s("consts_in"), 16)
            for b in range(B):
                sp.dma_start(x_nat[:, :, b, :], a["x"][b].rearrange("(t p) f -> p t f", p=P)).then_inc(s("x_in"), 16)
            for half in range(2):
                sp.dma_start(mask_t[half * E:half * E + E, :], a["HT"]).then_inc(s("ht_in"), 16)
            sp.dma_start(mask_n[:], a["H"].rearrange("(t p) e -> p t e", p=P)).then_inc(s("hn_in"), 16)
            for t in range(T):
                sp.dma_start(adjT[:, t, :], a["adjT"][t * P:t * P + P, :]).then_inc(s("adjT_in"), 16)
            for t in range(T):
                if t >= 2:
                    sp.wait_ge(s("mask_made"), t - 1)
                sp.dma_start(tmp_d[:, t % 2, :], a["adj"][t * P:t * P + P, :]).then_inc(s(f"adj_in{t % 2}"), 16)
            if stop != "x1":
                sp.wait_ge(s("x1_ready"), 2)
                for half in range(2):
                    sp.dma_start(w2[half * F:half * F + F, :], a["Wh"][0]).then_inc(s("w2_in"), 16)
                with sp.Fori(1, B * HEADS) as head:
                    sp.wait_ge(s("projected"), 2 * head + 1)
                    for half in range(2):
                        sp.dma_start(w2[half * F:half * F + F, :], a["Wh"][bass.ds(head % HEADS, 1)].rearrange("a f d -> (a f) d")).then_inc(s("w2_in"), 16)
                for q in range(4):
                    sp.wait_ge(s("ln1_out"), q + 1)
                    sp.dma_start(out[2 * q:2 * q + 2].rearrange("b (t p) f -> p b t f", p=P), x1[:, 2 * q:2 * q + 2]).then_inc(s("out_stored"), 16)
                sp.wait_ge(s("out_stored"), 64)
            if stop == "x1":
                sp.wait_ge(s("x1_ready"), 2)
                sp.wait_ge(s("wo_in"), 80)
                sp.dma_start(out.rearrange("b (t p) f -> p b t f", p=P), x1[:]).then_inc(s("out_stored"), 16)
                sp.wait_ge(s("out_stored"), 16)

        @block.scalar
        def _(act):
            act.dma_start(w_t[:], a["WT"]).then_inc(s("w_in"), 16)
            act.dma_start(w_cols[:, 0:1], a["a_node"]).then_inc(s("w_in"), 16)
            act.dma_start(w_cols[:, 1:2], a["a_gn"]).then_inc(s("w_in"), 16)
            act.wait_ge(s("w_block_zero"), 1)
            for half in range(2):
                r = slice(half * F, half * F + F)
                act.dma_start(w_block[r, half * F:half * F + F], a["W"]).then_inc(s("wb_in"), 16)
                act.dma_start(w_block[r, P + half * F:P + half * F + F], a["W_ind"]).then_inc(s("wb_in"), 16)
                act.dma_start(fc_w[r, :], a["fcW"]).then_inc(s("fc_in"), 16)
                act.dma_start(w_all[:, :, r], a["WhT"].rearrange("h d f -> d h f")).then_inc(s("wh_in"), 16)
                act.dma_start(w_out[:, :, r], a["W_out"].rearrange("(h d) f -> d h f", d=HID)).then_inc(s("wo_in"), 16)
            act.dma_start(fc_b[:], a["fcb"]).then_inc(s("fc_in"), 16)
            act.dma_start(av[:], a["av"]).then_inc(s("fc_in"), 16)
            act.dma_start(a_ge[:], a["a_ge"]).then_inc(s("fc_in"), 16)
            act.dma_start(bh[:], a["bhT"]).then_inc(s("wo_in"), 16)
            for half in range(2):
                act.dma_start(b_out[half * F:half * F + F, :], a["b_out"]).then_inc(s("wo_in"), 16)
            act.wait_ge(s("wh_in"), 32)
            for h in range(HEADS):
                if h:
                    act.wait_ge(s("w_square"), h)
                act.activation(tmp_b[:, 0, 0:F], w_all[:, h, 0:F], ACT.Square, accum_out=w_norm[:, h:h + 1]).then_inc(s("w_square"), 1)
            act.wait_ge(s("w_square"), HEADS)
            act.activation(w_norm[:], w_norm[:], ACT.Sqrt).then_inc(s("w_norm"), 1)
            for q in range(1, 2 * BP, 2):
                act.wait_ge(s("xt_made"), q + 1)
                act.activation(x_t[:, q // 2, HALF:N], ps[:, q % 4, :], ACT.Copy).then_inc(s("xt_out1"), 1)
            for i in range(1, T * BP, 2):
                act.wait_ge(s("proj_made"), i + 1)
                act.activation(proj[:, i // BP, i % BP, :], ps[:, i % 4, 0:WCOL], ACT.Copy).then_inc(s("proj_out1"), 1)
            for bp in range(BP):
                act.wait_ge(s("edge_masked"), bp + 1)
                if bp:
                    act.wait_ge(s("edge_tr"), bp)
                act.activation(tmp_b[:, 0, :], tmp_a[:, 0, :], ACT.Exp, scale=-1.0, bias=edge_max[:, bp:bp + 1],
                               accum_out=edge_sum[:, bp:bp + 1]).then_inc(s("edge_exp"), 1)
                act.wait_ge(s("edge_tr"), bp + 1)
                if bp:
                    act.wait_ge(s("agg_made"), bp)
                act.activation(tmp_c[:, 0, :], ps[:, 6:8, :], ACT.Copy).then_inc(s("edge_tr_out"), 1)
            act.wait_ge(s("aggt_out"), 1)
            act.activation(he_r[:], agg_t[:], ACT.Relu).then_inc(s("he_re"), 1)
            act.activation(he_e[:], agg_t[:], ACT.Exp).then_inc(s("he_re"), 1)
            act.wait_ge(s("he_hid"), 1)
            act.wait_ge(s("fc_in"), 80)
            act.activation(tmp_b[:, 1, 0:BF], ps[:, 5, :], ACT.Tanh, bias=fc_b[:]).then_inc(s("he_tanh"), 1)

            def slots(tag, start, end):
                act.sem_inc(s(tag + "exp"), 2)
                act.sem_inc(s(tag + "th"), 1)
                act.sem_inc(s(tag + "coef"), 1)
                with act.Fori(start, end) as k:
                    k0 = k - start
                    act.wait_ge(s(tag + "bl"), k0 + 1)
                    act.activation(th[:], bl[:], ACT.Tanh, scale=0.5).then_inc(s(tag + "th"), 1)
                    act.wait_ge(s(tag + "sx"), k0 + 1)
                    act.wait_ge(s(tag + "vc"), 4 * k0 + 1)
                    act.activation(coef[:], sx[:], ACT.Exp).then_inc(s(tag + "coef"), 1)
                    for c in range(4):
                        j = k0 * 4 + c
                        act.wait_ge(s(tag + "z"), j + 1)
                        act.wait_ge(s(tag + "v"), j + 1)
                        act.activation(tmp_b[:, c % 2, :], tmp_a[:, c % 2, :], ACT.Relu).then_inc(s(tag + "relu"), 1)
                        act.activation(tmp_c[:, c % 2, :], tmp_a[:, c % 2, :], ACT.Exp).then_inc(s(tag + "exp"), 1)
            def rest(start, end):
                act.wait_ge(s("max_count"), 1)
                many = act.value_load(max_count[0:1, 0:1], min_val=0, max_val=E)
                with act.If(many > start):
                    act.wait_ge(s("f_g"), 4 * start + 2)
                    act.wait_ge(s("f_csum"), start + 1)
                    slots("s_", start, end)
                    act.wait_ge(s("s_g"), 4 * (end - start) + 2)
                    act.wait_ge(s("s_csum"), end - start + 1)

            slots("f_", 0, FAST_SLOTS)
            rest(FAST_SLOTS, E)

            for j in range(32):
                act.wait_ge(s("pair_hid"), j + 1)
                if j >= 2:
                    act.wait_ge(s("pair_score"), j - 1)
                act.activation(tmp_c[:, j % 2, 0:HALF], ps[:, 4 + j % 2, :], ACT.Tanh, bias=fc_b[:]).then_inc(s("pair_tanh"), 1)
            act.wait_ge(s("pair_diff"), 1)
            act.activation(th[:], bl[:], ACT.Tanh, scale=0.5).then_inc(s("pair_th"), 1)
            layer_norm_act(act, "ln0_", g_sum.rearrange("p t (b f) -> p (t b) f", b=B),
                           industry.rearrange("p t (b f) -> p (t b) f", b=B))

            if stop == "x1":
                return

            def at(w, i, *rest):
                return w[(slice(None), i) + rest] if isinstance(i, int) else w[(slice(None), bass.ds(i, 1)) + rest].squeeze(1)

            def exp(v, t):
                act.wait_ge(s("masked"), 8 * v + t + 2)
                if t % 4 == 0:
                    act.wait_ge(s("rinv"), 2 * v + t // 4 + 1)
                act.wait_ge(s("pT"), 8 * v + t + 1)
                act.activation(probs[:, t % 2, :], masked[:, t % 2, :], ACT.Exp, scale=-1.0, bias=neg_max[:, t % 2:t % 2 + 1],
                               accum_out=sums[:, t:t + 1]).then_inc(s("probs"), 1)

            def hi(v, t):
                if t % 4 == 0:
                    act.wait_ge(s("pv"), 4 * (2 * v + t // 4) + 4)
                act.wait_ge(s("pT"), 8 * v + t + 3)
                act.activation(pt_hi[:, t // 4, :, t % 4 * P:t % 4 * P + P],
                               ps[:, 2 + 2 * (t % 2):4 + 2 * (t % 2), :].rearrange("p a (m n) -> p (a m) n", n=P), ACT.Copy, scale=PSC).then_inc(s("hi"), 1)

            def take_sum(v, cc):
                act.wait_ge(s("pv"), 4 * (2 * v + cc) + 12)
                act.wait_ge(s("normed"), 2 * v + cc + 1)
                act.activation(osum[:, cc, :], ps[:, 6, :], ACT.Copy).then_inc(s("osum"), 1)

            def take_proj(v, cc, out_unit):
                act.wait_ge(s("projected"), 2 * v + cc + 2)
                act.wait_ge(s("cat"), 2 * v + cc + 1)
                act.nop(nofuse=True)
                if out_unit:
                    act.activation(zc[:, cc, :], ps[:, 7, :], ACT.Identity, scale=z_scale[:], bias=b_out[:]).then_inc(s("z"), 1)
                else:
                    act.activation(zc[:, cc, :], ps[:, 7, :], ACT.Identity, scale=1.0 / (XS * PSC), bias=bh[:, bass.ds(v % HEADS, 1)]).then_inc(s("z"), 1)

            def take_y(v, cc):
                act.wait_ge(s("y"), 2 * v + cc + 1)
                if not isinstance(v, int) or v >= 2:
                    act.wait_ge(s("scores"), 8 * (v - 1) + 1)
                act.nop(nofuse=True)
                act.activation(at(y_hi, v % 2, slice(cc * HALF, cc * HALF + HALF)), ps[:, 7, :], ACT.Copy).then_inc(s("y_hi"), 1)

            def take_h(q, cc):
                act.wait_ge(s("h_made"), 2 * q + cc + 3)
                act.nop(nofuse=True)
                act.activation(at(ax, q, slice(cc * HALF, cc * HALF + HALF)), ps[:, 7, :], ACT.Copy, scale=h_inv[:]).then_inc(s("h_hi"), 1)

            def unit(v, first=False, last=False, out_unit=False, h_batch=None):
                for t in range(T):
                    if t == 0 and not first:
                        take_y(v, 1)
                        take_sum(v - 1, 0)
                    if t == 3 and not first:
                        take_proj(v - 1, 0, out_unit)
                    if t == 4:
                        if not last:
                            take_y(v + 1, 0)
                        if not first:
                            take_sum(v - 1, 1)
                    if t == 7 and not first:
                        take_proj(v - 1, 1, out_unit)
                    if t < 7:
                        exp(v, t + 1)
                    elif not last:
                        exp(v + 1, 0)
                    if t == 3 and h_batch is not None:
                        for cc in range(2):
                            take_h(h_batch, cc)
                    hi(v, t)

            def drain(v, out_unit):
                take_sum(v, 0)
                take_proj(v, 0, out_unit)
                take_sum(v, 1)
                take_proj(v, 1, out_unit)

            act.wait_ge(s("x1_ready"), 2)
            act.sem_inc(s("probs"), 2)
            act.sem_inc(s("osum"), 1)
            for b in range(B):
                act.wait_ge(s("xt16"), b + 1)
                act.activation(ax[:, b, :], ps[:, b % 2, :].bitcast(FP16), ACT.Copy).then_inc(s("ax"), 1)
            take_y(0, 0)
            take_y(0, 1)
            exp(0, 0)
            unit(0, first=True)
            with act.Fori(1, HEADS + 1) as v:
                unit(v)
            with act.Fori(1, B - 1) as q:
                unit(q * HEADS + 1, h_batch=q - 1)
                with act.Fori(2, HEADS + 1) as j:
                    unit(q * HEADS + j)
            unit((B - 1) * HEADS + 1, h_batch=B - 2)
            with act.Fori((B - 1) * HEADS + 2, B * HEADS - 1) as v:
                unit(v)
            unit(B * HEADS - 1, last=True)
            drain(B * HEADS - 1, False)
            for cc in range(2):
                take_h(B - 1, cc)
            for b in range(B):
                act.wait_ge(s("h_t"), b + 1)
                act.activation(x2[:, b], ps[:, b % 2, :].bitcast(FP16), ACT.Copy).then_inc(s("h_x2"), 1)
            v0 = B * HEADS
            take_y(v0, 0)
            take_y(v0, 1)
            exp(v0, 0)
            unit(v0, first=True, out_unit=True)
            with act.Fori(v0 + 1, v0 + B - 1) as v:
                unit(v, out_unit=True)
            unit(v0 + B - 1, last=True, out_unit=True)
            drain(v0 + B - 1, True)
            layer_norm_act(act, "ln1_", pt_sq, x1[:].rearrange("p b t f -> p (b t) f"))

        @block.tensor
        def _(pe):
            pe.wait_ge(s("w_in"), 48)
            pe.wait_ge(s("consts_in"), 48)
            nc.tensor.matmul(ps[0:F, 4, 0:2], w_t[:], w_cols[:], start=True, stop=True)
            nc.tensor.matmul(ps[F:P, 4, 0:2], w_t[:], w_cols[:], start=True, stop=True).then_inc(s("wa_made"), 1)
            pe.wait_ge(s("wh_in"), 32)
            for h in range(HEADS):
                last = nc.tensor.matmul(ps[:, 5, h * F:h * F + F], w_all[:, h, :], w_all[:, h, 0:F], start=True, stop=True)
            last.then_inc(s("g_made"), 1)
            pe.wait_ge(s("x_in"), 16 * B)
            pe.wait_ge(s("ones_made"), 1)
            for q in range(2 * BP):
                if q >= 4:
                    pe.wait_ge(s(f"xt_out{q % 2}"), (q - 4) // 2 + 1)
                for i in range(4):
                    t = (q % 2) * 4 + i
                    last = nc.tensor.transpose(ps[:, q % 4, i * P:i * P + P],
                                               x_nat[:, t, q // 2 * 2:q // 2 * 2 + 2, :].rearrange("p b f -> p (b f)"), ident[:])
                last.then_inc(s("xt_made"), 1)
            pe.wait_ge(s("xt_out0"), BP)
            pe.wait_ge(s("xt_out1"), BP)
            pe.wait_ge(s("w_ready"), 1)
            for i in range(T * BP):
                if i >= 4:
                    pe.wait_ge(s(f"proj_out{i % 2}"), (i - 4) // 2 + 1)
                nc.tensor.matmul(ps[:, i % 4, 0:WCOL], x_t[:, i % BP, i // BP * P:i // BP * P + P], w_block[:],
                                 start=True, stop=True).then_inc(s("proj_made"), 1)
            pe.wait_ge(s("w_abs"), 1)
            nc.tensor.matmul(ps[:, 6, :], ones[:], tmp_c[:, 0, 0:HALF], start=True, stop=True).then_inc(s("h_bound"), 1)
            pe.wait_ge(s("h_top"), 1)
            pe.wait_ge(s("mask_t_made"), 1)
            pe.wait_ge(s("ones_made"), 1)
            for c in range(2):
                last = nc.tensor.matmul(ps[0:E, 6 + c, :], ones[0:E, 0:E], mask_t[0:E, c * HALF:c * HALF + HALF], start=True, stop=True)
            last.then_inc(s("cnt_made"), 1)
            pe.wait_ge(s("eff_made"), 1)
            for c in range(2):
                last = nc.tensor.matmul(ps[0:E, 6 + c, :], tri[0:E, :], tmp_a[0:E, 1, c * HALF:c * HALF + HALF], start=True, stop=True)
            last.then_inc(s("rank_made"), 1)
            pe.wait_ge(s("g_out"), 1)
            pe.wait_ge(s("rank_out"), 1)
            for bp in range(BP):
                if bp:
                    pe.wait_ge(s("edge_lk"), bp)
                for c in range(2):
                    last = nc.tensor.matmul(ps[:, 4 + c, :], node_block[:], x_t[:, bp, c * HALF:c * HALF + HALF], start=True, stop=True)
                last.then_inc(s("edge_s"), 1)
                pe.wait_ge(s("edge_exp"), bp + 1)
                if bp:
                    pe.wait_ge(s("edge_tr_out"), bp)
                for t in range(T):
                    last = nc.tensor.transpose(ps[:, 6 + t // 4, t % 4 * P:t % 4 * P + P], tmp_b[:, 0, t * P:t * P + P], ident[:])
                last.then_inc(s("edge_tr"), 1)
                pe.wait_ge(s("edge_tr_out"), bp + 1)
                if bp == 0:
                    pe.wait_ge(s("proj_out0"), T * BP // 2)
                    pe.wait_ge(s("proj_out1"), T * BP // 2)
                for t in range(T):
                    last = nc.tensor.matmul(ps[:, bp, 0:P], tmp_c[:, 0, t * P:t * P + P], proj[:, t, bp, 0:P], start=(t == 0), stop=(t == T - 1))
                last.then_inc(s("agg_made"), 1)
            pe.wait_ge(s("agg_out"), 2 * BP)
            for b in range(B):
                last = nc.tensor.transpose(ps[0:F, 4, b * E:b * E + E], agg[:, b, :], ident[0:E, 0:E])
            last.then_inc(s("aggt_made"), 1)
            pe.wait_ge(s("he_made"), 1)
            pe.wait_ge(s("fc_in"), 80)
            nc.tensor.matmul(ps[:, 5, :], fc_w[0:F, :], he_r[:], start=True, stop=True).then_inc(s("he_hid"), 1)
            pe.wait_ge(s("he_tanh"), 1)
            for b in range(B):
                nc.tensor.matmul(ps[0:E, 7, b:b + 1], agg_t[:, b * E:b * E + E], a_ge[:], start=True, stop=True)
                nc.tensor.matmul(ps[0:E, 7, 8 + b:9 + b], tmp_b[:, 1, b * E:b * E + E], av[:], start=True, stop=True)
            pe.wait_ge(s("av_all_made"), 1)
            nc.tensor.matmul(ps[:, 6, :], av_all[:], tmp_b[:, 1, 0:BF], start=True, stop=True).then_inc(s("se_made"), 1)
            pe.wait_ge(s("adjT_in"), 16 * T)
            pe.wait_ge(s("extra_out"), 1)
            for t in range(T):
                for m in range(T):
                    last = nc.tensor.matmul(ps[:, 7, 16 + t:17 + t], adjT[:, m, t * P:t * P + P], ones[:, 0:1], start=(m == 0), stop=(m == T - 1))
            last.then_inc(s("deg_made"), 1)
            for t in range(T):
                if t == 0:
                    pe.wait_ge(s("agg_out"), 2 * BP)
                if t >= 4:
                    pe.wait_ge(s("ind_out"), t - 3)
                for m in range(T):
                    last = nc.tensor.matmul(ps[:, t % 4, :], adjT[:, m, t * P:t * P + P], proj[:, m, :, P:2 * P], start=(m == 0), stop=(m == T - 1))
                last.then_inc(s("ind_made"), 1)
            pe.wait_ge(s("ind_out"), T)
            pe.wait_ge(s("neg_ident"), 1)

            def slots(tag, start, end):
                pe.sem_inc(s(tag + "diff"), 1)
                pe.sem_inc(s(tag + "extra"), 1)
                with pe.Fori(start, end) as k:
                    k0 = k - start
                    pe.wait_ge(s(tag + "sel"), k0 + 1)
                    pe.wait_ge(s(tag + "extra_read"), 3 * k0 + 3)
                    for t in range(T):
                        last = nc.tensor.matmul(ps[:, 4, t * 17:t * 17 + 17], sel[:, t * P:t * P + P], extra[:], start=True, stop=True)
                    last.then_inc(s(tag + "extra"), 1)
                    for c in range(4):
                        j = k0 * 4 + c
                        pe.wait_ge(s(tag + "zw"), j + 1)
                        for u in range(2):
                            t = 2 * c + u
                            nc.tensor.matmul(ps[:, 2 * (c % 2) + u, :], sel[:, t * P:t * P + P], agg[:].rearrange("e b f -> e (b f)"), start=True, stop=False)
                            last = nc.tensor.matmul(ps[:, 2 * (c % 2) + u, :], av_all[:], h_of(t), start=False, stop=True)
                        last.then_inc(s(tag + "diff"), 1)
            def rest(start, end):
                pe.wait_ge(s("max_count"), 1)
                many = pe.value_load(max_count[0:1, 0:1], min_val=0, max_val=E)
                with pe.If(many > start):
                    pe.wait_ge(s("f_g"), 4 * start + 2)
                    pe.wait_ge(s("f_csum"), start + 1)
                    slots("s_", start, end)
                    pe.wait_ge(s("s_g"), 4 * (end - start) + 2)
                    pe.wait_ge(s("s_csum"), end - start + 1)

            slots("f_", 0, FAST_SLOTS)
            rest(FAST_SLOTS, E)

            j = 0
            for q in range(8):
                src = (industry, g_sum)[q // 4]
                bp = q % 4
                if q == 0:
                    pe.wait_ge(s("f_zw"), 4 * FAST_SLOTS + 2)
                if q == 4:
                    pe.wait_ge(s("g_final"), 1)
                if q >= 2:
                    pe.wait_ge(s("pair_t_out"), q - 1)
                for t in range(T):
                    last = nc.tensor.transpose(ps[:, 2 * (q % 2) + t // 4, t % 4 * P:t % 4 * P + P], src[:, t, bp * P:bp * P + P], ident[:])
                last.then_inc(s("pair_t"), 1)
                pe.wait_ge(s("pair_t_out"), q + 1)
                for half in range(2):
                    for c in range(2):
                        if j == 0:
                            pe.wait_ge(s("f_extra_read"), 3 * FAST_SLOTS + 3)
                        if j >= 2:
                            pe.wait_ge(s("pair_tanh"), j - 1)
                        r = slice(half * F, half * F + F)
                        nc.tensor.matmul(ps[:, 4 + j % 2, :], fc_w[r, :], tmp_a[r, q % 2, c * HALF:c * HALF + HALF], start=True, stop=True).then_inc(s("pair_hid"), 1)
                        if j >= 1:
                            pair_scores(pe, j - 1)
                        j += 1
            pair_scores(pe, j - 1)

            if stop == "x1":
                return

            def at(w, i, *rest):
                return w[(slice(None), i) + rest] if isinstance(i, int) else w[(slice(None), bass.ds(i, 1)) + rest].squeeze(1)

            def batch_of(v, out_unit):
                return v - B * HEADS if out_unit else v // HEADS

            def scores(v, t, out_unit):
                pe.wait_ge(s("masked"), 8 * v + t + 1)
                if t % 4 == 0:
                    pe.wait_ge(s("y_out"), 2 * v + t // 4 + 1)
                for part, y in enumerate((y_hi, y_lo)):
                    for c in range(2):
                        last = nc.tensor.matmul(ps[:, c, :], at(y, v % 2, slice(t * P, t * P + P)),
                                                at(ax, batch_of(v, out_unit), slice(c * HALF, c * HALF + HALF)),
                                                start=(part == 0), stop=(part == 1), skip_group_check=True)
                last.then_inc(s("scores"), 1)

            def transpose(v, t):
                pe.wait_ge(s("probs"), 8 * v + t + 3)
                pe.wait_ge(s("lo"), 8 * v + t + 1)
                for m in range(T):
                    last = nc.tensor.transpose(ps[:, 2 + 2 * (t % 2) + m // 4, m % 4 * P:m % 4 * P + P], probs[:, t % 2, m * P:m * P + P], ident[:])
                last.then_inc(s("pT"), 1)

            def weigh(v, cc, part, out_unit):
                if part == 0:
                    pe.wait_ge(s("lo"), 4 * (2 * v + cc) + 6)
                    pe.wait_ge(s("osum"), 2 * v + cc + 1)
                for m in (2 * part, 2 * part + 1):
                    nc.tensor.matmul(ps[:, 6, :], at(x2, batch_of(v, out_unit), m, slice(0, P)), pt_hi[:, cc, m, :], start=(m == 0), stop=False)
                    last = nc.tensor.matmul(ps[:, 6, :], at(x2, batch_of(v, out_unit), m, slice(0, P)), pt_lo[:, cc, m, :], start=False, stop=(m == T - 1))
                last.then_inc(s("pv"), 1)

            def repeat_inverse(v, cc):
                pe.wait_ge(s("rinv"), 2 * v + cc + 3)
                for i in range(4):
                    last = nc.tensor.transpose(ps[:, 7, i * P:i * P + P], rinv[:, 4 * cc + i:4 * cc + i + 1].to_broadcast([P, P]), ident[:])
                last.then_inc(s("rinv_rows"), 1)

            def project(v, cc, out_unit):
                pe.wait_ge(s("normed"), 2 * v + cc + 3)
                if not out_unit:
                    pe.wait_ge(s("w2_in"), 32 * v + 32)
                nc.tensor.matmul(ps[:, 7, :], (fold if out_unit else w2)[:], onorm[:], start=True, stop=True).then_inc(s("projected"), 1)

            def make_y(v, cc, out_unit):
                x_t_parts = at(ax, batch_of(v, out_unit), slice(cc * HALF, cc * HALF + HALF))
                if out_unit:
                    nc.tensor.matmul(ps[:, 7, :], fold16[:], x_t_parts, start=True, stop=True).then_inc(s("y"), 1)
                else:
                    nc.tensor.matmul(ps[:, 7, :], at(g_hi, v % HEADS, slice(0, P)), x_t_parts, start=True, stop=False)
                    nc.tensor.matmul(ps[:, 7, :], at(g_lo, v % HEADS, slice(0, P)), x_t_parts, start=False, stop=True).then_inc(s("y"), 1)

            def make_h(q, cc):
                pe.wait_ge(s("cat"), 2 * HEADS * q + 2 * HEADS + cc + 1)
                for h in range(HEADS):
                    last = nc.tensor.matmul(ps[:, 7, :], w_out[:, h, :], cat[:, h, cc * HALF:cc * HALF + HALF], start=(h == 0), stop=(h == HEADS - 1))
                last.then_inc(s("h_made"), 1)

            def unit(v, first=False, last=False, out_unit=False, h_batch=None):
                o = out_unit
                for t in range(T):
                    if t < 7:
                        scores(v, t + 1, o)
                    elif not last:
                        scores(v + 1, 0, o)
                    if t >= 5:
                        weigh(v, 0, t - 5, o)
                    elif not first:
                        weigh(v - 1, 0 if t == 0 else 1, 3 if t == 0 else t - 1, o)
                    transpose(v, t)
                    if t == 1 and not first:
                        pe.wait_ge(s("y_out"), 2 * v + 2)
                        repeat_inverse(v - 1, 0)
                    if t == 2 and not first:
                        project(v - 1, 0, o)
                    if t == 3:
                        if first:
                            pe.wait_ge(s("y_out"), 2 * v + 2)
                        else:
                            pe.wait_ge(s("z"), 2 * v - 1)
                        if h_batch is not None:
                            make_h(h_batch, 0)
                            pe.wait_ge(s("h_lo"), 2 * h_batch + 1)
                            make_h(h_batch, 1)
                            pe.wait_ge(s("h_lo"), 2 * h_batch + 2)
                        if not last:
                            make_y(v + 1, 0, o)
                    if t == 5 and not first:
                        if last:
                            pe.wait_ge(s("z"), 2 * v - 1)
                        else:
                            pe.wait_ge(s("y_out"), 2 * v + 3)
                        repeat_inverse(v - 1, 1)
                    if t == 6 and not first:
                        project(v - 1, 1, o)
                    if t == 7 and not last:
                        if first:
                            pe.wait_ge(s("y_out"), 2 * v + 3)
                        else:
                            pe.wait_ge(s("z"), 2 * v)
                        make_y(v + 1, 1, o)

            def drain(v, o):
                weigh(v, 0, 3, o)
                pe.wait_ge(s("z"), 2 * v)
                repeat_inverse(v, 0)
                project(v, 0, o)
                for part in range(4):
                    weigh(v, 1, part, o)
                pe.wait_ge(s("z"), 2 * v + 1)
                repeat_inverse(v, 1)
                project(v, 1, o)
                pe.wait_ge(s("z"), 2 * v + 2)

            pe.wait_ge(s("x1_ready"), 2)
            pe.wait_ge(s("wo_in"), 80)
            pe.sem_inc(s("pT"), 2)
            pe.sem_inc(s("scores"), 1)
            pe.sem_inc(s("projected"), 1)
            pe.sem_inc(s("h_made"), 2)
            pe.sem_inc(s("pv"), 8)
            pe.sem_inc(s("rinv_rows"), 2)
            for b in range(B):
                pe.wait_ge(s("x2"), 2 * b + 2)
                if b >= 2:
                    pe.wait_ge(s("ax"), b - 1)
                for t in range(T):
                    last_t = nc.tensor.transpose(ps[:, b % 2, :].bitcast(FP16)[:, t * P:t * P + P], x2[:, b, t, :], ident16[:])
                last_t.then_inc(s("xt16"), 1)
            pe.wait_ge(s("ax"), B)
            make_y(0, 0, False)
            pe.wait_ge(s("y_out"), 1)
            make_y(0, 1, False)
            scores(0, 0, False)
            unit(0, first=True)
            with pe.Fori(1, HEADS + 1) as v:
                unit(v)
            with pe.Fori(1, B - 1) as q:
                unit(q * HEADS + 1, h_batch=q - 1)
                with pe.Fori(2, HEADS + 1) as j:
                    unit(q * HEADS + j)
            unit((B - 1) * HEADS + 1, h_batch=B - 2)
            with pe.Fori((B - 1) * HEADS + 2, B * HEADS - 1) as v:
                unit(v)
            unit(B * HEADS - 1, last=True)
            drain(B * HEADS - 1, False)
            make_h(B - 1, 0)
            pe.wait_ge(s("h_lo"), 2 * B - 1)
            make_h(B - 1, 1)
            pe.wait_ge(s("h_lo"), 2 * B)
            for b in range(B):
                if b >= 2:
                    pe.wait_ge(s("h_x2"), b - 1)
                for t in range(T):
                    last_t = nc.tensor.transpose(ps[:, b % 2, :].bitcast(FP16)[:, t * P:t * P + P], ax[:, b, t * P:t * P + P], ident16[:])
                last_t.then_inc(s("h_t"), 1)
            v0 = B * HEADS
            make_y(v0, 0, True)
            pe.wait_ge(s("y_out"), 2 * v0 + 1)
            make_y(v0, 1, True)
            pe.wait_ge(s("h_x2"), B)
            scores(v0, 0, True)
            unit(v0, first=True, out_unit=True)
            with pe.Fori(v0 + 1, v0 + B - 1) as v:
                unit(v, out_unit=True)
            unit(v0 + B - 1, last=True, out_unit=True)
            drain(v0 + B - 1, True)
            pe.wait_ge(s("cat"), 2 * (v0 + B) + 2)
            for b in range(B):
                for t in range(T):
                    last_t = nc.tensor.transpose(ps[:, b, t * F:t * F + F], cat[0:F, b, t * P:t * P + P], ident[0:F, 0:F])
                last_t.then_inc(s("zo"), 1)

        @block.vector
        def _(dve):
            v = nc.vector
            v.memset(w_block[:], 0.0).then_inc(s("w_block_zero"), 1)
            link(v.memset(node_block[:], 0.0))
            v.memset(ones[:], 1.0).then_inc(s("ones_made"), 1)
            dve.wait_ge(s("consts_in"), 48)
            v.tensor_copy(ident16[:], ident[:])
            for dup in range(2):
                v.tensor_tensor(fold[:, dup * F:dup * F + F], ident[:, 0:F], ident[:, F:P], ALU.add)
                v.tensor_tensor(fold16[:, dup * F:dup * F + F], ident[:, 0:F], ident[:, F:P], ALU.add)
            dve.wait_ge(s("wa_made"), 1)
            dve.wait_ge(s("w_block_zero"), 1)
            for half in range(2):
                r = slice(half * F, half * F + F)
                v.tensor_copy(w_block[r, 2 * P + half:2 * P + half + 1], ps[r, 4, 1:2])
                v.tensor_copy(node_block[r, half * F:half * F + F], ps[r, 4, 0:1].to_broadcast([F, F])).then_inc(s("wa_out"), 1)
            dve.wait_ge(s("wb_in"), 64)
            dve.wait_ge(s("wa_out"), 2)
            v.nop().then_inc(s("w_ready"), 1)
            for q in range(0, 2 * BP, 2):
                dve.wait_ge(s("xt_made"), q + 1)
                v.tensor_copy(x_t[:, q // 2, 0:HALF], ps[:, q % 4, :]).then_inc(s("xt_out0"), 1)
            dve.wait_ge(s("g_made"), 1)
            gp = ps[:, 5, :].rearrange("p (h f) -> p h f", h=HEADS)
            v.tensor_reduce(g_abs[:], gp, axis=AX.X, op=ALU.max, apply_absolute_value=True).then_inc(s("g_abs"), 1)
            dve.wait_ge(s("g_max"), 1)
            v.tensor_scalar(g_max[:], g_max[:], 1.0 / GTOP, 1e-30, ALU.mult, ALU.max).then_inc(s("g_max"), 1)
            dve.wait_ge(s("g_max"), 2)
            link(v.reciprocal(g_inv[:], g_max[:]))
            v.tensor_scalar(g_scale[:], g_max[:], -1.0 / (XS * XS), None, ALU.mult)
            for dup in range(2):
                link(v.tensor_tensor(g_hi[:, :, dup * F:dup * F + F], gp, g_inv[:].unsqueeze(2).to_broadcast([P, HEADS, F]), ALU.mult))
            gs = tmp_a[:, 0, 0:BF].rearrange("p (h f) -> p h f", h=HEADS)
            link(v.tensor_tensor(gs, gp, g_inv[:].unsqueeze(2).to_broadcast([P, HEADS, F]), ALU.mult))
            for dup in range(2):
                v.tensor_tensor(g_lo[:, :, dup * F:dup * F + F], gs, g_hi[:, :, 0:F], ALU.subtract).then_inc(s("g_out"), 1)
            dve.wait_ge(s("w_norm"), 1)
            dve.wait_ge(s("wo_in"), 80)
            link(v.tensor_scalar(b_abs[:], bh[:], -1.0, None, ALU.mult))
            link(v.tensor_tensor(b_abs[:], b_abs[:], bh[:], ALU.max))
            link(v.scalar_tensor_tensor(w_norm[:], w_norm[:], float(F) ** 0.5, b_abs[:], ALU.mult, ALU.add))
            wa = tmp_c[:, 0, 0:HALF].rearrange("p (h f) -> p h f", h=HEADS)
            link(v.tensor_scalar(wa, w_out[:, :, 0:F], -1.0, None, ALU.mult))
            link(v.tensor_tensor(wa, wa, w_out[:, :, 0:F], ALU.max))
            v.tensor_tensor(wa, wa, w_norm[:].unsqueeze(2).to_broadcast([P, HEADS, F]), ALU.mult).then_inc(s("w_abs"), 1)
            for i in range(0, T * BP, 2):
                dve.wait_ge(s("proj_made"), i + 1)
                v.tensor_copy(proj[:, i // BP, i % BP, :], ps[:, i % 4, 0:WCOL]).then_inc(s("proj_out0"), 1)
            dve.wait_ge(s("h_bound"), 1)
            v.tensor_reduce(h_top[:], ps[:, 6, :].rearrange("p (h f) -> p f h", h=HEADS), axis=AX.X, op=ALU.add).then_inc(s("h_top"), 1)
            dve.wait_ge(s("h_top"), 1)
            link(v.tensor_reduce(h_unit[:], h_top[:], axis=AX.X, op=ALU.max))
            link(v.tensor_scalar(h_unit[:], h_unit[:], 1.0 / HTOP, 1e-15, ALU.mult, ALU.max))
            v.reciprocal(h_inv[:], h_unit[:])
            v.tensor_scalar(h_scale[:], h_unit[:], h_unit[:], -1.0, ALU.mult, ALU.mult)
            link(v.tensor_scalar(z_scale[:], h_unit[:], 1.0 / PSC, None, ALU.mult))
            dve.wait_ge(s("ht_in"), 32)
            v.tensor_scalar(mask_t[:], mask_t[:], 0.0, None, ALU.is_gt).then_inc(s("mask_t_made"), 1)
            dve.wait_ge(s("mask_t_made"), 1)
            link(v.tensor_scalar(edge_bias[:], mask_t[:], -MASKED, MASKED, ALU.mult, ALU.add))
            dve.wait_ge(s("cnt_made"), 1)
            dve.wait_ge(s("g_out"), 2)
            v.scalar_tensor_tensor(tmp_a[0:E, 1, :], ps[0:E, 6:8, :].rearrange("p a b -> p (a b)"), 0.0, mask_t[0:E, :], ALU.is_equal, ALU.add).then_inc(s("eff_made"), 1)
            dve.wait_ge(s("rank_made"), 1)
            dve.wait_ge(s("eff_made"), 1)
            v.tensor_tensor(rank[:], ps[0:E, 6:8, :].rearrange("p a b -> p (a b)"), tmp_a[0:E, 1, :], ALU.mult).then_inc(s("rank_out"), 1)
            link(v.memset(max_all[:], 0.0))
            dve.wait_ge(s("rank_out"), 1)
            v.tensor_reduce(max_all[0:E, :], rank[:], axis=AX.X, op=ALU.max).then_inc(s("max_all"), 1)
            dve.wait_ge(s("hn_in"), 16)
            link(v.tensor_scalar(mask_n[:], mask_n[:], 0.0, None, ALU.is_gt))
            link(v.tensor_reduce(node_cnt[:], mask_n[:], axis=AX.X, op=ALU.add))
            link(v.tensor_scalar(node_empty[:], node_cnt[:], 0.0, None, ALU.is_equal))
            link(v.tensor_tensor(mask_n[:], mask_n[:], node_empty[:].unsqueeze(2).to_broadcast([P, T, E]), ALU.add))
            link(v.tensor_scalar(mask_n[:], mask_n[:], -MASKED, MASKED, ALU.mult, ALU.add))
            for bp in range(BP):
                dve.wait_ge(s("edge_s"), bp + 1)
                if bp:
                    dve.wait_ge(s("edge_exp"), bp)
                e_s = ps[:, 4:6, :].rearrange("p a b -> p (a b)")
                link(v.tensor_copy(tmp_a[:, 1, :], e_s))
                v.scalar_tensor_tensor(tmp_a[:, 1, :], e_s, 0.2, tmp_a[:, 1, :], ALU.mult, ALU.max).then_inc(s("edge_lk"), 1)
                dve.wait_ge(s("edge_lk"), bp + 1)
                v.tensor_tensor_reduce(out=tmp_a[:, 0, :], in0=tmp_a[:, 1, :], in1=edge_bias[:], scale=-1.0, scalar=3e38,
                                       op0=ALU.add, op1=ALU.min, accum_out=edge_max[:, bp:bp + 1]).then_inc(s("edge_masked"), 1)
                dve.wait_ge(s("edge_exp"), bp + 1)
                link(v.reciprocal(edge_inv[:, bp:bp + 1], edge_sum[:, bp:bp + 1]))
                dve.wait_ge(s("agg_made"), bp + 1)
                for half in range(2):
                    r = slice(half * F, half * F + F)
                    v.tensor_scalar(agg[:, 2 * bp + half, :], ps[r, bp, r], edge_inv[r, bp:bp + 1], None, ALU.mult).then_inc(s("agg_out"), 1)
            dve.wait_ge(s("aggt_made"), 1)
            v.tensor_copy(agg_t[:], ps[0:F, 4, :]).then_inc(s("aggt_out"), 1)
            dve.wait_ge(s("he_re"), 2)
            link(v.scalar_tensor_tensor(he_r[:], he_e[:], 1.0, he_r[:], ALU.min, ALU.add))
            v.tensor_scalar(he_r[:], he_r[:], -1.0, None, ALU.add).then_inc(s("he_made"), 1)
            dve.wait_ge(s("fc_in"), 80)
            v.tensor_copy(av_all[:], av[:].to_broadcast([P, P])).then_inc(s("av_all_made"), 1)
            dve.wait_ge(s("se_made"), 1)
            v.memset(extra[:, 16:17], 1.0)
            v.tensor_copy(extra[:, 0:16], ps[0:E, 7, 0:16]).then_inc(s("extra_out"), 1)
            dve.wait_ge(s("max_one"), 1)
            v.tensor_copy(max_count[:], max_one[0:1, :]).then_inc(s("max_count"), 1)
            v.tensor_scalar(av_all[:], ident[:], -1.0, None, ALU.mult).then_inc(s("neg_ident"), 1)
            se = ps[:, 6, :].rearrange("p (b e) -> p b e", b=B)
            tse = [tmp_a[:, i, 0:BF].rearrange("p (b e) -> p b e", b=B) for i in range(2)]
            for t in range(T):
                link(v.tensor_tensor(tse[t % 2], se, mask_n[:, t, :].unsqueeze(1).to_broadcast([P, B, E]), ALU.add))
                link(v.tensor_reduce(se_max[:, t, :], tse[t % 2], axis=AX.X, op=ALU.max))
            for t in range(T):
                dve.wait_ge(s(f"adj_in{t % 2}"), 16 * (t // 2 + 1))
                v.tensor_scalar(adj_mask[:, t, :], tmp_d[:, t % 2, :], 0.0, MASKED, ALU.is_equal, ALU.mult).then_inc(s("mask_made"), 1)
            dve.wait_ge(s("deg_made"), 1)
            link(v.tensor_scalar(deg[:], ps[:, 7, 16:16 + T], 1.0, None, ALU.max))
            link(v.reciprocal(deg[:], deg[:]))
            for t in range(T):
                dve.wait_ge(s("ind_made"), t + 1)
                v.tensor_scalar(industry[:, t, :], ps[:, t % 4, :], deg[:, t:t + 1], None, ALU.mult).then_inc(s("ind_out"), 1)

            def slots(tag, start, end):
                dve.sem_inc(s(tag + "extra_read"), 3)
                dve.sem_inc(s(tag + "zw"), 2)
                dve.sem_inc(s(tag + "v"), 2)
                with dve.Fori(start, end) as k:
                    k0 = k - start
                    dve.wait_ge(s(tag + "diff"), k0 * 4 + 1)
                    dve.wait_ge(s(tag + "extra"), k0 + 1)
                    v.tensor_scalar(sel, rank[:], slot_no[0:E, bass.ds(k, 1)], None, ALU.is_equal).then_inc(s(tag + "sel"), 1)
                    ex = ps[:, 4, 0:T * 17].rearrange("p (t c) -> p t c", t=T)
                    hn = proj[:, :, :, 2 * P:2 * P + 2]
                    dve.wait_ge(s(tag + "extra"), k0 + 2)
                    dve.wait_ge(s(tag + "th"), k0 + 1)
                    v.tensor_tensor(bl[:].rearrange("p t (a b) -> p t a b", a=BP), ex[:, :, 0:8].rearrange("p t (a b) -> p t a b", a=BP), hn, ALU.add).then_inc(s(tag + "bl"), 1)
                    dve.wait_ge(s(tag + "coef"), k0 + 1)
                    v.tensor_tensor(sx[:], ex[:, :, 8:16], se_max[:], ALU.subtract).then_inc(s(tag + "extra_read"), 1)
                    v.tensor_scalar(vb[:], ex[:, :, 16:17].rearrange("p t a -> p (t a)"), -MASKED, MASKED, ALU.mult, ALU.add).then_inc(s(tag + "extra_read"), 1)
                    dve.wait_ge(s(tag + "extra_read"), 3 * k0 + 5)
                    v.tensor_tensor(sx[:], sx[:], vb[:].unsqueeze(2).to_broadcast([P, T, B]), ALU.add).then_inc(s(tag + "sx"), 1)
                    dve.wait_ge(s(tag + "th"), k0 + 2)
                    dve.wait_ge(s(tag + "zw"), 4 * k0 + 2)
                    v.tensor_scalar(wgt[:], th[:], -0.5, 0.5, ALU.mult, ALU.add).then_inc(s(tag + "wgt"), 1)
                    v.nop().then_inc(s(tag + "extra_read"), 1)
                    dve.wait_ge(s(tag + "wgt"), k0 + 1)
                    for c in range(4):
                        j = k0 * 4 + c
                        dve.wait_ge(s(tag + "diff"), j + 2)
                        dve.wait_ge(s(tag + "exp"), j + 1)
                        for u in range(2):
                            t = 2 * c + u
                            w3 = wgt[:, t, :].unsqueeze(2).to_broadcast([P, B, F])
                            last = v.tensor_tensor(tmp_a[:, c % 2, u * HALF:u * HALF + HALF].rearrange("p (b f) -> p b f", b=B), ps[:, 2 * (c % 2) + u, :].rearrange("p (b f) -> p b f", b=B), w3, ALU.mult)
                        last.then_inc(s(tag + "zw"), 1)
                        dve.wait_ge(s(tag + "zw"), j + 3)
                        zz = tmp_a[:, c % 2, :].rearrange("p (u a b) -> p u a b", u=2, a=BP)
                        v.tensor_tensor(zz, zz, proj[:, 2 * c:2 * c + 2, :, 0:P], ALU.add).then_inc(s(tag + "z"), 1)
                        dve.wait_ge(s(tag + "exp"), j + 3)
                        dve.wait_ge(s(tag + "g"), j + 1)
                        v.scalar_tensor_tensor(tmp_d[:, c % 2, :], tmp_c[:, c % 2, :], 1.0, tmp_b[:, c % 2, :], ALU.min, ALU.add).then_inc(s(tag + "v"), 1)
            def rest(start, end):
                dve.wait_ge(s("max_count"), 1)
                many = dve.value_load(max_count[0:1, 0:1], min_val=0, max_val=E)
                with dve.If(many > start):
                    dve.wait_ge(s("f_g"), 4 * start + 2)
                    dve.wait_ge(s("f_csum"), start + 1)
                    slots("s_", start, end)
                    dve.wait_ge(s("s_g"), 4 * (end - start) + 2)
                    dve.wait_ge(s("s_csum"), end - start + 1)

            slots("f_", 0, FAST_SLOTS)
            rest(FAST_SLOTS, E)

            dve.wait_ge(s("f_g"), 4 * FAST_SLOTS + 2)
            dve.wait_ge(s("f_csum"), FAST_SLOTS + 1)
            link(v.reciprocal(coef_sum[:], coef_sum[:]))
            g4 = g_sum.rearrange("p t (b f) -> p (t b) f", b=B)
            link(v.tensor_tensor(g4, g4, coef_sum[:].rearrange("p t b -> p (t b)").unsqueeze(2).to_broadcast([P, T * B, F]), ALU.mult))
            v.tensor_scalar(g_sum, g_sum, -1.0, None, ALU.add).then_inc(s("g_final"), 1)
            for q in range(8):
                dve.wait_ge(s("pair_t"), q + 1)
                if q >= 2:
                    dve.wait_ge(s("pair_hid"), 4 * (q - 1))
                v.tensor_copy(tmp_a[:, q % 2, :], ps[:, 2 * (q % 2):2 * (q % 2) + 2, :].rearrange("p a b -> p (a b)")).then_inc(s("pair_t_out"), 1)
            dve.wait_ge(s("pair_score"), 32)
            link(v.tensor_copy(sc[:].rearrange("p s t b -> p (s t b)"), ps[:, 6, 0:2 * T * B]))
            v.tensor_tensor(bl[:], sc[:, 1, :, :], sc[:, 0, :, :], ALU.subtract).then_inc(s("pair_diff"), 1)
            i4 = industry.rearrange("p t (b f) -> p (t b) f", b=B)
            dve.wait_ge(s("g_final"), 1)
            link(v.tensor_tensor(g4, g4, i4, ALU.subtract))
            dve.wait_ge(s("pair_th"), 1)
            link(v.tensor_scalar(wgt[:], th[:], 0.5, 0.5, ALU.mult, ALU.add))
            link(v.tensor_tensor(g4, g4, wgt[:].rearrange("p t b -> p (t b)").unsqueeze(2).to_broadcast([P, T * B, F]), ALU.mult))
            x4 = x_nat[:].rearrange("p t b f -> p (t b) f")
            link(v.tensor_tensor(i4, i4, x4, ALU.add))
            link(v.tensor_tensor(i4, i4, g4, ALU.add))
            layer_norm_dve(dve, "ln0_", i4, g4)
            for b2 in range(2):
                v.tensor_tensor(x1[:, 4 * b2:4 * b2 + 4, :, :].rearrange("p b t f -> p t b f") if False else x1[:, 4 * b2:4 * b2 + 4, :, :].transpose([0, 2, 1, 3]),
                                industry.rearrange("p t (b f) -> p t b f", b=B)[:, :, 4 * b2:4 * b2 + 4, :],
                                ln_var[:].rearrange("p (t b) -> p t b", b=B)[:, :, 4 * b2:4 * b2 + 4].unsqueeze(3).to_broadcast([P, T, 4, F]), ALU.mult).then_inc(s("x1_ready"), 1)

            if stop == "x1":
                return

            def at(w, i, *rest):
                return w[(slice(None), i) + rest] if isinstance(i, int) else w[(slice(None), bass.ds(i, 1)) + rest].squeeze(1)

            def mask(v, t):
                dve.wait_ge(s("scores"), 8 * v + t + 2)
                dve.wait_ge(s("probs"), 8 * v + t + 1)
                nc.vector.nop(nofuse=True)
                nc.vector.tensor_tensor_reduce(out=masked[:, t % 2, :], in0=ps[:, 0:2, :].rearrange("p a b -> p (a b)"), in1=adj_mask[:, t, :], scale=cur_scale[:],
                                               scalar=3e38, op0=ALU.add, op1=ALU.min, accum_out=neg_max[:, t % 2:t % 2 + 1]).then_inc(s("masked"), 1)

            def lo(v, t):
                dve.wait_ge(s("hi"), 8 * v + t + 1)
                where = (slice(None), t // 4, slice(None), slice(t % 4 * P, t % 4 * P + P))
                nc.vector.scalar_tensor_tensor(pt_lo[where], ps[:, 2 + 2 * (t % 2):4 + 2 * (t % 2), :].rearrange("p a (m n) -> p (a m) n", n=P), PSC,
                                               pt_hi[where], ALU.mult, ALU.subtract).then_inc(s("lo"), 1)

            def invert(v, cc):
                dve.wait_ge(s("probs"), 8 * v + 4 * cc + 6)
                dve.wait_ge(s("rinv_rows"), 2 * v + cc + 1)
                nc.vector.reciprocal(rinv[:, 4 * cc:4 * cc + 4], sums[:, 4 * cc:4 * cc + 4]).then_inc(s("rinv"), 1)

            def normalise(v, cc):
                dve.wait_ge(s("rinv_rows"), 2 * v + cc + 3)
                dve.wait_ge(s("osum"), 2 * v + cc + 2)
                dve.wait_ge(s("projected"), 2 * v + cc + 1)
                nc.vector.tensor_tensor(onorm[:], osum[:, cc, :], ps[:, 7, :], ALU.mult).then_inc(s("normed"), 1)

            def take_y(v, cc):
                half = slice(cc * HALF, cc * HALF + HALF)
                dve.wait_ge(s("y_hi"), 2 * v + cc + 1)
                nc.vector.tensor_tensor(at(y_lo, v % 2, half), ps[:, 7, :], at(y_hi, v % 2, half), ALU.subtract).then_inc(s("y_out"), 1)

            def take_h(q, cc):
                dve.wait_ge(s("h_hi"), 2 * q + cc + 1)
                half = slice(cc * HALF, cc * HALF + HALF)
                low = ax[F:P, q, half] if isinstance(q, int) else ax[F:P, bass.ds(q, 1), half].squeeze(1)
                nc.vector.scalar_tensor_tensor(low, ps[F:P, 7, :], h_inv[F:P, :], low, ALU.mult, ALU.subtract).then_inc(s("h_lo"), 1)

            def unit(v, first=False, last=False, out_unit=False, h_batch=None):
                for t in range(T):
                    if t < 7:
                        mask(v, t + 1)
                    elif not last:
                        if not out_unit:
                            dve.wait_ge(s("masked"), 8 * v + 9)
                            nc.vector.tensor_copy(cur_scale[:], g_scale[:, bass.ds((v + 1) % HEADS, 1)]).then_inc(s("cur_scale"), 1)
                            dve.wait_ge(s("cur_scale"), v + 2)
                        mask(v + 1, 0)
                    if t > 0:
                        lo(v, t - 1)
                    elif not first:
                        lo(v - 1, 7)
                    if t == 1 and not first:
                        normalise(v - 1, 0)
                    if t == 5 and not first:
                        normalise(v - 1, 1)
                    if t == 0 and not first:
                        take_y(v, 1)
                        invert(v - 1, 1)
                    if t == 4:
                        invert(v, 0)
                    if t == 3 and h_batch is not None:
                        for cc in range(2):
                            take_h(h_batch, cc)
                    if t == 4 and not last:
                        take_y(v + 1, 0)

            def drain(v):
                lo(v, 7)
                normalise(v, 0)
                invert(v, 1)
                normalise(v, 1)

            dve.wait_ge(s("x1_ready"), 2)
            dve.sem_inc(s("lo"), 2)
            dve.sem_inc(s("masked"), 1)
            dve.sem_inc(s("rinv"), 2)
            dve.sem_inc(s("normed"), 2)
            for b in range(B):
                nc.vector.tensor_scalar(x2[:, b, :, 0:F], x1[:, b], XS, None, ALU.mult).then_inc(s("x2"), 1)
                dve.wait_ge(s("x2"), 2 * b + 1)
                nc.vector.scalar_tensor_tensor(x2[:, b, :, F:P], x1[:, b], XS, x2[:, b, :, 0:F], ALU.mult, ALU.subtract).then_inc(s("x2"), 1)
            nc.vector.tensor_copy(cur_scale[:], g_scale[:, 0:1]).then_inc(s("cur_scale"), 1)
            take_y(0, 0)
            take_y(0, 1)
            dve.wait_ge(s("cur_scale"), 1)
            mask(0, 0)
            unit(0, first=True)
            with dve.Fori(1, HEADS + 1) as v:
                unit(v)
            with dve.Fori(1, B - 1) as q:
                unit(q * HEADS + 1, h_batch=q - 1)
                with dve.Fori(2, HEADS + 1) as j:
                    unit(q * HEADS + j)
            unit((B - 1) * HEADS + 1, h_batch=B - 2)
            with dve.Fori((B - 1) * HEADS + 2, B * HEADS - 1) as v:
                unit(v)
            unit(B * HEADS - 1, last=True)
            drain(B * HEADS - 1)
            for cc in range(2):
                take_h(B - 1, cc)
            v0 = B * HEADS
            dve.wait_ge(s("masked"), 8 * v0 + 1)
            nc.vector.tensor_copy(cur_scale[:], h_scale[:]).then_inc(s("cur_scale"), 1)
            take_y(v0, 0)
            take_y(v0, 1)
            dve.wait_ge(s("cur_scale"), v0 + 1)
            mask(v0, 0)
            unit(v0, first=True, out_unit=True)
            with dve.Fori(v0 + 1, v0 + B - 1) as v:
                unit(v, out_unit=True)
            unit(v0 + B - 1, last=True, out_unit=True)
            drain(v0 + B - 1)
            for b in range(B):
                dve.wait_ge(s("zo"), b + 1)
                nc.vector.tensor_tensor(x1[:, b], x1[:, b], ps[:, b, :].rearrange("p (t f) -> p t f", f=F), ALU.add).then_inc(s("x1_done"), 1)
            dve.wait_ge(s("x1_done"), B)
            xf = x1[:].rearrange("p b t f -> p (b t) f")
            layer_norm_dve(dve, "ln1_", xf, pt_sq)
            for q in range(4):
                nc.vector.tensor_tensor(xf[:, 16 * q:16 * q + 16, :], xf[:, 16 * q:16 * q + 16, :], ln_var[:, 16 * q:16 * q + 16].unsqueeze(2).to_broadcast([P, 16, F]), ALU.mult).then_inc(s("ln1_out"), 1)

        @block.gpsimd
        def _(pool):
            g = nc.gpsimd
            pool.wait_ge(s("g_abs"), 1)
            g.partition_all_reduce(g_max[:], g_abs[:], P, RMAX).then_inc(s("g_max"), 1)
            pool.wait_ge(s("max_all"), 1)
            g.partition_all_reduce(max_one[:], max_all[:], P, RMAX).then_inc(s("max_one"), 1)
            pool.wait_ge(s("ind_made"), T)
            g.memset(g_sum, 0.0).then_inc(s("f_g"), 2)
            g.memset(coef_sum[:], 0.0).then_inc(s("f_csum"), 1)

            def slots(tag, start, end):
                pool.sem_inc(s(tag + "vc"), 1)
                if tag == "s_":
                    pool.sem_inc(s(tag + "g"), 2)
                    pool.sem_inc(s(tag + "csum"), 1)
                with pool.Fori(start, end) as k:
                    k0 = k - start
                    pool.wait_ge(s(tag + "coef"), k0 + 2)
                    pool.wait_ge(s(tag + "csum"), k0 + 1)
                    g.tensor_tensor(coef_sum[:], coef_sum[:], coef[:], ALU.add).then_inc(s(tag + "csum"), 1)
                    for c in range(4):
                        j = k0 * 4 + c
                        vv = tmp_d[:, c % 2, :].rearrange("p (t f) -> p t f", f=F)
                        pool.wait_ge(s(tag + "v"), j + 3)
                        g.tensor_tensor(vv, vv, coef[:, 2 * c:2 * c + 2, :].rearrange("p t b -> p (t b)").unsqueeze(2).to_broadcast([P, 2 * B, F]), ALU.mult).then_inc(s(tag + "vc"), 1)
                        pool.wait_ge(s(tag + "vc"), j + 2)
                        pool.wait_ge(s(tag + "g"), j + 2)
                        gg = g_sum[:, 2 * c:2 * c + 2, :].rearrange("p t q -> p (t q)")
                        g.tensor_tensor(gg, gg, tmp_d[:, c % 2, :], ALU.add).then_inc(s(tag + "g"), 1)
            def rest(start, end):
                pool.wait_ge(s("max_count"), 1)
                many = pool.value_load(max_count[0:1, 0:1], min_val=0, max_val=E)
                with pool.If(many > start):
                    pool.wait_ge(s("f_g"), 4 * start + 2)
                    pool.wait_ge(s("f_csum"), start + 1)
                    slots("s_", start, end)
                    pool.wait_ge(s("s_g"), 4 * (end - start) + 2)
                    pool.wait_ge(s("s_csum"), end - start + 1)

            slots("f_", 0, FAST_SLOTS)
            rest(FAST_SLOTS, E)


            if stop == "x1":
                return

            def leaky(v, cc, slot):
                pool.wait_ge(s("z"), 2 * v + cc + 1)
                pool.nop(nofuse=True)
                g.tensor_scalar(zm[:, cc, :], zc[:, cc, :], 0.0, -0.99, ALU.min, ALU.mult).then_inc(s("zm"), 1)
                pool.wait_ge(s("zm"), 2 * v + cc + 1)
                where = cat[:, bass.ds(slot, 1), cc * HALF:cc * HALF + HALF].squeeze(1)
                g.tensor_tensor(where, zc[:, cc, :], zm[:, cc, :], ALU.add).then_inc(s("cat"), 1)

            pool.wait_ge(s("x1_ready"), 2)
            pool.sem_inc(s("cat"), 2)
            with pool.Fori(0, B) as b:
                with pool.Fori(0, HEADS) as h:
                    for cc in range(2):
                        pool.wait_ge(s("h_made"), 2 * b + cc + 1)
                        pool.wait_ge(s("cat"), 2 * (b * HEADS + h) + cc + 1)
                        leaky(b * HEADS + h, cc, h)
            pool.wait_ge(s("h_made"), 2 * B + 2)
            with pool.Fori(0, B) as b:
                for cc in range(2):
                    pool.wait_ge(s("cat"), 2 * (B * HEADS + b) + cc + 1)
                    leaky(B * HEADS + b, cc, b)




def _layout(i):
    import numpy as np
    c = np.ascontiguousarray
    n = {k: np.asarray(v) for k, v in i.items()}
    consts = np.zeros((P, 2 * P), np.float32)
    consts[:, 0:P] = np.eye(P)
    consts[0:E, P:P + E] = np.triu(np.ones((E, E)))
    consts[:, P + E:P + 2 * E] = np.arange(1, E + 1)
    return {
        "consts": consts, "x": c(n["x"]), "adj": c(n["adj"]), "adjT": c(n["adj"].T),
        "H": c(n["L0_gnn_H"]), "HT": c(n["L0_gnn_H"].T), "W": c(n["L0_gnn_W"]), "WT": c(n["L0_gnn_W"].T),
        "W_ind": c(n["L0_gnn_W_ind"]), "a_node": c(n["L0_gnn_a_node"].reshape(F, 1)), "a_gn": c(n["L0_gnn_a_gn"].reshape(F, 1)),
        "a_ge": c(n["L0_gnn_a_ge"].reshape(F, 1)), "fcW": c(n["L0_gnn_fcW"]), "fcb": c(n["L0_gnn_fcb"].reshape(P, 1)),
        "av": c(n["L0_gnn_av"].reshape(P, 1)), "Wh": c(n["L1_gnn_Wh"]), "WhT": c(n["L1_gnn_Wh"].transpose(0, 2, 1)),
        "bhT": c(n["L1_gnn_bh"].T), "W_out": c(n["L1_gnn_W_out"]), "b_out": c(n["L1_gnn_b_out"].reshape(F, 1)),
    }


def kernel(**inputs):
    import concourse.bacc as _bacc
    from concourse.bass_utils import run_bass_kernel_spmd as _run

    nc = _bacc.Bacc("TRN2", target_bir_lowering=False, num_devices=1)
    arrays = _layout(inputs)
    args = {k: nc.dram_tensor(f"in_{k}", v.shape, mybir.dt.from_np(v.dtype), kind="ExternalInput").ap() for k, v in arrays.items()}
    out = nc.dram_tensor("out", (B, N, F), FP32, kind="ExternalOutput").ap()
    residual_graph_layers(nc, args, out)
    r = _run(nc, [{f"in_{k}": v for k, v in arrays.items()}], core_ids=[0])
    return r.results[0]["out"]
```

```python
from contextlib import ExitStack

import concourse.bass as bass
from concourse import mybir

FP32, FP16, BF16, I32 = mybir.dt.float32, mybir.dt.float16, mybir.dt.bfloat16, mybir.dt.int32
ALU, ACT, AX = mybir.AluOpType, mybir.ActivationFunctionType, mybir.AxisListType
RMAX = bass.bass_isa.ReduceOp.max

P = 128
B = 8
N = 1024
F = 64
T = N // P
BP = B // 2
BF = B * F
E = 64
HEADS = 8
HID = 128
HALF = 512
WCOL = 2 * P + 2
MASKED = -1e30
XS = 64.0
PSC = 16384.0
GTOP = 4.0
HTOP = 30000.0
EPS = 1e-5
FAST_SLOTS = 10


def residual_graph_layers(nc, a, out):
    ctx = ExitStack()
    with ctx:
        sems = {}

        def s(name):
            if name not in sems:
                sems[name] = ctx.enter_context(nc.semaphore(name))
            return sems[name]

        def sb(name, shape, dt=FP32, c=ctx):
            return c.enter_context(nc.sbuf_tensor(name, shape, dt))

        ident = sb("ident", [P, P])
        ident16 = sb("ident16", [P, P], FP16)
        x1 = sb("x1", [P, B, T, F])
        adj_mask = sb("adj_mask", [P, T, N], BF16)
        g_hi = sb("g_hi", [P, HEADS, P], FP16)
        g_lo = sb("g_lo", [P, HEADS, P], FP16)
        fold16 = sb("fold16", [P, P], FP16)
        fold = sb("fold", [P, P])
        h_unit = sb("h_unit", [P, 1])
        h_inv = sb("h_inv", [P, 1])
        h_scale = sb("h_scale", [P, 1])
        z_scale = sb("z_scale", [P, 1])
        g_scale = sb("g_scale", [P, HEADS])
        w_out = sb("w_out", [P, HEADS, P])
        bh = sb("bh", [P, HEADS])
        b_out = sb("b_out", [P, 1])
        ln_mean = sb("ln_mean", [P, T * B])
        ln_var = sb("ln_var", [P, T * B])

        L0 = ExitStack()
        x_nat = sb("x_nat", [P, T, B, F], c=L0)
        proj = sb("proj", [P, T, BP, WCOL], c=L0)
        adjT = sb("adjT", [P, T, N], c=L0)
        x_t = sb("x_t", [P, BP, N], c=L0)
        industry = x_t[:].rearrange("p a (t q) -> p (a t) q", t=2)
        g_less_ind = adjT[:, T // 2:T, :].rearrange("p a (t q) -> p (a t) q", t=2)
        g_sum = adjT[:, 0:T // 2, :].rearrange("p a (t q) -> p (a t) q", t=2)
        tmp_a = sb("tmp_a", [P, 2, N], c=L0)
        tmp_b = sb("tmp_b", [P, 2, N], c=L0)
        tmp_c = sb("tmp_c", [P, 2, N], c=L0)
        tmp_d = sb("tmp_d", [P, 2, N], c=L0)
        tri = sb("tri", [P, E], c=L0)
        slot_no = sb("slot_no", [P, E], c=L0)
        w_t = sb("w_t", [F, F], c=L0)
        w_cols = sb("w_cols", [F, 2], c=L0)
        w_block = sb("w_block", [P, WCOL], c=L0)
        node_block = sb("node_block", [P, P], c=L0)
        w_all = sb("w_all", [P, HEADS, P], c=L0)
        a_ge = sb("a_ge", [F, 1], c=L0)
        fc_w = sb("fc_w", [P, P], c=L0)
        fc_b = sb("fc_b", [P, 1], c=L0)
        av = sb("av", [P, 1], c=L0)
        av_all = sb("av_all", [P, P], c=L0)
        ones = sb("ones", [P, P], c=L0)
        g_abs = sb("g_abs", [P, HEADS], c=L0)
        w_norm = sb("w_norm", [P, HEADS], c=L0)
        b_abs = sb("b_abs", [P, HEADS], c=L0)
        h_top = sb("h_top", [P, F], c=L0)
        g_max = sb("g_max", [P, HEADS], c=L0)
        g_inv = sb("g_inv", [P, HEADS], c=L0)
        mask_t = sb("mask_t", [P, N], c=L0)
        edge_bias = sb("edge_bias", [P, N], BF16, c=L0)
        rank = sb("rank", [E, N], c=L0)
        mask_n = sb("mask_n", [P, T, E], c=L0)
        node_cnt = sb("node_cnt", [P, T], c=L0)
        node_empty = sb("node_empty", [P, T], c=L0)
        edge_max = sb("edge_max", [P, BP], c=L0)
        edge_sum = sb("edge_sum", [P, BP], c=L0)
        edge_inv = sb("edge_inv", [P, BP], c=L0)
        agg = sb("agg", [E, B, F], c=L0)
        agg_t = sb("agg_t", [F, BF], c=L0)
        he_r = sb("he_r", [F, BF], c=L0)
        he_e = sb("he_e", [F, BF], c=L0)
        extra = sb("extra", [E, 17], c=L0)
        se_max = sb("se_max", [P, T, B], c=L0)
        bl = sb("bl", [P, T, B], c=L0)
        th = sb("th", [P, T, B], c=L0)
        wgt = sb("wgt", [P, 2, T, B], c=L0)
        sx = sb("sx", [P, T, B], c=L0)
        vb = sb("vb", [P, T], c=L0)
        coef = sb("coef", [P, 2, T, B], c=L0)
        coef_sum = sb("coef_sum", [P, T, B], c=L0)
        sel = (mask_t[0:E, :], adjT[0:E, T - 1, :])
        max_all = sb("max_all", [P, 1], c=L0)
        max_one = sb("max_one", [P, 1], c=L0)
        max_count = sb("max_count", [1, 1], I32, c=L0)
        deg = sb("deg", [P, T], c=L0)
        av_row = sb("av_row", [P, 2, 31], c=L0)
        L0.close()

        ax = sb("ax", [P, B, N], FP16)
        x2 = sb("x2", [P, B, T, P], FP16)
        y_hi = sb("y_hi", [P, 2, N], FP16)
        y_lo = sb("y_lo", [P, 2, N], FP16)
        masked = sb("masked", [P, 2, N])
        probs = sb("probs", [P, 2, N])
        pt_hi = sb("pt_hi", [P, 2, T, HALF], FP16)
        pt_lo = sb("pt_lo", [P, 2, T, HALF], FP16)
        neg_max = sb("neg_max", [P, 2])
        sums = sb("sums", [P, T])
        rinv = sb("rinv", [P, T])
        cur_scale = sb("cur_scale", [P, 1])
        osum = sb("osum", [P, 2, HALF])
        onorm = sb("onorm", [P, HALF])
        w2 = sb("w2", [P, P])
        zc = sb("zc", [P, 2, HALF])
        zm = sb("zm", [P, 2, HALF])
        cat = sb("cat", [P, HEADS, N])

        squares = [w[:].rearrange("p a n -> p (a n)").rearrange("p (b t f) -> p b t f", b=B // 2, f=F) for w in (masked, probs)]
        ps = ctx.enter_context(nc.psum_tensor("ps", [P, 8, HALF], FP32))

        def pair_in(q):
            return (tmp_a if q in (2, 3) else tmp_d)[:, q % 2, :]

        def half_batches(w, half):
            return w.rearrange("p t (b f) -> p t b f", b=B)[:, :, 4 * half:4 * half + 4, :]

        def h_of(t):
            return proj[:, t, :, 0:P]

        def by_batches(w, half):
            return w[:].rearrange("p (t b) -> p t b", b=B)[:, :, 4 * half:4 * half + 4]

        def layer_norm_act(act, tag, sq_out, centred):
            for half in range(2):
                act.wait_ge(s(tag + "centred"), half + 1)
                act.activation(sq_out[half], centred[half], ACT.Square).then_inc(s(tag + "square"), 1)
            act.wait_ge(s(tag + "var"), 2)
            act.activation(ln_var[:], ln_var[:], ACT.Sqrt).then_inc(s(tag + "sqrt"), 1)

        def pair_scores(pe, j):
            src, row = j // 16, j % 16
            pe.wait_ge(s("pair_tanh"), j + 1)
            nc.tensor.matmul(ps[0:16, 7, :], av_row[:, src, 15 - row:31 - row], tmp_c[:, j % 2, 0:HALF],
                             start=(j == 0), stop=(j == 31), skip_group_check=True).then_inc(s("pair_score"), 1)

        chained = [0]

        def link(ins):
            chained[0] += 1
            ins.then_inc(s("dve_chain"), 1)
            nc.vector.wait_ge(s("dve_chain"), chained[0])

        def centre(tag, xs, mean):
            v = nc.vector
            link(v.tensor_reduce(mean, xs, axis=AX.X, op=ALU.add))
            link(v.tensor_scalar(mean, mean, 1.0 / F, None, ALU.mult))
            v.tensor_tensor(xs, xs, mean.unsqueeze(3).to_broadcast([P, xs.shape[1], xs.shape[2], F]), ALU.subtract).then_inc(s(tag + "centred"), 1)

        def variance(dve, tag, half, sq, var):
            v = nc.vector
            dve.wait_ge(s(tag + "square"), half + 1)
            link(v.tensor_reduce(var, sq, axis=AX.X, op=ALU.add))
            v.tensor_scalar(var, var, 1.0 / F, EPS, ALU.mult, ALU.add).then_inc(s(tag + "var"), 1)

        def deviation(dve, tag):
            dve.wait_ge(s(tag + "sqrt"), 1)
            link(nc.vector.reciprocal(ln_var[:], ln_var[:]))

        block = ctx.enter_context(nc.Block())

        @block.sync
        def _(sp):
            sp.dma_start(ident[:], a["consts"][:, 0:P]).then_inc(s("consts_in"), 16)
            sp.dma_start(tri[:], a["consts"][:, P:P + E]).then_inc(s("consts_in"), 16)
            sp.dma_start(slot_no[:], a["consts"][:, P + E:P + 2 * E]).then_inc(s("consts_in"), 16)
            for b in range(B):
                sp.dma_start(x_nat[:, :, b, :], a["x"][b].rearrange("(t p) f -> p t f", p=P)).then_inc(s("x_in"), 16)
            for half in range(2):
                sp.dma_start(mask_t[half * E:half * E + E, :], a["HT"]).then_inc(s("ht_in"), 16)
            sp.dma_start(mask_n[:], a["H"].rearrange("(t p) e -> p t e", p=P)).then_inc(s("hn_in"), 16)
            for t in range(T):
                if t >= 2:
                    sp.wait_ge(s("mask_made"), t - 1)
                    sp.wait_ge(s("deg_sum"), t - 1)
                sp.dma_start(tmp_d[:, t % 2, :], a["adj"][t * P:t * P + P, :]).then_inc(s(f"adj_in{t % 2}"), 16)
            sp.wait_ge(s("x1_ready"), 2)
            for half in range(2):
                sp.dma_start(w2[half * F:half * F + F, :], a["Wh"][0]).then_inc(s("w2_in"), 16)
            with sp.Fori(1, B * HEADS) as head:
                sp.wait_ge(s("projected"), 2 * head + 1)
                for half in range(2):
                    sp.dma_start(w2[half * F:half * F + F, :], a["Wh"][bass.ds(head % HEADS, 1)].rearrange("a f d -> (a f) d")).then_inc(s("w2_in"), 16)
            for q in range(4):
                sp.wait_ge(s("ln1_out"), q + 1)
                sp.dma_start(out[2 * q:2 * q + 2].rearrange("b (t p) f -> p b t f", p=P), x1[:, 2 * q:2 * q + 2]).then_inc(s("out_stored"), 16)
            sp.wait_ge(s("out_stored"), 64)

        @block.scalar
        def _(act):
            act.dma_start(w_t[:], a["WT"]).then_inc(s("w_in"), 16)
            act.dma_start(w_cols[:, 0:1], a["a_node"]).then_inc(s("w_in"), 16)
            act.dma_start(w_cols[:, 1:2], a["a_gn"]).then_inc(s("w_in"), 16)
            act.wait_ge(s("w_block_zero"), 1)
            for half in range(2):
                r = slice(half * F, half * F + F)
                act.dma_start(w_block[r, half * F:half * F + F], a["W"]).then_inc(s("wb_in"), 16)
                act.dma_start(w_block[r, P + half * F:P + half * F + F], a["W_ind"]).then_inc(s("wb_in"), 16)
                act.dma_start(fc_w[r, :], a["fcW"]).then_inc(s("fc_in"), 16)
                act.dma_start(w_all[:, :, r], a["WhT"].rearrange("h d f -> d h f")).then_inc(s("wh_in"), 16)
                act.dma_start(w_out[:, :, r], a["W_out"].rearrange("(h d) f -> d h f", d=HID)).then_inc(s("wo_in"), 16)
            act.dma_start(fc_b[:], a["fcb"]).then_inc(s("fc_in"), 16)
            act.dma_start(av[:], a["av"]).then_inc(s("fc_in"), 16)
            act.dma_start(a_ge[:], a["a_ge"]).then_inc(s("fc_in"), 16)
            act.dma_start(bh[:], a["bhT"]).then_inc(s("wo_in"), 16)
            for half in range(2):
                act.dma_start(b_out[half * F:half * F + F, :], a["b_out"]).then_inc(s("wo_in"), 16)
            for t in range(T):
                act.dma_start(adjT[:, t, :], a["adjT"][t * P:t * P + P, :]).then_inc(s("adjT_in"), 16)
            for q in range(1, 2 * BP, 2):
                act.wait_ge(s("xt_made"), q + 1)
                act.activation(x_t[:, q // 2, HALF:N], ps[:, q % 4, :], ACT.Copy).then_inc(s("xt_out1"), 1)
            def degree(t):
                act.wait_ge(s(f"adj_in{t % 2}"), 16 * (t // 2 + 1))
                if t:
                    act.wait_ge(s("deg_sum"), t)
                act.activation(tmp_b[:, 1, :], tmp_d[:, t % 2, :], ACT.Copy, accum_out=deg[:, t:t + 1]).then_inc(s("deg_sum"), 1)

            for i in range(1, T * BP, 2):
                if i in (1, 5):
                    degree(i // 4)
                act.wait_ge(s("proj_made"), i + 1)
                act.activation(proj[:, i // BP, i % BP, :], ps[:, i % 4, 0:WCOL], ACT.Copy).then_inc(s("proj_out1"), 1)
            act.wait_ge(s("wh_in"), 32)
            for h in range(HEADS):
                if h:
                    act.wait_ge(s("w_square"), h)
                act.activation(tmp_b[:, 0, 0:F], w_all[:, h, 0:F], ACT.Square, accum_out=w_norm[:, h:h + 1]).then_inc(s("w_square"), 1)
            act.wait_ge(s("w_square"), HEADS)
            act.activation(w_norm[:], w_norm[:], ACT.Sqrt).then_inc(s("w_norm"), 1)
            for t in range(2, T):
                degree(t)
            for bp in range(BP):
                act.wait_ge(s("edge_masked"), bp + 1)
                if bp:
                    act.wait_ge(s("edge_tr"), bp)
                act.activation(tmp_b[:, 0, :], tmp_a[:, 0, :], ACT.Exp, scale=-1.0, bias=edge_max[:, bp:bp + 1],
                               accum_out=edge_sum[:, bp:bp + 1]).then_inc(s("edge_exp"), 1)
                act.wait_ge(s("edge_tr"), bp + 1)
                if bp:
                    act.wait_ge(s("agg_made"), bp)
                act.activation(tmp_c[:, 0, :], ps[:, 6:8, :], ACT.Copy).then_inc(s("edge_tr_out"), 1)
            act.wait_ge(s("aggt_out"), 1)
            act.activation(he_r[:], agg_t[:], ACT.Relu).then_inc(s("he_re"), 1)
            act.activation(he_e[:], agg_t[:], ACT.Exp).then_inc(s("he_re"), 1)
            act.wait_ge(s("he_hid"), 1)
            act.wait_ge(s("fc_in"), 80)
            act.wait_ge(s("deg_sum"), T)
            act.activation(tmp_b[:, 1, 0:BF], ps[:, 5, :], ACT.Tanh, bias=fc_b[:]).then_inc(s("he_tanh"), 1)

            def pair(js):
                for j in js:
                    act.wait_ge(s("pair_hid"), j + 1)
                    if j >= 2:
                        act.wait_ge(s("pair_score"), j - 1)
                    act.activation(tmp_c[:, j % 2, 0:HALF], ps[:, 4 + j % 2, :], ACT.Tanh, bias=fc_b[:]).then_inc(s("pair_tanh"), 1)

            pair(range(8))

            def slots(tag, start, end):
                act.sem_inc(s(tag + "exp"), 2)
                act.sem_inc(s(tag + "th"), 1)
                act.sem_inc(s(tag + "coef"), 1)

                def weights(m, u):
                    act.wait_ge(s(tag + "bl"), m + 1)
                    act.wait_ge(s(tag + "wgt"), m + 1)
                    act.activation(th[:], bl[:], ACT.Tanh, scale=0.5).then_inc(s(tag + "th"), 1)
                    act.wait_ge(s(tag + "sx"), m + 1)
                    act.wait_ge(s(tag + "vc"), 4 * m + 1)
                    act.activation(coef[:, u], sx[:], ACT.Exp).then_inc(s(tag + "coef"), 1)

                def relu_exp(m, c):
                    act.wait_ge(s(tag + "z"), 4 * m + c + 1)
                    act.wait_ge(s(tag + "v"), 4 * m + c + 1)
                    act.activation(tmp_b[:, c % 2, :], tmp_a[:, c % 2, :], ACT.Relu).then_inc(s(tag + "relu"), 1)
                    act.activation(tmp_c[:, c % 2, :], tmp_a[:, c % 2, :], ACT.Exp).then_inc(s(tag + "exp"), 1)

                def prologue():
                    weights(0, 0)
                    relu_exp(0, 0)

                def slot(m, u, last=False):
                    relu_exp(m, 1)
                    relu_exp(m, 2)
                    if not last:
                        weights(m + 1, 1 - u)
                    relu_exp(m, 3)
                    if not last:
                        relu_exp(m + 1, 0)

                prologue()
                with act.Fori(0, (end - start) // 2 - 1) as pair:
                    for u in range(2):
                        slot(pair * 2 + u, u)
                for u in range(2):
                    slot(end - start - 2 + u, u, last=(u == 1))

            def rest(start, end):
                act.wait_ge(s("max_count"), 1)
                many = act.value_load(max_count[0:1, 0:1], min_val=0, max_val=E)
                with act.If(many > start):
                    act.wait_ge(s("f_g"), 4 * start + 2)
                    act.wait_ge(s("f_csum"), start + 1)
                    slots("s_", start, end)
                    act.wait_ge(s("s_g"), 4 * (end - start) + 2)
                    act.wait_ge(s("s_csum"), end - start + 1)

            slots("f_", 0, FAST_SLOTS)
            rest(FAST_SLOTS, E)

            pair(range(8, 32))
            act.wait_ge(s("pair_score"), 32)
            act.activation(tmp_b[0:16, 0, 0:HALF], ps[0:16, 7, :], ACT.Tanh, scale=0.5).then_inc(s("pair_th"), 1)
            layer_norm_act(act, "ln0_", [half_batches(g_sum, half) for half in range(2)], [half_batches(industry, half) for half in range(2)])

            def at(w, i, *rest):
                return w[(slice(None), i) + rest] if isinstance(i, int) else w[(slice(None), bass.ds(i, 1)) + rest].squeeze(1)

            def exp(v, t):
                act.wait_ge(s("masked"), 8 * v + t + 2)
                if t % 4 == 0:
                    act.wait_ge(s("rinv"), 2 * v + t // 4 + 1)
                act.wait_ge(s("pT"), 8 * v + t + 1)
                act.activation(probs[:, t % 2, :], masked[:, t % 2, :], ACT.Exp, scale=-1.0, bias=neg_max[:, t % 2:t % 2 + 1],
                               accum_out=sums[:, t:t + 1]).then_inc(s("probs"), 1)

            def hi(v, t):
                if t % 4 == 0:
                    act.wait_ge(s("pv"), 4 * (2 * v + t // 4) + 4)
                act.wait_ge(s("pT"), 8 * v + t + 3)
                act.activation(pt_hi[:, t // 4, :, t % 4 * P:t % 4 * P + P],
                               ps[:, 2 + 2 * (t % 2):4 + 2 * (t % 2), :].rearrange("p a (m n) -> p (a m) n", n=P), ACT.Copy, scale=PSC).then_inc(s("hi"), 1)

            def take_sum(v, cc):
                act.wait_ge(s("pv"), 4 * (2 * v + cc) + 12)
                act.wait_ge(s("normed"), 2 * v + cc + 1)
                act.activation(osum[:, cc, :], ps[:, 6, :], ACT.Copy).then_inc(s("osum"), 1)

            def take_proj(v, cc, out_unit):
                act.wait_ge(s("projected"), 2 * v + cc + 2)
                act.wait_ge(s("cat"), 2 * v + cc + 1)
                act.nop(nofuse=True)
                if out_unit:
                    act.activation(zc[:, cc, :], ps[:, 7, :], ACT.Identity, scale=z_scale[:], bias=b_out[:]).then_inc(s("z"), 1)
                else:
                    act.activation(zc[:, cc, :], ps[:, 7, :], ACT.Identity, scale=1.0 / (XS * PSC), bias=bh[:, bass.ds(v % HEADS, 1)]).then_inc(s("z"), 1)

            def take_y(v, cc):
                act.wait_ge(s("y"), 2 * v + cc + 1)
                if not isinstance(v, int) or v >= 2:
                    act.wait_ge(s("scores"), 8 * (v - 1) + 1)
                act.nop(nofuse=True)
                act.activation(at(y_hi, v % 2, slice(cc * HALF, cc * HALF + HALF)), ps[:, 7, :], ACT.Copy).then_inc(s("y_hi"), 1)

            def take_h(q, cc):
                act.wait_ge(s("h_made"), 2 * q + cc + 3)
                act.nop(nofuse=True)
                act.activation(at(ax, q, slice(cc * HALF, cc * HALF + HALF)), ps[:, 7, :], ACT.Copy, scale=h_inv[:]).then_inc(s("h_hi"), 1)

            def take_back(b):
                act.wait_ge(s("h_t"), b + 1)
                act.activation(x2[:, b], ps[:, 7, :].bitcast(FP16), ACT.Copy).then_inc(s("h_x2"), 1)

            def unit(v, first=False, last=False, out_unit=False, h_batch=None, late=False, prev_out=None, next_out=None, back=()):
                prev_out = out_unit if prev_out is None else prev_out
                for t in range(T):
                    for t_back, b in back:
                        if t == t_back + 1:
                            take_back(b)
                    if t == 0 and late:
                        take_proj(v - 2, 1, out_unit)
                    if t == (1 if late else 0) and not first:
                        take_y(v, 1)
                    if t == 0 and not first:
                        take_sum(v - 1, 0)
                    if t == 3 and not first:
                        take_proj(v - 1, 0, prev_out)
                    if t == 4:
                        if not last:
                            take_y(v + 1, 0)
                        if not first:
                            take_sum(v - 1, 1)
                    if t in (5, 6) and h_batch is not None:
                        take_h(h_batch, t - 5)
                    if t == 7 and not first and h_batch is None:
                        take_proj(v - 1, 1, prev_out)
                    if t < 7:
                        exp(v, t + 1)
                    elif not last:
                        exp(v + 1, 0)
                    hi(v, t)

            def drain(v, out_unit):
                take_sum(v, 0)
                take_proj(v, 0, out_unit)
                take_sum(v, 1)
                take_proj(v, 1, out_unit)

            act.wait_ge(s("x1_ready"), 2)
            act.sem_inc(s("probs"), 2)
            act.sem_inc(s("osum"), 1)
            def take_x_t(b):
                act.wait_ge(s("xt16"), b + 1)
                act.activation(ax[:, b, :], ps[:, 4 + b % 2, :].bitcast(FP16), ACT.Copy).then_inc(s("ax"), 1)

            take_x_t(0)
            take_y(0, 0)
            take_x_t(1)
            take_y(0, 1)
            take_x_t(2)
            take_x_t(3)
            exp(0, 0)
            for b in range(4, B):
                take_x_t(b)
            unit(0, first=True)
            with act.Fori(1, HEADS + 1) as v:
                unit(v)
            with act.Fori(1, B - 1) as q:
                unit(q * HEADS + 1, h_batch=q - 1)
                unit(q * HEADS + 2, late=True)
                with act.Fori(3, HEADS + 1) as j:
                    unit(q * HEADS + j)
            unit((B - 1) * HEADS + 1, h_batch=B - 2)
            unit((B - 1) * HEADS + 2, late=True)
            with act.Fori((B - 1) * HEADS + 3, B * HEADS - 1) as v:
                unit(v)
            v0 = B * HEADS
            unit(v0 - 1, next_out=True, back=((0, 0), (4, 1)))
            unit(v0, out_unit=True, prev_out=False, back=((0, 2), (4, 3)))
            unit(v0 + 1, out_unit=True, h_batch=B - 1, back=((0, 4),))
            unit(v0 + 2, out_unit=True, late=True, back=((4, 5),))
            unit(v0 + 3, out_unit=True, back=((0, 6), (4, 7)))
            with act.Fori(v0 + 4, v0 + B - 1) as v:
                unit(v, out_unit=True)
            unit(v0 + B - 1, last=True, out_unit=True)
            drain(v0 + B - 1, True)
            act.wait_ge(s("probs"), 8 * (v0 + B) + 2)
            act.wait_ge(s("pT"), 8 * (v0 + B) + 2)
            for half in range(2):
                act.wait_ge(s("ln1_centred"), half + 1)
                act.activation(squares[half], x1[:, 4 * half:4 * half + 4], ACT.Square).then_inc(s("ln1_square"), 1)
                act.wait_ge(s("ln1_var"), half + 1)
                var = ln_var[:, 4 * T * half:4 * T * half + 4 * T]
                act.activation(var, var, ACT.Sqrt).then_inc(s("ln1_sqrt"), 1)

        @block.tensor
        def _(pe):
            pe.wait_ge(s("w_in"), 48)
            pe.wait_ge(s("consts_in"), 48)
            nc.tensor.matmul(ps[0:F, 4, 0:2], w_t[:], w_cols[:], start=True, stop=True)
            nc.tensor.matmul(ps[F:P, 4, 0:2], w_t[:], w_cols[:], start=True, stop=True).then_inc(s("wa_made"), 1)
            pe.wait_ge(s("x_in"), 16 * B)
            pe.wait_ge(s("ones_made"), 1)
            for q in range(2 * BP):
                if q >= 4:
                    pe.wait_ge(s(f"xt_out{q % 2}"), (q - 4) // 2 + 1)
                for i in range(4):
                    t = (q % 2) * 4 + i
                    last = nc.tensor.transpose(ps[:, q % 4, i * P:i * P + P],
                                               x_nat[:, t, q // 2 * 2:q // 2 * 2 + 2, :].rearrange("p b f -> p (b f)"), ident[:])
                last.then_inc(s("xt_made"), 1)
            pe.wait_ge(s("xt_out0"), BP)
            pe.wait_ge(s("xt_out1"), BP)
            pe.wait_ge(s("w_ready"), 1)
            for i in range(T * BP):
                if i >= 4:
                    pe.wait_ge(s(f"proj_out{i % 2}"), (i - 4) // 2 + 1)
                nc.tensor.matmul(ps[:, i % 4, 0:WCOL], x_t[:, i % BP, i // BP * P:i // BP * P + P], w_block[:],
                                 start=True, stop=True).then_inc(s("proj_made"), 1)
            pe.wait_ge(s("mask_t_made"), 1)
            pe.wait_ge(s("ones_made"), 1)
            for c in range(2):
                last = nc.tensor.matmul(ps[0:E, 6 + c, :], ones[0:E, 0:E], mask_t[0:E, c * HALF:c * HALF + HALF], start=True, stop=True)
            last.then_inc(s("cnt_made"), 1)
            pe.wait_ge(s("eff_made"), 1)
            for c in range(2):
                last = nc.tensor.matmul(ps[0:E, 6 + c, :], tri[0:E, :], tmp_a[0:E, 1, c * HALF:c * HALF + HALF], start=True, stop=True)
            last.then_inc(s("rank_made"), 1)
            pe.wait_ge(s("rank_out"), 1)
            pe.wait_ge(s("proj_out0"), T * BP // 2)
            pe.wait_ge(s("proj_out1"), T * BP // 2)
            pe.wait_ge(s("wh_in"), 32)
            for h in range(HEADS):
                last = nc.tensor.matmul(ps[:, 1, h * F:h * F + F], w_all[:, h, :], w_all[:, h, 0:F], start=True, stop=True)
            last.then_inc(s("g_made"), 1)

            def industry_sum(t):
                if t >= 2:
                    pe.wait_ge(s("ind_out"), t - 1)
                for m in range(T):
                    last = nc.tensor.matmul(ps[:, 2 + t % 2, :], adjT[:, m, t * P:t * P + P], proj[:, m, :, P:2 * P], start=(m == 0), stop=(m == T - 1))
                last.then_inc(s("ind_made"), 1)

            for bp in range(BP):
                if bp:
                    pe.wait_ge(s("edge_lk"), bp)
                for c in range(2):
                    last = nc.tensor.matmul(ps[:, 4 + c, :], node_block[:], x_t[:, bp, c * HALF:c * HALF + HALF], start=True, stop=True)
                last.then_inc(s("edge_s"), 1)
                if bp == 0:
                    pe.wait_ge(s("adjT_in"), 16 * T)
                industry_sum(2 * bp)
                pe.wait_ge(s("edge_exp"), bp + 1)
                if bp:
                    pe.wait_ge(s("edge_tr_out"), bp)
                for t in range(T):
                    last = nc.tensor.transpose(ps[:, 6 + t // 4, t % 4 * P:t % 4 * P + P], tmp_b[:, 0, t * P:t * P + P], ident[:])
                last.then_inc(s("edge_tr"), 1)
                industry_sum(2 * bp + 1)
                if bp == 0:
                    pe.wait_ge(s("w_abs"), 1)
                    pe.wait_ge(s("g_out"), 2)
                    nc.tensor.matmul(ps[:, 1, :], ones[:], tmp_c[:, 1, 0:HALF], start=True, stop=True).then_inc(s("h_bound"), 1)
                pe.wait_ge(s("edge_tr_out"), bp + 1)
                if bp:
                    pe.wait_ge(s("agg_out"), 2 * bp)
                for t in range(T):
                    last = nc.tensor.matmul(ps[:, 0, bp * P:bp * P + P], tmp_c[:, 0, t * P:t * P + P], proj[:, t, bp, 0:P], start=(t == 0), stop=(t == T - 1))
                last.then_inc(s("agg_made"), 1)
            pe.wait_ge(s("agg_out"), 2 * BP)
            for b in range(B):
                last = nc.tensor.transpose(ps[0:F, 4, b * E:b * E + E], agg[:, b, :], ident[0:E, 0:E])
            last.then_inc(s("aggt_made"), 1)
            pe.wait_ge(s("he_made"), 1)
            pe.wait_ge(s("fc_in"), 80)
            nc.tensor.matmul(ps[:, 5, :], fc_w[0:F, :], he_r[:], start=True, stop=True).then_inc(s("he_hid"), 1)
            pe.wait_ge(s("he_tanh"), 1)
            for b in range(B):
                nc.tensor.matmul(ps[0:E, 7, b:b + 1], agg_t[:, b * E:b * E + E], a_ge[:], start=True, stop=True)
                nc.tensor.matmul(ps[0:E, 7, 8 + b:9 + b], tmp_b[:, 1, b * E:b * E + E], av[:], start=True, stop=True)
            pe.wait_ge(s("av_all_made"), 1)
            nc.tensor.matmul(ps[:, 6, :], av_all[:], tmp_b[:, 1, 0:BF], start=True, stop=True).then_inc(s("se_made"), 1)
            pe.wait_ge(s("av_row"), 2)
            pe.wait_ge(s("extra_out"), 1)
            pe.wait_ge(s("ind_out"), T)

            def pair(q):
                src = (industry, g_sum)[q // 4]
                bp = q % 4
                if q >= 2:
                    pe.wait_ge(s("pair_t_out"), q - 1)
                for t in range(T):
                    last = nc.tensor.transpose(ps[:, 2 * (q % 2) + t // 4, t % 4 * P:t % 4 * P + P], src[:, t, bp * P:bp * P + P], ident[:])
                last.then_inc(s("pair_t"), 1)
                if q not in (0, 2, 4):
                    pair_scores(pe, 4 * q - 1)
                pe.wait_ge(s("pair_t_out"), q + 1)
                for i in range(4):
                    j = 4 * q + i
                    if j >= 2:
                        pe.wait_ge(s("pair_tanh"), j - 1)
                    r = slice(i // 2 * F, i // 2 * F + F)
                    c = i % 2
                    nc.tensor.matmul(ps[:, 4 + j % 2, :], fc_w[r, :], pair_in(q)[r, c * HALF:c * HALF + HALF], start=True, stop=True).then_inc(s("pair_hid"), 1)
                    if i:
                        pair_scores(pe, j - 1)

            for q in range(2):
                pair(q)
            pair_scores(pe, 7)
            pe.wait_ge(s("pair_t_out"), 2)
            pe.wait_ge(s("pair_tanh"), 8)
            pe.wait_ge(s("neg_ident"), 1)

            def slots(tag, start, end):
                pe.sem_inc(s(tag + "diff"), 1)

                def scores(m, u):
                    pe.wait_ge(s(tag + "sel"), m + 1)
                    pe.wait_ge(s(tag + "th"), m + 1)
                    pe.wait_ge(s(tag + "extra_read"), 2 * m + 1)
                    for t in range(T):
                        last = nc.tensor.matmul(ps[:, 4, t * 17:t * 17 + 17], sel[u][:, t * P:t * P + P], extra[:], start=True, stop=True)
                    last.then_inc(s(tag + "extra"), 1)

                def diff(m, u, c):
                    pe.wait_ge(s(tag + "zw"), 4 * m + c + 1)
                    for i in range(2):
                        t = 2 * c + i
                        nc.tensor.matmul(ps[:, 2 * (c % 2) + i, :], sel[u][:, t * P:t * P + P], agg[:].rearrange("e b f -> e (b f)"), start=True, stop=False)
                        last = nc.tensor.matmul(ps[:, 2 * (c % 2) + i, :], av_all[:], h_of(t), start=False, stop=True)
                    last.then_inc(s(tag + "diff"), 1)

                def prologue():
                    scores(0, 0)
                    diff(0, 0, 0)

                def slot(m, u, last=False):
                    diff(m, u, 1)
                    diff(m, u, 2)
                    if not last:
                        scores(m + 1, 1 - u)
                    diff(m, u, 3)
                    if not last:
                        diff(m + 1, 1 - u, 0)

                prologue()
                with pe.Fori(0, (end - start) // 2 - 1) as pair:
                    for u in range(2):
                        slot(pair * 2 + u, u)
                for u in range(2):
                    slot(end - start - 2 + u, u, last=(u == 1))

            def rest(start, end):
                pe.wait_ge(s("max_count"), 1)
                many = pe.value_load(max_count[0:1, 0:1], min_val=0, max_val=E)
                with pe.If(many > start):
                    pe.wait_ge(s("f_g"), 4 * start + 2)
                    pe.wait_ge(s("f_csum"), start + 1)
                    slots("s_", start, end)
                    pe.wait_ge(s("s_g"), 4 * (end - start) + 2)
                    pe.wait_ge(s("s_csum"), end - start + 1)

            slots("f_", 0, FAST_SLOTS)
            rest(FAST_SLOTS, E)

            pe.wait_ge(s("f_zw"), 4 * FAST_SLOTS + 2)
            pe.wait_ge(s("f_extra_read"), 2 * FAST_SLOTS + 1)
            pe.wait_ge(s("f_th"), FAST_SLOTS + 1)
            for q in range(2, 4):
                pair(q)
            pair_scores(pe, 15)
            for q in range(4, 8):
                pe.wait_ge(s("g_final"), q - 3)
                pair(q)
            pair_scores(pe, 31)
            pe.wait_ge(s("pair_wgt"), 1)
            for i in range(4):
                last = nc.tensor.transpose(ps[:, 6, i * 16:i * 16 + 16], tmp_b[0:16, 1, i * P:i * P + P], ident[0:16, 0:16])
            last.then_inc(s("pair_wgt_t"), 1)

            def at(w, i, *rest):
                return w[(slice(None), i) + rest] if isinstance(i, int) else w[(slice(None), bass.ds(i, 1)) + rest].squeeze(1)

            def batch_of(v, out_unit):
                return v - B * HEADS if out_unit else v // HEADS

            def scores(v, t, out_unit):
                pe.wait_ge(s("masked"), 8 * v + t + 1)
                if t % 4 == 0:
                    pe.wait_ge(s("y_out"), 2 * v + t // 4 + 1)
                for part, y in enumerate((y_hi, y_lo)):
                    for c in range(2):
                        last = nc.tensor.matmul(ps[:, c, :], at(y, v % 2, slice(t * P, t * P + P)),
                                                at(ax, batch_of(v, out_unit), slice(c * HALF, c * HALF + HALF)),
                                                start=(part == 0), stop=(part == 1), skip_group_check=True)
                last.then_inc(s("scores"), 1)

            def transpose(v, t):
                pe.wait_ge(s("probs"), 8 * v + t + 3)
                pe.wait_ge(s("lo"), 8 * v + t + 1)
                for m in range(T):
                    last = nc.tensor.transpose(ps[:, 2 + 2 * (t % 2) + m // 4, m % 4 * P:m % 4 * P + P], probs[:, t % 2, m * P:m * P + P], ident[:])
                last.then_inc(s("pT"), 1)

            def weigh(v, cc, part, out_unit):
                if part == 0:
                    pe.wait_ge(s("hi"), 4 * (2 * v + cc) + 4)
                    pe.wait_ge(s("osum"), 2 * v + cc + 1)
                for m in (2 * part, 2 * part + 1):
                    nc.tensor.matmul(ps[:, 6, :], at(x2, batch_of(v, out_unit), m, slice(0, P)), pt_hi[:, cc, m, :], start=(m == 0), stop=False)
                if part == 0:
                    pe.wait_ge(s("lo"), 4 * (2 * v + cc) + 6)
                for m in (2 * part, 2 * part + 1):
                    last = nc.tensor.matmul(ps[:, 6, :], at(x2, batch_of(v, out_unit), m, slice(0, P)), pt_lo[:, cc, m, :], start=False, stop=(m == T - 1))
                last.then_inc(s("pv"), 1)

            def repeat_inverse(v, cc):
                pe.wait_ge(s("rinv"), 2 * v + cc + 3)
                for i in range(4):
                    last = nc.tensor.transpose(ps[:, 7, i * P:i * P + P], rinv[:, 4 * cc + i:4 * cc + i + 1].to_broadcast([P, P]), ident[:])
                last.then_inc(s("rinv_rows"), 1)

            def project(v, cc, out_unit):
                pe.wait_ge(s("normed"), 2 * v + cc + 3)
                if not out_unit:
                    pe.wait_ge(s("w2_in"), 32 * v + 32)
                nc.tensor.matmul(ps[:, 7, :], (fold if out_unit else w2)[:], onorm[:], start=True, stop=True).then_inc(s("projected"), 1)

            def make_y(v, cc, out_unit):
                x_t_parts = at(ax, batch_of(v, out_unit), slice(cc * HALF, cc * HALF + HALF))
                if out_unit:
                    nc.tensor.matmul(ps[:, 7, :], fold16[:], x_t_parts, start=True, stop=True).then_inc(s("y"), 1)
                else:
                    nc.tensor.matmul(ps[:, 7, :], at(g_hi, v % HEADS, slice(0, P)), x_t_parts, start=True, stop=False)
                    nc.tensor.matmul(ps[:, 7, :], at(g_lo, v % HEADS, slice(0, P)), x_t_parts, start=False, stop=True).then_inc(s("y"), 1)

            def make_h(q, cc):
                pe.wait_ge(s("cat"), 2 * HEADS * q + 2 * HEADS + cc + 1)
                for h in range(HEADS):
                    last = nc.tensor.matmul(ps[:, 7, :], w_out[:, h, :], cat[:, h, cc * HALF:cc * HALF + HALF], start=(h == 0), stop=(h == HEADS - 1))
                last.then_inc(s("h_made"), 1)

            def unit(v, first=False, last=False, out_unit=False, h_batch=None, late=False, prev_out=None, next_out=None, back=()):
                o = out_unit
                prev_out = o if prev_out is None else prev_out
                next_out = o if next_out is None else next_out
                for t in range(T):
                    if t < 7:
                        scores(v, t + 1, o)
                    elif not last:
                        scores(v + 1, 0, next_out)
                    if t >= 5:
                        weigh(v, 0, t - 5, o)
                    elif not first:
                        weigh(v - 1, 0 if t == 0 else 1, 3 if t == 0 else t - 1, prev_out)
                    transpose(v, t)
                    if t == 0 and late:
                        pe.wait_ge(s("z"), 2 * (v - 1))
                        make_y(v, 1, o)
                    for t_back, b in back:
                        if t == t_back:
                            pe.wait_ge(s("y_out"), 2 * v + 2 + t // 4)
                            for m in range(T):
                                last_t = nc.tensor.transpose(ps[:, 7, :].bitcast(FP16)[:, m * P:m * P + P], ax[:, b, m * P:m * P + P], ident16[:])
                            last_t.then_inc(s("h_t"), 1)
                        if t == t_back + 1:
                            pe.wait_ge(s("h_x2"), b + 1)
                    if t == 1 and not first:
                        pe.wait_ge(s("y_out"), 2 * v + 2)
                        repeat_inverse(v - 1, 0)
                    if t == 2 and not first:
                        project(v - 1, 0, prev_out)
                    if t == 3:
                        if first:
                            pe.wait_ge(s("y_out"), 2 * v + 2)
                        else:
                            pe.wait_ge(s("z"), 2 * v - 1)
                        if not last:
                            make_y(v + 1, 0, next_out)
                    if t == 4 and h_batch is not None:
                        pe.wait_ge(s("y_out"), 2 * v + 3)
                        make_h(h_batch, 0)
                    if t == 5 and h_batch is not None:
                        pe.wait_ge(s("h_lo"), 2 * h_batch + 1)
                        make_h(h_batch, 1)
                    if t == (5 if h_batch is None else 6) and not first:
                        if h_batch is not None:
                            pe.wait_ge(s("h_lo"), 2 * h_batch + 2)
                        elif last:
                            pe.wait_ge(s("z"), 2 * v - 1)
                        else:
                            pe.wait_ge(s("y_out"), 2 * v + 3)
                        repeat_inverse(v - 1, 1)
                    if t == (6 if h_batch is None else 7) and not first:
                        project(v - 1, 1, prev_out)
                    if t == 7 and not last and h_batch is None:
                        if first:
                            pe.wait_ge(s("y_out"), 2 * v + 3)
                        else:
                            pe.wait_ge(s("z"), 2 * v)
                        make_y(v + 1, 1, next_out)

            pe.wait_ge(s("x1_ready"), 2)
            pe.wait_ge(s("wo_in"), 80)
            pe.sem_inc(s("pT"), 2)
            pe.sem_inc(s("scores"), 1)
            pe.sem_inc(s("projected"), 1)
            pe.sem_inc(s("h_made"), 2)
            pe.sem_inc(s("pv"), 8)
            pe.sem_inc(s("rinv_rows"), 2)
            def x_t_parts(b):
                pe.wait_ge(s("x2"), 2 * b + 2)
                if b >= 2:
                    pe.wait_ge(s("ax"), b - 1)
                for t in range(T):
                    last_t = nc.tensor.transpose(ps[:, 4 + b % 2, :].bitcast(FP16)[:, t * P:t * P + P], x2[:, b, t, :], ident16[:])
                last_t.then_inc(s("xt16"), 1)

            x_t_parts(0)
            pe.wait_ge(s("ax"), 1)
            make_y(0, 0, False)
            x_t_parts(1)
            pe.wait_ge(s("y_out"), 1)
            make_y(0, 1, False)
            x_t_parts(2)
            x_t_parts(3)
            scores(0, 0, False)
            for b in range(4, B):
                x_t_parts(b)
            pe.wait_ge(s("ax"), B)
            unit(0, first=True)
            with pe.Fori(1, HEADS + 1) as v:
                unit(v)
            with pe.Fori(1, B - 1) as q:
                unit(q * HEADS + 1, h_batch=q - 1)
                unit(q * HEADS + 2, late=True)
                with pe.Fori(3, HEADS + 1) as j:
                    unit(q * HEADS + j)
            unit((B - 1) * HEADS + 1, h_batch=B - 2)
            unit((B - 1) * HEADS + 2, late=True)
            with pe.Fori((B - 1) * HEADS + 3, B * HEADS - 1) as v:
                unit(v)
            v0 = B * HEADS
            unit(v0 - 1, next_out=True, back=((0, 0), (4, 1)))
            unit(v0, out_unit=True, prev_out=False, back=((0, 2), (4, 3)))
            unit(v0 + 1, out_unit=True, h_batch=B - 1, back=((0, 4),))
            unit(v0 + 2, out_unit=True, late=True, back=((4, 5),))
            unit(v0 + 3, out_unit=True, back=((0, 6), (4, 7)))
            with pe.Fori(v0 + 4, v0 + B - 1) as v:
                unit(v, out_unit=True)
            unit(v0 + B - 1, last=True, out_unit=True)
            def output(b):
                pe.wait_ge(s("cat"), 2 * (v0 + b) + 4)
                if b >= 2:
                    pe.wait_ge(s("x1_done"), b - 1)
                for t in range(T):
                    last_t = nc.tensor.transpose(ps[:, b % 2, t * F:t * F + F], cat[0:F, b, t * P:t * P + P], ident[0:F, 0:F])
                last_t.then_inc(s("zo"), 1)

            v = v0 + B - 1
            weigh(v, 0, 3, True)
            pe.wait_ge(s("z"), 2 * v)
            repeat_inverse(v, 0)
            pe.wait_ge(s("masked"), 8 * v + 9)
            output(0)
            output(1)
            project(v, 0, True)
            for part in range(4):
                weigh(v, 1, part, True)
                if part < 2:
                    output(2 + part)
            pe.wait_ge(s("z"), 2 * v + 1)
            repeat_inverse(v, 1)
            output(4)
            output(5)
            project(v, 1, True)
            output(6)
            output(7)
            pe.wait_ge(s("z"), 2 * v + 2)

        @block.vector
        def _(dve):
            v = nc.vector
            v.memset(w_block[:], 0.0).then_inc(s("w_block_zero"), 1)
            link(v.memset(node_block[:], 0.0))
            v.memset(ones[:], 1.0).then_inc(s("ones_made"), 1)
            dve.wait_ge(s("consts_in"), 48)
            v.tensor_copy(ident16[:], ident[:])
            for dup in range(2):
                v.tensor_tensor(fold[:, dup * F:dup * F + F], ident[:, 0:F], ident[:, F:P], ALU.add)
                v.tensor_tensor(fold16[:, dup * F:dup * F + F], ident[:, 0:F], ident[:, F:P], ALU.add)
            dve.wait_ge(s("wa_made"), 1)
            dve.wait_ge(s("w_block_zero"), 1)
            for half in range(2):
                r = slice(half * F, half * F + F)
                v.tensor_copy(w_block[r, 2 * P + half:2 * P + half + 1], ps[r, 4, 1:2])
                v.tensor_copy(node_block[r, half * F:half * F + F], ps[r, 4, 0:1].to_broadcast([F, F])).then_inc(s("wa_out"), 1)
            dve.wait_ge(s("wb_in"), 64)
            dve.wait_ge(s("wa_out"), 2)
            v.nop().then_inc(s("w_ready"), 1)
            for q in range(0, 2 * BP, 2):
                dve.wait_ge(s("xt_made"), q + 1)
                v.tensor_copy(x_t[:, q // 2, 0:HALF], ps[:, q % 4, :]).then_inc(s("xt_out0"), 1)
            def mask_adj(t):
                dve.wait_ge(s(f"adj_in{t % 2}"), 16 * (t // 2 + 1))
                v.tensor_scalar(adj_mask[:, t, :], tmp_d[:, t % 2, :], 0.0, MASKED, ALU.is_equal, ALU.mult).then_inc(s("mask_made"), 1)

            for i in range(0, T * BP, 2):
                if i in (0, 4):
                    mask_adj(i // 4)
                dve.wait_ge(s("proj_made"), i + 1)
                v.tensor_copy(proj[:, i // BP, i % BP, :], ps[:, i % 4, 0:WCOL]).then_inc(s("proj_out0"), 1)
            dve.wait_ge(s("ht_in"), 32)
            v.tensor_scalar(mask_t[:], mask_t[:], 0.0, None, ALU.is_gt).then_inc(s("mask_t_made"), 1)
            dve.wait_ge(s("mask_t_made"), 1)
            link(v.tensor_scalar(edge_bias[:], mask_t[:], -MASKED, MASKED, ALU.mult, ALU.add))
            mask_adj(2)
            dve.wait_ge(s("cnt_made"), 1)
            v.scalar_tensor_tensor(tmp_a[0:E, 1, :], ps[0:E, 6:8, :].rearrange("p a b -> p (a b)"), 0.0, mask_t[0:E, :], ALU.is_equal, ALU.add).then_inc(s("eff_made"), 1)
            mask_adj(3)
            dve.wait_ge(s("rank_made"), 1)
            dve.wait_ge(s("eff_made"), 1)
            v.tensor_tensor(rank[:], ps[0:E, 6:8, :].rearrange("p a b -> p (a b)"), tmp_a[0:E, 1, :], ALU.mult).then_inc(s("rank_out"), 1)
            link(v.memset(max_all[:], 0.0))
            dve.wait_ge(s("rank_out"), 1)
            v.tensor_reduce(max_all[0:E, :], rank[:], axis=AX.X, op=ALU.max).then_inc(s("max_all"), 1)
            mask_adj(4)
            dve.wait_ge(s("hn_in"), 16)
            link(v.tensor_scalar(mask_n[:], mask_n[:], 0.0, None, ALU.is_gt))
            link(v.tensor_reduce(node_cnt[:], mask_n[:], axis=AX.X, op=ALU.add))
            link(v.tensor_scalar(node_empty[:], node_cnt[:], 0.0, None, ALU.is_equal))
            link(v.tensor_tensor(mask_n[:], mask_n[:], node_empty[:].unsqueeze(2).to_broadcast([P, T, E]), ALU.add))
            link(v.tensor_scalar(mask_n[:], mask_n[:], -MASKED, MASKED, ALU.mult, ALU.add))
            mask_adj(5)
            mask_adj(6)

            def industry_mean(t):
                dve.wait_ge(s("ind_made"), t + 1)
                v.tensor_scalar(industry[:, t, :], ps[:, 2 + t % 2, :], deg[:, t:t + 1], None, ALU.mult).then_inc(s("ind_out"), 1)

            def scale_g():
                dve.wait_ge(s("g_made"), 1)
                gp = ps[:, 1, :].rearrange("p (h f) -> p h f", h=HEADS)
                v.tensor_reduce(g_abs[:], gp, axis=AX.X, op=ALU.max, apply_absolute_value=True).then_inc(s("g_abs"), 1)
                dve.wait_ge(s("g_max"), 1)
                v.tensor_scalar(g_max[:], g_max[:], 1.0 / GTOP, 1e-30, ALU.mult, ALU.max).then_inc(s("g_max"), 1)
                dve.wait_ge(s("g_max"), 2)
                link(v.reciprocal(g_inv[:], g_max[:]))
                v.tensor_scalar(g_scale[:], g_max[:], -1.0 / (XS * XS), None, ALU.mult)
                for dup in range(2):
                    link(v.tensor_tensor(g_hi[:, :, dup * F:dup * F + F], gp, g_inv[:].unsqueeze(2).to_broadcast([P, HEADS, F]), ALU.mult))
                gs = tmp_d[:, 0, 0:BF].rearrange("p (h f) -> p h f", h=HEADS)
                link(v.tensor_tensor(gs, gp, g_inv[:].unsqueeze(2).to_broadcast([P, HEADS, F]), ALU.mult))
                for dup in range(2):
                    v.tensor_tensor(g_lo[:, :, dup * F:dup * F + F], gs, g_hi[:, :, 0:F], ALU.subtract).then_inc(s("g_out"), 1)
                dve.wait_ge(s("w_norm"), 1)
                dve.wait_ge(s("wo_in"), 80)
                link(v.tensor_scalar(b_abs[:], bh[:], -1.0, None, ALU.mult))
                link(v.tensor_tensor(b_abs[:], b_abs[:], bh[:], ALU.max))
                link(v.scalar_tensor_tensor(w_norm[:], w_norm[:], float(F) ** 0.5, b_abs[:], ALU.mult, ALU.add))
                wa = tmp_c[:, 1, 0:HALF].rearrange("p (h f) -> p h f", h=HEADS)
                link(v.tensor_scalar(wa, w_out[:, :, 0:F], -1.0, None, ALU.mult))
                link(v.tensor_tensor(wa, wa, w_out[:, :, 0:F], ALU.max))
                v.tensor_tensor(wa, wa, w_norm[:].unsqueeze(2).to_broadcast([P, HEADS, F]), ALU.mult).then_inc(s("w_abs"), 1)

            def scale_h():
                dve.wait_ge(s("h_bound"), 1)
                v.tensor_reduce(h_top[:], ps[:, 1, :].rearrange("p (h f) -> p f h", h=HEADS), axis=AX.X, op=ALU.add).then_inc(s("h_top"), 1)
                dve.wait_ge(s("h_top"), 1)
                link(v.tensor_reduce(h_unit[:], h_top[:], axis=AX.X, op=ALU.max))
                link(v.tensor_scalar(h_unit[:], h_unit[:], 1.0 / HTOP, 1e-15, ALU.mult, ALU.max))
                v.reciprocal(h_inv[:], h_unit[:])
                v.tensor_scalar(h_scale[:], h_unit[:], h_unit[:], -1.0, ALU.mult, ALU.mult)
                link(v.tensor_scalar(z_scale[:], h_unit[:], 1.0 / PSC, None, ALU.mult))

            for bp in range(BP):
                dve.wait_ge(s("edge_s"), bp + 1)
                if bp:
                    dve.wait_ge(s("edge_exp"), bp)
                e_s = ps[:, 4:6, :].rearrange("p a b -> p (a b)")
                link(v.tensor_copy(tmp_a[:, 1, :], e_s))
                v.scalar_tensor_tensor(tmp_a[:, 1, :], e_s, 0.2, tmp_a[:, 1, :], ALU.mult, ALU.max).then_inc(s("edge_lk"), 1)
                dve.wait_ge(s("edge_lk"), bp + 1)
                v.tensor_tensor_reduce(out=tmp_a[:, 0, :], in0=tmp_a[:, 1, :], in1=edge_bias[:], scale=-1.0, scalar=3e38,
                                       op0=ALU.add, op1=ALU.min, accum_out=edge_max[:, bp:bp + 1]).then_inc(s("edge_masked"), 1)
                if bp == 0:
                    mask_adj(7)
                    dve.wait_ge(s("deg_sum"), T)
                    link(v.tensor_scalar(deg[:], deg[:], 1.0, None, ALU.max))
                    link(v.reciprocal(deg[:], deg[:]))
                industry_mean(2 * bp)
                if bp == 0:
                    scale_g()
                if bp == 1:
                    scale_h()
                dve.wait_ge(s("edge_exp"), bp + 1)
                link(v.reciprocal(edge_inv[:, bp:bp + 1], edge_sum[:, bp:bp + 1]))
                industry_mean(2 * bp + 1)
                dve.wait_ge(s("agg_made"), bp + 1)
                for half in range(2):
                    r = slice(half * F, half * F + F)
                    v.tensor_scalar(agg[:, 2 * bp + half, :], ps[r, 0, bp * P + half * F:bp * P + half * F + F], edge_inv[r, bp:bp + 1], None, ALU.mult).then_inc(s("agg_out"), 1)
            dve.wait_ge(s("aggt_made"), 1)
            v.tensor_copy(agg_t[:], ps[0:F, 4, :]).then_inc(s("aggt_out"), 1)
            dve.wait_ge(s("he_re"), 2)
            link(v.scalar_tensor_tensor(he_r[:], he_e[:], 1.0, he_r[:], ALU.min, ALU.add))
            v.tensor_scalar(he_r[:], he_r[:], -1.0, None, ALU.add).then_inc(s("he_made"), 1)
            dve.wait_ge(s("fc_in"), 80)
            link(v.memset(av_row[:], 0.0))
            v.tensor_scalar(av_row[:, 0, 15:16], av[:], -1.0, None, ALU.mult).then_inc(s("av_row"), 1)
            v.tensor_copy(av_row[:, 1, 15:16], av[:]).then_inc(s("av_row"), 1)
            v.tensor_copy(av_all[:], av[:].to_broadcast([P, P])).then_inc(s("av_all_made"), 1)
            dve.wait_ge(s("se_made"), 1)
            v.memset(extra[:, 16:17], 1.0)
            v.tensor_copy(extra[:, 0:16], ps[0:E, 7, 0:16]).then_inc(s("extra_out"), 1)
            dve.wait_ge(s("max_one"), 1)
            v.tensor_copy(max_count[:], max_one[0:1, :]).then_inc(s("max_count"), 1)
            v.tensor_scalar(av_all[:], ident[:], -1.0, None, ALU.mult).then_inc(s("neg_ident"), 1)
            def pair(q):
                dve.wait_ge(s("pair_t"), q + 1)
                if q >= 2:
                    dve.wait_ge(s("pair_hid"), 4 * (q - 1))
                v.tensor_copy(pair_in(q), ps[:, 2 * (q % 2):2 * (q % 2) + 2, :].rearrange("p a b -> p (a b)")).then_inc(s("pair_t_out"), 1)

            se = ps[:, 6, :].rearrange("p (b e) -> p b e", b=B)
            tse = [tmp_a[:, i, 0:BF].rearrange("p (b e) -> p b e", b=B) for i in range(2)]
            for t in range(T):
                if t % 4 == 0:
                    pair(t // 4)
                link(v.tensor_tensor(tse[t % 2], se, mask_n[:, t, :].unsqueeze(1).to_broadcast([P, B, E]), ALU.add))
                link(v.tensor_reduce(se_max[:, t, :], tse[t % 2], axis=AX.X, op=ALU.max))

            def slots(tag, start, end):
                dve.sem_inc(s(tag + "extra_read"), 1)
                dve.sem_inc(s(tag + "wgt"), 1)
                dve.sem_inc(s(tag + "zw"), 2)
                dve.sem_inc(s(tag + "v"), 2)

                def select(m, u):
                    k = m + start
                    column = slot_no[0:E, k:k + 1] if isinstance(m, int) else slot_no[0:E, bass.ds(k, 1)]
                    if not isinstance(m, int) or m > 0:
                        dve.wait_ge(s(tag + "diff"), 4 * (m - 1) + 1)
                    v.tensor_scalar(sel[u], rank[:], column, None, ALU.is_equal).then_inc(s(tag + "sel"), 1)

                def scores(m):
                    ex = ps[:, 4, 0:T * 17].rearrange("p (t c) -> p t c", t=T)
                    hn = proj[:, :, :, 2 * P:2 * P + 2]
                    dve.wait_ge(s(tag + "extra"), m + 1)
                    dve.wait_ge(s(tag + "th"), m + 1)
                    v.tensor_tensor(bl[:].rearrange("p t (a b) -> p t a b", a=BP), ex[:, :, 0:8].rearrange("p t (a b) -> p t a b", a=BP), hn, ALU.add).then_inc(s(tag + "bl"), 1)
                    dve.wait_ge(s(tag + "coef"), m + 1)
                    v.tensor_tensor(sx[:], ex[:, :, 8:16], se_max[:], ALU.subtract).then_inc(s(tag + "extra_read"), 1)
                    v.tensor_scalar(vb[:], ex[:, :, 16:17].rearrange("p t a -> p (t a)"), -MASKED, MASKED, ALU.mult, ALU.add).then_inc(s(tag + "extra_read"), 1)
                    dve.wait_ge(s(tag + "extra_read"), 2 * m + 3)
                    v.tensor_tensor(sx[:], sx[:], vb[:].unsqueeze(2).to_broadcast([P, T, B]), ALU.add).then_inc(s(tag + "sx"), 1)

                def weight(m, u):
                    dve.wait_ge(s(tag + "th"), m + 2)
                    if not isinstance(m, int) or m > 0:
                        dve.wait_ge(s(tag + "zw"), 4 * (m - 1) + 2)
                    v.tensor_scalar(wgt[:, u], th[:], -0.5, 0.5, ALU.mult, ALU.add).then_inc(s(tag + "wgt"), 1)

                def blend(m, u, c):
                    j = m * 4 + c
                    dve.wait_ge(s(tag + "diff"), j + 2)
                    dve.wait_ge(s(tag + "wgt"), m + 2)
                    dve.wait_ge(s(tag + "exp"), j + 1)
                    for i in range(2):
                        t = 2 * c + i
                        w3 = wgt[:, u, t, :].unsqueeze(2).to_broadcast([P, B, F])
                        last = v.tensor_tensor(tmp_a[:, c % 2, i * HALF:i * HALF + HALF].rearrange("p (b f) -> p b f", b=B),
                                               ps[:, 2 * (c % 2) + i, :].rearrange("p (b f) -> p b f", b=B), w3, ALU.mult)
                    last.then_inc(s(tag + "zw"), 1)
                    dve.wait_ge(s(tag + "zw"), j + 3)
                    zz = tmp_a[:, c % 2, :].rearrange("p (i a b) -> p i a b", i=2, a=BP)
                    v.tensor_tensor(zz, zz, proj[:, 2 * c:2 * c + 2, :, 0:P], ALU.add).then_inc(s(tag + "z"), 1)

                def elu(m, c):
                    j = m * 4 + c
                    dve.wait_ge(s(tag + "exp"), j + 3)
                    dve.wait_ge(s(tag + "g"), j + 1)
                    v.scalar_tensor_tensor(tmp_d[:, c % 2, :], tmp_c[:, c % 2, :], 1.0, tmp_b[:, c % 2, :], ALU.min, ALU.add).then_inc(s(tag + "v"), 1)

                def prologue():
                    select(0, 0)
                    scores(0)
                    weight(0, 0)
                    blend(0, 0, 0)

                def slot(m, u, last=False):
                    if not last:
                        select(m + 1, 1 - u)
                    blend(m, u, 1)
                    elu(m, 0)
                    blend(m, u, 2)
                    elu(m, 1)
                    if not last:
                        scores(m + 1)
                    blend(m, u, 3)
                    elu(m, 2)
                    if not last:
                        weight(m + 1, 1 - u)
                        blend(m + 1, 1 - u, 0)
                    elu(m, 3)

                prologue()
                with dve.Fori(0, (end - start) // 2 - 1) as pair:
                    for u in range(2):
                        slot(pair * 2 + u, u)
                for u in range(2):
                    slot(end - start - 2 + u, u, last=(u == 1))

            def rest(start, end):
                dve.wait_ge(s("max_count"), 1)
                many = dve.value_load(max_count[0:1, 0:1], min_val=0, max_val=E)
                with dve.If(many > start):
                    dve.wait_ge(s("f_g"), 4 * start + 2)
                    dve.wait_ge(s("f_csum"), start + 1)
                    slots("s_", start, end)
                    dve.wait_ge(s("s_g"), 4 * (end - start) + 2)
                    dve.wait_ge(s("s_csum"), end - start + 1)

            slots("f_", 0, FAST_SLOTS)
            rest(FAST_SLOTS, E)

            for q in range(2, 4):
                pair(q)
            dve.wait_ge(s("f_g"), 4 * FAST_SLOTS + 2)
            dve.wait_ge(s("f_csum"), FAST_SLOTS + 1)
            link(v.reciprocal(coef_sum[:], coef_sum[:]))
            g4 = g_sum.rearrange("p t (b f) -> p (t b) f", b=B)

            def g_mean(bp):
                gb = g_sum[:, :, bp * P:bp * P + P].rearrange("p t (b f) -> p t b f", b=2)
                link(v.tensor_tensor(gb, gb, coef_sum[:, :, 2 * bp:2 * bp + 2].unsqueeze(3).to_broadcast([P, T, 2, F]), ALU.mult))
                v.tensor_scalar(gb, gb, -1.0, None, ALU.add).then_inc(s("g_final"), 1)

            g_mean(0)
            for q in range(4, 8):
                if q < 7:
                    g_mean(q - 3)
                pair(q)
            dve.wait_ge(s("pair_th"), 1)
            v.tensor_scalar(tmp_b[0:16, 1, 0:HALF], tmp_b[0:16, 0, 0:HALF], 0.5, 0.5, ALU.mult, ALU.add).then_inc(s("pair_wgt"), 1)
            dve.wait_ge(s("pair_wgt_t"), 1)
            v.tensor_copy(wgt[:, 0].rearrange("p (c i) b -> p c i b", c=2), ps[:, 6, 0:T * B].rearrange("p (i b c) -> p c i b", b=B, c=2)).then_inc(s("pair_w"), 1)
            dve.wait_ge(s("pair_w"), 1)
            dve.wait_ge(s("x_and_ind"), 1)
            dve.wait_ge(s("g_less_ind"), BP)
            d = half_batches(g_less_ind, 0)
            link(v.tensor_tensor(d, d, wgt[:, 0, :, 0:4].unsqueeze(3).to_broadcast([P, T, 4, F]), ALU.mult))
            link(v.tensor_tensor(half_batches(industry, 0), x_nat[:, :, 0:4, :], d, ALU.add))
            centre("ln0_", half_batches(industry, 0), by_batches(ln_mean, 0))
            dve.wait_ge(s("blended"), 1)
            centre("ln0_", half_batches(industry, 1), by_batches(ln_mean, 1))
            for half in range(2):
                variance(dve, "ln0_", half, half_batches(g_sum, half), by_batches(ln_var, half))
            deviation(dve, "ln0_")
            for half in range(2):
                v.tensor_tensor(x1[:, 4 * half:4 * half + 4, :, :].transpose([0, 2, 1, 3]), half_batches(industry, half),
                                by_batches(ln_var, half).unsqueeze(3).to_broadcast([P, T, 4, F]), ALU.mult).then_inc(s("x1_ready"), 1)

            def at(w, i, *rest):
                return w[(slice(None), i) + rest] if isinstance(i, int) else w[(slice(None), bass.ds(i, 1)) + rest].squeeze(1)

            def mask(v, t):
                dve.wait_ge(s("scores"), 8 * v + t + 2)
                dve.wait_ge(s("probs"), 8 * v + t + 1)
                nc.vector.nop(nofuse=True)
                nc.vector.tensor_tensor_reduce(out=masked[:, t % 2, :], in0=ps[:, 0:2, :].rearrange("p a b -> p (a b)"), in1=adj_mask[:, t, :], scale=cur_scale[:],
                                               scalar=3e38, op0=ALU.add, op1=ALU.min, accum_out=neg_max[:, t % 2:t % 2 + 1]).then_inc(s("masked"), 1)

            def lo(v, t):
                dve.wait_ge(s("hi"), 8 * v + t + 1)
                where = (slice(None), t // 4, slice(None), slice(t % 4 * P, t % 4 * P + P))
                nc.vector.scalar_tensor_tensor(pt_lo[where], ps[:, 2 + 2 * (t % 2):4 + 2 * (t % 2), :].rearrange("p a (m n) -> p (a m) n", n=P), PSC,
                                               pt_hi[where], ALU.mult, ALU.subtract).then_inc(s("lo"), 1)

            def invert(v, cc):
                dve.wait_ge(s("probs"), 8 * v + 4 * cc + 6)
                dve.wait_ge(s("rinv_rows"), 2 * v + cc + 1)
                nc.vector.reciprocal(rinv[:, 4 * cc:4 * cc + 4], sums[:, 4 * cc:4 * cc + 4]).then_inc(s("rinv"), 1)

            def normalise(v, cc):
                dve.wait_ge(s("rinv_rows"), 2 * v + cc + 3)
                dve.wait_ge(s("osum"), 2 * v + cc + 2)
                dve.wait_ge(s("projected"), 2 * v + cc + 1)
                nc.vector.tensor_tensor(onorm[:], osum[:, cc, :], ps[:, 7, :], ALU.mult).then_inc(s("normed"), 1)

            def take_y(v, cc):
                half = slice(cc * HALF, cc * HALF + HALF)
                dve.wait_ge(s("y_hi"), 2 * v + cc + 1)
                nc.vector.tensor_tensor(at(y_lo, v % 2, half), ps[:, 7, :], at(y_hi, v % 2, half), ALU.subtract).then_inc(s("y_out"), 1)

            def take_h(q, cc):
                dve.wait_ge(s("h_hi"), 2 * q + cc + 1)
                half = slice(cc * HALF, cc * HALF + HALF)
                low = ax[F:P, q, half] if isinstance(q, int) else ax[F:P, bass.ds(q, 1), half].squeeze(1)
                nc.vector.scalar_tensor_tensor(low, ps[F:P, 7, :], h_inv[F:P, :], low, ALU.mult, ALU.subtract).then_inc(s("h_lo"), 1)

            def unit(v, first=False, last=False, out_unit=False, h_batch=None, late=False, prev_out=None, next_out=None, back=()):
                for t in range(T):
                    if t in (5, 6) and h_batch is not None:
                        take_h(h_batch, t - 5)
                    if t < 7:
                        mask(v, t + 1)
                    elif not last:
                        if not out_unit:
                            dve.wait_ge(s("masked"), 8 * v + 9)
                            following = h_scale[:] if next_out else g_scale[:, bass.ds((v + 1) % HEADS, 1)]
                            nc.vector.tensor_copy(cur_scale[:], following).then_inc(s("cur_scale"), 1)
                            dve.wait_ge(s("cur_scale"), v + 2)
                        mask(v + 1, 0)
                    if t == 1 and late:
                        take_y(v, 1)
                    early = {0: any(t_back == 0 for t_back, b in back), 4: h_batch is not None or any(t_back == 4 for t_back, b in back)}
                    if t == 0 and early[0]:
                        take_y(v, 1)
                    if t == 4 and early[4]:
                        take_y(v + 1, 0)
                    if t > 0:
                        lo(v, t - 1)
                    elif not first:
                        lo(v - 1, 7)
                    if t == 1 and not first:
                        normalise(v - 1, 0)
                    if t == (5 if h_batch is None else 6) and not first:
                        normalise(v - 1, 1)
                    if t == 0 and not first:
                        if not late and not early[0]:
                            take_y(v, 1)
                    if t == 2 and not first:
                        invert(v - 1, 1)
                    if t == 6:
                        invert(v, 0)
                    if t == 4 and not last and not early[4]:
                        take_y(v + 1, 0)

            dve.wait_ge(s("x1_ready"), 2)
            dve.sem_inc(s("lo"), 2)
            dve.sem_inc(s("masked"), 1)
            dve.sem_inc(s("rinv"), 2)
            dve.sem_inc(s("normed"), 2)
            def x_parts(b):
                nc.vector.tensor_scalar(x2[:, b, :, 0:F], x1[:, b], XS, None, ALU.mult).then_inc(s("x2"), 1)
                dve.wait_ge(s("x2"), 2 * b + 1)
                nc.vector.scalar_tensor_tensor(x2[:, b, :, F:P], x1[:, b], XS, x2[:, b, :, 0:F], ALU.mult, ALU.subtract).then_inc(s("x2"), 1)

            x_parts(0)
            nc.vector.tensor_copy(cur_scale[:], g_scale[:, 0:1]).then_inc(s("cur_scale"), 1)
            x_parts(1)
            take_y(0, 0)
            x_parts(2)
            take_y(0, 1)
            x_parts(3)
            dve.wait_ge(s("cur_scale"), 1)
            mask(0, 0)
            for b in range(4, B):
                x_parts(b)
            unit(0, first=True)
            with dve.Fori(1, HEADS + 1) as v:
                unit(v)
            with dve.Fori(1, B - 1) as q:
                unit(q * HEADS + 1, h_batch=q - 1)
                unit(q * HEADS + 2, late=True)
                with dve.Fori(3, HEADS + 1) as j:
                    unit(q * HEADS + j)
            unit((B - 1) * HEADS + 1, h_batch=B - 2)
            unit((B - 1) * HEADS + 2, late=True)
            with dve.Fori((B - 1) * HEADS + 3, B * HEADS - 1) as v:
                unit(v)
            v0 = B * HEADS
            unit(v0 - 1, next_out=True, back=((0, 0), (4, 1)))
            unit(v0, out_unit=True, prev_out=False, back=((0, 2), (4, 3)))
            unit(v0 + 1, out_unit=True, h_batch=B - 1, back=((0, 4),))
            unit(v0 + 2, out_unit=True, late=True, back=((4, 5),))
            unit(v0 + 3, out_unit=True, back=((0, 6), (4, 7)))
            with dve.Fori(v0 + 4, v0 + B - 1) as v:
                unit(v, out_unit=True)
            unit(v0 + B - 1, last=True, out_unit=True)

            def add_output(b):
                dve.wait_ge(s("zo"), b + 1)
                nc.vector.tensor_tensor(x1[:, b], x1[:, b], ps[:, b % 2, :].rearrange("p (t f) -> p t f", f=F), ALU.add).then_inc(s("x1_done"), 1)

            def stats(w, half):
                return w[:, 4 * T * half:4 * T * half + 4 * T].rearrange("p (b t) -> p b t", t=T)

            def scale(half):
                dve.wait_ge(s("ln1_sqrt"), half + 1)
                link(nc.vector.reciprocal(stats(ln_var, half), stats(ln_var, half)))
                for q in range(2 * half, 2 * half + 2):
                    pair = x1[:, 2 * q:2 * q + 2]
                    inv = stats(ln_var, half)[:, 2 * (q % 2):2 * (q % 2) + 2]
                    nc.vector.tensor_tensor(pair, pair, inv.unsqueeze(3).to_broadcast([P, 2, T, F]), ALU.mult).then_inc(s("ln1_out"), 1)

            v = v0 + B - 1
            lo(v, 7)
            normalise(v, 0)
            invert(v, 1)
            for b in range(4):
                add_output(b)
            normalise(v, 1)
            dve.wait_ge(s("x1_done"), 4)
            centre("ln1_", x1[:, 0:4], stats(ln_mean, 0))
            for b in range(4, 7):
                add_output(b)
            variance(dve, "ln1_", 0, squares[0], stats(ln_var, 0))
            add_output(7)
            dve.wait_ge(s("x1_done"), B)
            centre("ln1_", x1[:, 4:8], stats(ln_mean, 1))
            scale(0)
            variance(dve, "ln1_", 1, squares[1], stats(ln_var, 1))
            scale(1)

        @block.gpsimd
        def _(pool):
            g = nc.gpsimd
            pool.wait_ge(s("max_all"), 1)
            g.partition_all_reduce(max_one[:], max_all[:], P, RMAX).then_inc(s("max_one"), 1)
            pool.wait_ge(s("g_abs"), 1)
            g.partition_all_reduce(g_max[:], g_abs[:], P, RMAX).then_inc(s("g_max"), 1)
            pool.wait_ge(s("ind_made"), T)
            g.memset(g_sum, 0.0).then_inc(s("f_g"), 2)
            pool.wait_ge(s("ind_out"), T)
            g.tensor_tensor(x_nat[:], x_nat[:], industry.rearrange("p t (b f) -> p t b f", b=B), ALU.add).then_inc(s("x_and_ind"), 1)
            g.memset(coef_sum[:], 0.0).then_inc(s("f_csum"), 1)

            def slots(tag, start, end):
                pool.sem_inc(s(tag + "vc"), 5)
                if tag == "s_":
                    pool.sem_inc(s(tag + "g"), 2)
                    pool.sem_inc(s(tag + "csum"), 1)

                def slot(m, u):
                    pool.wait_ge(s(tag + "coef"), m + 2)
                    pool.wait_ge(s(tag + "csum"), m + 1)
                    g.tensor_tensor(coef_sum[:], coef_sum[:], coef[:, u], ALU.add).then_inc(s(tag + "csum"), 1)
                    for c in range(4):
                        j = m * 4 + c
                        vv = tmp_d[:, c % 2, :].rearrange("p (t f) -> p t f", f=F)
                        pool.wait_ge(s(tag + "v"), j + 3)
                        g.tensor_tensor(vv, vv, coef[:, u, 2 * c:2 * c + 2, :].rearrange("p t b -> p (t b)").unsqueeze(2).to_broadcast([P, 2 * B, F]), ALU.mult).then_inc(s(tag + "vc"), 1)
                        pool.wait_ge(s(tag + "vc"), j + 6)
                        pool.wait_ge(s(tag + "g"), j + 2)
                        gg = g_sum[:, 2 * c:2 * c + 2, :].rearrange("p t q -> p (t q)")
                        g.tensor_tensor(gg, gg, tmp_d[:, c % 2, :], ALU.add).then_inc(s(tag + "g"), 1)

                with pool.Fori(0, (end - start) // 2) as pair:
                    for u in range(2):
                        slot(pair * 2 + u, u)

            def rest(start, end):
                pool.wait_ge(s("max_count"), 1)
                many = pool.value_load(max_count[0:1, 0:1], min_val=0, max_val=E)
                with pool.If(many > start):
                    pool.wait_ge(s("f_g"), 4 * start + 2)
                    pool.wait_ge(s("f_csum"), start + 1)
                    slots("s_", start, end)
                    pool.wait_ge(s("s_g"), 4 * (end - start) + 2)
                    pool.wait_ge(s("s_csum"), end - start + 1)

            slots("f_", 0, FAST_SLOTS)
            rest(FAST_SLOTS, E)

            for bp in range(BP):
                pool.wait_ge(s("g_final"), bp + 1)
                both = (slice(None), slice(None), slice(bp * P, bp * P + P))
                g.tensor_tensor(g_less_ind[both], g_sum[both], industry[both], ALU.subtract).then_inc(s("g_less_ind"), 1)
            pool.wait_ge(s("pair_w"), 1)
            pool.wait_ge(s("g_less_ind"), BP)
            pool.wait_ge(s("x_and_ind"), 1)
            d = half_batches(g_less_ind, 1)
            g.tensor_tensor(d, d, wgt[:, 0, :, 4:8].unsqueeze(3).to_broadcast([P, T, 4, F]), ALU.mult).then_inc(s("weighted"), 1)
            pool.wait_ge(s("weighted"), 1)
            g.tensor_tensor(half_batches(industry, 1), x_nat[:, :, 4:8, :], d, ALU.add).then_inc(s("blended"), 1)

            def leaky(v, cc, slot):
                pool.wait_ge(s("z"), 2 * v + cc + 1)
                pool.nop(nofuse=True)
                g.tensor_scalar(zm[:, cc, :], zc[:, cc, :], 0.0, -0.99, ALU.min, ALU.mult).then_inc(s("zm"), 1)
                pool.wait_ge(s("zm"), 2 * v + cc + 1)
                where = cat[:, bass.ds(slot, 1), cc * HALF:cc * HALF + HALF].squeeze(1)
                g.tensor_tensor(where, zc[:, cc, :], zm[:, cc, :], ALU.add).then_inc(s("cat"), 1)

            pool.wait_ge(s("x1_ready"), 2)
            pool.sem_inc(s("cat"), 2)
            with pool.Fori(0, B) as b:
                with pool.Fori(0, HEADS) as h:
                    for cc in range(2):
                        pool.wait_ge(s("h_made"), 2 * b + cc + 1)
                        pool.wait_ge(s("cat"), 2 * (b * HEADS + h) + cc + 1)
                        leaky(b * HEADS + h, cc, h)
            pool.wait_ge(s("h_made"), 2 * B + 2)
            with pool.Fori(0, B) as b:
                for cc in range(2):
                    pool.wait_ge(s("cat"), 2 * (B * HEADS + b) + cc + 1)
                    leaky(B * HEADS + b, cc, b)




def _layout(i):
    import numpy as np
    c = np.ascontiguousarray
    n = {k: np.asarray(v) for k, v in i.items()}
    consts = np.zeros((P, 2 * P), np.float32)
    consts[:, 0:P] = np.eye(P)
    consts[0:E, P:P + E] = np.triu(np.ones((E, E)))
    consts[:, P + E:P + 2 * E] = np.arange(1, E + 1)
    return {
        "consts": consts, "x": c(n["x"]), "adj": c(n["adj"]), "adjT": c(n["adj"].T),
        "H": c(n["L0_gnn_H"]), "HT": c(n["L0_gnn_H"].T), "W": c(n["L0_gnn_W"]), "WT": c(n["L0_gnn_W"].T),
        "W_ind": c(n["L0_gnn_W_ind"]), "a_node": c(n["L0_gnn_a_node"].reshape(F, 1)), "a_gn": c(n["L0_gnn_a_gn"].reshape(F, 1)),
        "a_ge": c(n["L0_gnn_a_ge"].reshape(F, 1)), "fcW": c(n["L0_gnn_fcW"]), "fcb": c(n["L0_gnn_fcb"].reshape(P, 1)),
        "av": c(n["L0_gnn_av"].reshape(P, 1)), "Wh": c(n["L1_gnn_Wh"]), "WhT": c(n["L1_gnn_Wh"].transpose(0, 2, 1)),
        "bhT": c(n["L1_gnn_bh"].T), "W_out": c(n["L1_gnn_W_out"]), "b_out": c(n["L1_gnn_b_out"].reshape(F, 1)),
    }


def kernel(**inputs):
    import concourse.bacc as _bacc
    from concourse.bass_utils import run_bass_kernel_spmd as _run

    nc = _bacc.Bacc("TRN2", target_bir_lowering=False, num_devices=1)
    arrays = _layout(inputs)
    args = {k: nc.dram_tensor(f"in_{k}", v.shape, mybir.dt.from_np(v.dtype), kind="ExternalInput").ap() for k, v in arrays.items()}
    out = nc.dram_tensor("out", (B, N, F), FP32, kind="ExternalOutput").ap()
    residual_graph_layers(nc, args, out)
    r = _run(nc, [{f"in_{k}": v for k, v in arrays.items()}], core_ids=[0])
    return r.results[0]["out"]
```
